# Optimizing a Trainium2 kernel written in Bass

```python
import numpy as np
import jax
import jax.numpy as jnp

def _softmax(x, axis=-1):
    return jax.nn.softmax(x, axis=axis)

def _gelu(x):
    return jax.nn.gelu(x, approximate=True)

def _silu(x):
    return jax.nn.silu(x)

def _sigmoid(x):
    return jax.nn.sigmoid(x)

def _layernorm(x, axis=-1, eps=1e-05):
    m = jnp.mean(x, axis=axis, keepdims=True)
    v = jnp.var(x, axis=axis, keepdims=True)
    return (x - m) / jnp.sqrt(v + eps)

def _scatter_add(tgt, idx, src, axis=0):
    return tgt.at[idx].add(src)

def _segment_sum(src, seg, n):
    return jax.ops.segment_sum(src, seg, n)
kernel_name = 'mk_perceiver_d1_seqx_r4_40e0aa'

def setup_inputs(seed: int=0):
    np.random.seed(seed)
    _w = jnp.asarray

    def _rec_inputs():
        import jax
        import jax.numpy as jnp
        _rk = jax.random.key(seed)
        x = -0.0002928 + 1 * jax.random.normal(jax.random.fold_in(_rk, 1), (64, 32, 512), jnp.float32)
        _lenS = 32 - jax.random.randint(jax.random.fold_in(_rk, 7), (64,), 0, max(1, 32 // 4) + 1, jnp.int32)
        _lenS2 = 257 - jax.random.randint(jax.random.fold_in(_rk, 8), (64,), 0, max(1, 257 // 4) + 1, jnp.int32)
        _ctx_512P = jax.random.normal(jax.random.fold_in(_rk, 11), (64, 16, 128), jnp.float32)
        _ctx_512c = jax.random.dirichlet(jax.random.fold_in(_rk, 511), 0.3 * jnp.ones((16,), jnp.float32), (64, 257))
        _ctx_512t = jnp.einsum('bsk,bkd->bsd', _ctx_512c, _ctx_512P)
        _ctx_512t = _ctx_512t * jax.lax.rsqrt(jnp.mean(jnp.square(_ctx_512t)) + 1e-12) * 0.953939
        ctx_512 = 0.000227908 + 0.99994 * (_ctx_512t + 0.3 * jax.random.normal(jax.random.fold_in(_rk, 611), (64, 257, 128), jnp.float32))
        return (x, ctx_512)
    x, ctx_512 = _rec_inputs()

    def _L0_xattn_setup():
        import jax, jax.numpy as jnp
        import numpy as np
        B, S, L = (2, 256, 256)
        DIM_Q, H, K, D_C, D_CQ, R = (512, 16, 128, 128, 384, 64)

        def _rope_tables(length, dim):
            inv = 1.0 / 10000.0 ** (jnp.arange(0, dim, 2, dtype=jnp.float32) / dim)
            f = jnp.arange(length, dtype=jnp.float32)[:, None] * inv[None, :]
            sin = jnp.repeat(jnp.sin(f), 2, axis=-1)
            cos = jnp.repeat(jnp.cos(f), 2, axis=-1)
            return (sin, cos)

        def _rotate_half(x):
            half = x.shape[-1] // 2
            return jnp.concatenate([-x[..., half:], x[..., :half]], axis=-1)

        def _apply_rope(x, sin, cos):
            return x * cos + _rotate_half(x) * sin
        key = jax.random.key(seed)
        ks = jax.random.split(key, 8)
        return {'hidden_q': jax.random.normal(ks[0], (B, S, DIM_Q), jnp.float32), 'kv_c': jax.random.normal(ks[1], (B, L, D_C), jnp.float32), 'Wq': jax.random.normal(ks[2], (H * K, DIM_Q), jnp.float32) / np.sqrt(DIM_Q).astype(np.float32), 'w_kc_q': jax.random.normal(ks[3], (H, K, D_CQ), jnp.float32) / np.sqrt(K).astype(np.float32), 'w_kc_kv': jax.random.normal(ks[4], (H, K, D_C), jnp.float32) / np.sqrt(K).astype(np.float32), 'W_qr': jax.random.normal(ks[5], (H, D_CQ, R), jnp.float32) / np.float32(np.sqrt(D_CQ) * np.sqrt(R)), 'W_kr': jax.random.normal(ks[6], (H, D_C, R), jnp.float32) / np.sqrt(D_C).astype(np.float32), 'Wo': jax.random.normal(ks[7], (DIM_Q, H * K), jnp.float32) / np.sqrt(H * K).astype(np.float32)}
    _L0_xattn_all = _L0_xattn_setup()
    _L0_xattn_in = {k: v for k, v in _L0_xattn_all.items() if k in ('Wq', 'w_kc_q', 'w_kc_kv', 'W_qr', 'W_kr', 'Wo')}
    del _L0_xattn_all

    def _L0_attn_setup():
        import jax, jax.numpy as jnp
        import numpy as np
        HIDDEN = 512
        NUM_HEADS = 16
        HEAD_DIM = HIDDEN // NUM_HEADS
        HARMONICS = 64

        def _holo_params(key, in_features, out_features, harmonics):
            kb, kp = jax.random.split(key)
            basis = jax.random.normal(kb, (harmonics, in_features), dtype=jnp.float32)
            basis = basis / jnp.linalg.norm(basis, axis=1, keepdims=True)
            phase = jax.random.normal(kp, (out_features, harmonics), dtype=jnp.float32) * 0.1
            amp = jnp.ones((out_features, harmonics), dtype=jnp.float32) / np.sqrt(harmonics).astype(np.float32)
            return (basis, phase, amp)

        def _holo_linear(x, basis, phase, amp):
            resonance = jnp.einsum('bsd,hd->bsh', x, basis)
            w = amp * jnp.cos(phase)
            return jnp.einsum('bsh,oh->bso', resonance, w)
        key = jax.random.key(seed)
        ks = jax.random.split(key, 5)
        hidden_states = jax.random.normal(ks[0], (2, 512, HIDDEN), dtype=jnp.float32)
        inp = {'hidden_states': hidden_states}
        for name, k in zip(('q', 'k', 'v', 'o'), ks[1:]):
            basis, phase, amp = _holo_params(k, HIDDEN, HIDDEN, HARMONICS)
            inp[f'basis_{name}'] = basis
            inp[f'phase_{name}'] = phase
            inp[f'amp_{name}'] = amp
        return inp
    _L0_attn_all = _L0_attn_setup()
    _L0_attn_in = {k: v for k, v in _L0_attn_all.items() if k in ('basis_q', 'phase_q', 'amp_q', 'basis_k', 'phase_k', 'amp_k', 'basis_v', 'phase_v', 'amp_v', 'basis_o', 'phase_o', 'amp_o')}
    del _L0_attn_all

    def _L0_ffn_setup():
        import jax, jax.numpy as jnp
        import numpy as np
        import math
        B, S, D = (2, 512, 512)
        P = 4
        PW = 2
        L = 2
        STD = 0.02
        EPS = 1e-05

        def _layer_norm(x, g, b):
            m = jnp.mean(x, axis=-1, keepdims=True)
            v = jnp.mean(jnp.square(x - m), axis=-1, keepdims=True)
            return (x - m) * jax.lax.rsqrt(v + EPS) * g + b
        key = jax.random.key(seed)
        ks = jax.random.split(key, 16)
        n = lambda k, shape: jax.random.normal(k, shape, dtype=jnp.float32) * STD
        inp = {'x': jax.random.normal(ks[0], (B, S, D), dtype=jnp.float32), 'amp_w': n(ks[1], (D, D)), 'amp_b': jnp.zeros((D,), jnp.float32), 'ph_w': n(ks[2], (D, D)), 'ph_b': jnp.zeros((D,), jnp.float32), 'ent_w': n(ks[3], (L, D, P * D)), 'ent_b': jnp.zeros((L, P * D), jnp.float32), 'ent_pw': n(ks[4], (L, P * D, D)), 'ent_pb': jnp.zeros((L, D), jnp.float32), 'path_w': n(ks[5], (L, PW, D, D)), 'path_b': jnp.zeros((L, PW, D), jnp.float32), 'phase': jax.random.normal(ks[6], (L, PW, D), dtype=jnp.float32), 'ln3_g': jnp.ones((L, D), jnp.float32), 'ln3_b': jnp.zeros((L, D), jnp.float32), 'ln4_g': jnp.ones((L, D), jnp.float32), 'ln4_b': jnp.zeros((L, D), jnp.float32)}
        return inp
    _L0_ffn_all = _L0_ffn_setup()
    _L0_ffn_in = {k: v for k, v in _L0_ffn_all.items() if k in ('amp_w', 'amp_b', 'ph_w', 'ph_b', 'ent_w', 'ent_b', 'ent_pw', 'ent_pb', 'path_w', 'path_b', 'phase', 'ln3_g', 'ln3_b', 'ln4_g', 'ln4_b')}
    del _L0_ffn_all
    return {'x': x, 'ctx_512': ctx_512, 'L0_xattn_Wq': _L0_xattn_in['Wq'], 'L0_xattn_w_kc_q': _L0_xattn_in['w_kc_q'], 'L0_xattn_w_kc_kv': _L0_xattn_in['w_kc_kv'], 'L0_xattn_W_qr': _L0_xattn_in['W_qr'], 'L0_xattn_W_kr': _L0_xattn_in['W_kr'], 'L0_xattn_Wo': _L0_xattn_in['Wo'], 'L0_attn_basis_q': _L0_attn_in['basis_q'], 'L0_attn_phase_q': _L0_attn_in['phase_q'], 'L0_attn_amp_q': _L0_attn_in['amp_q'], 'L0_attn_basis_k': _L0_attn_in['basis_k'], 'L0_attn_phase_k': _L0_attn_in['phase_k'], 'L0_attn_amp_k': _L0_attn_in['amp_k'], 'L0_attn_basis_v': _L0_attn_in['basis_v'], 'L0_attn_phase_v': _L0_attn_in['phase_v'], 'L0_attn_amp_v': _L0_attn_in['amp_v'], 'L0_attn_basis_o': _L0_attn_in['basis_o'], 'L0_attn_phase_o': _L0_attn_in['phase_o'], 'L0_attn_amp_o': _L0_attn_in['amp_o'], 'L0_ffn_amp_w': _L0_ffn_in['amp_w'], 'L0_ffn_amp_b': _L0_ffn_in['amp_b'], 'L0_ffn_ph_w': _L0_ffn_in['ph_w'], 'L0_ffn_ph_b': _L0_ffn_in['ph_b'], 'L0_ffn_ent_w': _L0_ffn_in['ent_w'], 'L0_ffn_ent_b': _L0_ffn_in['ent_b'], 'L0_ffn_ent_pw': _L0_ffn_in['ent_pw'], 'L0_ffn_ent_pb': _L0_ffn_in['ent_pb'], 'L0_ffn_path_w': _L0_ffn_in['path_w'], 'L0_ffn_path_b': _L0_ffn_in['path_b'], 'L0_ffn_phase': _L0_ffn_in['phase'], 'L0_ffn_ln3_g': _L0_ffn_in['ln3_g'], 'L0_ffn_ln3_b': _L0_ffn_in['ln3_b'], 'L0_ffn_ln4_g': _L0_ffn_in['ln4_g'], 'L0_ffn_ln4_b': _L0_ffn_in['ln4_b']}

def reference(x, ctx_512, L0_xattn_Wq, L0_xattn_w_kc_q, L0_xattn_w_kc_kv, L0_xattn_W_qr, L0_xattn_W_kr, L0_xattn_Wo, L0_attn_basis_q, L0_attn_phase_q, L0_attn_amp_q, L0_attn_basis_k, L0_attn_phase_k, L0_attn_amp_k, L0_attn_basis_v, L0_attn_phase_v, L0_attn_amp_v, L0_attn_basis_o, L0_attn_phase_o, L0_attn_amp_o, L0_ffn_amp_w, L0_ffn_amp_b, L0_ffn_ph_w, L0_ffn_ph_b, L0_ffn_ent_w, L0_ffn_ent_b, L0_ffn_ent_pw, L0_ffn_ent_pb, L0_ffn_path_w, L0_ffn_path_b, L0_ffn_phase, L0_ffn_ln3_g, L0_ffn_ln3_b, L0_ffn_ln4_g, L0_ffn_ln4_b):
    import jax
    import jax.numpy as jnp

    def _L0_xattn_ref(hidden_q, kv_c, Wq, w_kc_q, w_kc_kv, W_qr, W_kr, Wo):
        import jax, jax.numpy as jnp
        import numpy as np
        B, S, L = (2, 256, 256)
        DIM_Q, H, K, D_C, D_CQ, R = (512, 16, 128, 128, 384, 64)

        def _rope_tables(length, dim):
            inv = 1.0 / 10000.0 ** (jnp.arange(0, dim, 2, dtype=jnp.float32) / dim)
            f = jnp.arange(length, dtype=jnp.float32)[:, None] * inv[None, :]
            sin = jnp.repeat(jnp.sin(f), 2, axis=-1)
            cos = jnp.repeat(jnp.cos(f), 2, axis=-1)
            return (sin, cos)

        def _rotate_half(x):
            half = x.shape[-1] // 2
            return jnp.concatenate([-x[..., half:], x[..., :half]], axis=-1)

        def _apply_rope(x, sin, cos):
            return x * cos + _rotate_half(x) * sin
        Bv, Sv, _ = hidden_q.shape
        _, Lv, _ = kv_c.shape
        q_hk = (hidden_q @ Wq.T).reshape(Bv, Sv, H, K)
        q_big = jnp.einsum('bshk,hkq->bshq', q_hk, w_kc_q)
        sin_q, cos_q = _rope_tables(Sv, D_CQ)
        q_big = _apply_rope(q_big, sin_q[None, :, None, :], cos_q[None, :, None, :])
        sin_k, cos_k = _rope_tables(Lv, D_C)
        kv_r = _apply_rope(kv_c, sin_k[None], cos_k[None])
        q_r = jnp.einsum('bshq,hqr->bhsr', q_big, W_qr)
        k_r = jnp.einsum('bld,hdr->bhlr', kv_r, W_kr)
        scores = jnp.einsum('bhsr,bhlr->bhsl', q_r, k_r)
        attn = jax.nn.softmax(scores, axis=-1)
        ctx_c = jnp.einsum('bhsl,bld->bhsd', attn, kv_r)
        ctx_lat = jnp.einsum('bhsd,hkd->bhsk', ctx_c, w_kc_kv)
        ctx = ctx_lat.transpose(0, 2, 1, 3).reshape(Bv, Sv, H * K)
        return ctx @ Wo.T

    def _L0_attn_ref(hidden_states, basis_q, phase_q, amp_q, basis_k, phase_k, amp_k, basis_v, phase_v, amp_v, basis_o, phase_o, amp_o):
        import jax, jax.numpy as jnp
        import numpy as np
        HIDDEN = 512
        NUM_HEADS = 16
        HEAD_DIM = HIDDEN // NUM_HEADS
        HARMONICS = 64

        def _holo_params(key, in_features, out_features, harmonics):
            kb, kp = jax.random.split(key)
            basis = jax.random.normal(kb, (harmonics, in_features), dtype=jnp.float32)
            basis = basis / jnp.linalg.norm(basis, axis=1, keepdims=True)
            phase = jax.random.normal(kp, (out_features, harmonics), dtype=jnp.float32) * 0.1
            amp = jnp.ones((out_features, harmonics), dtype=jnp.float32) / np.sqrt(harmonics).astype(np.float32)
            return (basis, phase, amp)

        def _holo_linear(x, basis, phase, amp):
            resonance = jnp.einsum('bsd,hd->bsh', x, basis)
            w = amp * jnp.cos(phase)
            return jnp.einsum('bsh,oh->bso', resonance, w)
        bsz, seq_len, _ = hidden_states.shape
        q = _holo_linear(hidden_states, basis_q, phase_q, amp_q)
        k = _holo_linear(hidden_states, basis_k, phase_k, amp_k)
        v = _holo_linear(hidden_states, basis_v, phase_v, amp_v)
        q = q.reshape(bsz, seq_len, NUM_HEADS, HEAD_DIM).transpose(0, 2, 1, 3)
        k = k.reshape(bsz, seq_len, NUM_HEADS, HEAD_DIM).transpose(0, 2, 1, 3)
        v = v.reshape(bsz, seq_len, NUM_HEADS, HEAD_DIM).transpose(0, 2, 1, 3)
        scale = 1.0 / np.sqrt(HEAD_DIM).astype(np.float32)
        scores = jnp.einsum('bhqd,bhkd->bhqk', q, k) * scale
        attn = jax.nn.softmax(scores, axis=-1)
        out = jnp.einsum('bhqk,bhkd->bhqd', attn, v)
        out = out.transpose(0, 2, 1, 3).reshape(bsz, seq_len, HIDDEN)
        return _holo_linear(out, basis_o, phase_o, amp_o)

    def _L0_ffn_ref(x, amp_w, amp_b, ph_w, ph_b, ent_w, ent_b, ent_pw, ent_pb, path_w, path_b, phase, ln3_g, ln3_b, ln4_g, ln4_b):
        import jax, jax.numpy as jnp
        import numpy as np
        import math
        B, S, D = (2, 512, 512)
        P = 4
        PW = 2
        L = 2
        STD = 0.02
        EPS = 1e-05

        def _layer_norm(x, g, b):
            m = jnp.mean(x, axis=-1, keepdims=True)
            v = jnp.mean(jnp.square(x - m), axis=-1, keepdims=True)
            return (x - m) * jax.lax.rsqrt(v + EPS) * g + b
        amp = jax.nn.sigmoid(x @ amp_w + amp_b)
        ph = jnp.tanh(x @ ph_w + ph_b) * math.pi
        h = (jnp.cos(ph) + jnp.sin(ph)) * amp
        for l in range(L):
            e = h @ ent_w[l] + ent_b[l]
            ent = e @ ent_pw[l] + ent_pb[l]
            h = _layer_norm(h + ent, ln3_g[l], ln3_b[l])
            t = jnp.einsum('bsd,pdf->pbsf', h, path_w[l]) + path_b[l][:, None, None, :]
            mod = jnp.cos(phase[l]) + jnp.sin(phase[l])
            interf = jnp.sum(t * mod[:, None, None, :], axis=0)
            h = _layer_norm(h + interf, ln4_g[l], ln4_b[l])
        return h
    x = x + _L0_xattn_ref(_layernorm(x, axis=-1), ctx_512, L0_xattn_Wq, L0_xattn_w_kc_q, L0_xattn_w_kc_kv, L0_xattn_W_qr, L0_xattn_W_kr, L0_xattn_Wo)
    x = x + _L0_attn_ref(_layernorm(x, axis=-1), L0_attn_basis_q, L0_attn_phase_q, L0_attn_amp_q, L0_attn_basis_k, L0_attn_phase_k, L0_attn_amp_k, L0_attn_basis_v, L0_attn_phase_v, L0_attn_amp_v, L0_attn_basis_o, L0_attn_phase_o, L0_attn_amp_o)
    x = x + _L0_ffn_ref(_layernorm(x, axis=-1), L0_ffn_amp_w, L0_ffn_amp_b, L0_ffn_ph_w, L0_ffn_ph_b, L0_ffn_ent_w, L0_ffn_ent_b, L0_ffn_ent_pw, L0_ffn_ent_pb, L0_ffn_path_w, L0_ffn_path_b, L0_ffn_phase, L0_ffn_ln3_g, L0_ffn_ln3_b, L0_ffn_ln4_g, L0_ffn_ln4_b)
    return x

_drawn_inputs = setup_inputs


def setup_inputs(seed=0):
    import zlib

    import numpy as np

    out = dict(_drawn_inputs(seed))
    spreads = {'L0_attn_amp_q': (0.125, 0.6),
     'L0_attn_amp_k': (0.125, 0.583),
     'L0_attn_amp_v': (0.125, 0.2),
     'L0_attn_amp_o': (0.125, 0.2),
     'L0_ffn_amp_b': (0.0, 0.1),
     'L0_ffn_ph_b': (0.0, 0.1),
     'L0_ffn_ent_b': (0.0, 0.1),
     'L0_ffn_ent_pb': (0.0, 0.1),
     'L0_ffn_path_b': (0.0, 0.1),
     'L0_ffn_ln3_g': (1.0, 0.2),
     'L0_ffn_ln3_b': (0.0, 0.1),
     'L0_ffn_ln4_g': (1.0, 0.2),
     'L0_ffn_ln4_b': (0.0, 0.1)}
    factors = {'L0_attn_phase_q': 8.0,
     'L0_attn_phase_k': 8.0,
     'L0_attn_phase_v': 8.0,
     'L0_attn_phase_o': 8.0}
    for name, (base, spread) in spreads.items():
        noise = np.random.default_rng([zlib.crc32(name.encode()), seed]).standard_normal(out[name].shape)
        drawn = base * np.exp(spread * noise) if base else spread * noise
        out[name] = jnp.asarray(drawn.astype(out[name].dtype))
    for name, factor in factors.items():
        out[name] = (out[name] * factor).astype(out[name].dtype)
    return out
```

```python
from contextlib import ExitStack

import numpy as np
import concourse.bass as bass
from concourse import mybir

ALU = mybir.AluOpType
ACT = mybir.ActivationFunctionType
F32 = mybir.dt.float32
AX_X = mybir.AxisListType.X

P = 128
B, S, D = 64, 32, 512
L, DC = 257, 128
H, K = 16, 128
DQ, R = 384, 64
HARM, HD = 64, 32
FE = 2048
TILES = B * S // P
BT = P // S
CD, CQ, CF = D // P, DQ // P, FE // P
SG = 8
NSG = S // SG
HG = 4
EPS = 1e-5
PI = float(np.pi)

W_Q, W_KCQ, W_QR, W_QR2, W_KR, W_KV, W_O, W_ALL = np.cumsum([0, D, DQ, CQ * R, CQ * R, P, P, D]).tolist()


def wait(engine, sem, value):
    if isinstance(value, int) and value <= 0:
        return
    engine.wait_ge(sem, value)


def repeat(engine, count, body):
    body(0)
    with engine.Fori(1, count) as i:
        body(i)


class Chain:

    def __init__(self, engine, sem, per_turn=0):
        self.engine, self.sem, self.per_turn, self.base, self.n = engine, sem, per_turn, 0, 0

    def turn(self, i):
        if not isinstance(i, int) or i > 0:
            assert self.n == self.per_turn, self.n
        self.base, self.n = i * self.per_turn, 0

    def __call__(self, instruction):
        self.n += 1
        instruction.then_inc(self.sem, 1)
        self.engine.wait_ge(self.sem, self.base + self.n)


def normalise_input(nc, x, x_t, ident, eps):
    with ExitStack() as ctx:
        sb = lambda n, s: ctx.enter_context(nc.sbuf_tensor(n, s, F32))
        sem = lambda n: ctx.enter_context(nc.semaphore(n))
        xin = sb("a_xin", [P, 4, D])
        xn = sb("a_xn", [P, 4, D])
        total, neg_mean, squares, deviation, rstd = (
            sb(f"a_{n}", [P, 4]) for n in ("total", "neg_mean", "squares", "deviation", "rstd"))
        scratch = sb("a_scratch", [P, D])
        flipped = ctx.enter_context(nc.psum_tensor("a_flipped", [P, 2, D], F32))
        x_loaded = [sem(f"a_x_loaded{u}") for u in range(4)]
        normed, turned, stored, chained = sem("a_normed"), sem("a_turned"), sem("a_stored"), sem("a_chained")
        centred, squared, rooted = sem("a_centred"), sem("a_squared"), sem("a_rooted")
        x_tiles = x.rearrange("(t p) d -> t p d", p=P)
        block = ctx.enter_context(nc.Block())

        @block.sync
        def _(sp):
            def body(i):
                for u in range(4):
                    wait(sp, normed, 4 * i + u - 3)
                    sp.dma_start(xin[:, u], x_tiles[bass.ds(4 * i + u, 1)].rearrange("t p d -> p (t d)")).then_inc(x_loaded[u], 16)
            repeat(sp, TILES // 4, body)

        @block.vector
        def _(dve):
            chain = Chain(dve, chained, 5)

            def body(i):
                chain.turn(i)
                for u in range(4):
                    dve.wait_ge(x_loaded[u], 16 * (i + 1))
                    chain(nc.vector.tensor_reduce(total[:, u:u + 1], xin[:, u], AX_X, ALU.add))
                nc.vector.tensor_scalar(neg_mean[:], total[:], -1.0 / D, None, ALU.mult).then_inc(centred, 1)
                dve.wait_ge(rooted, i + 1)
                chain(nc.vector.reciprocal(rstd[:], deviation[:]))
                for u in range(4):
                    wait(dve, turned, 4 * i + u - 3)
                    nc.vector.tensor_scalar(xn[:, u], xin[:, u], neg_mean[:, u:u + 1], rstd[:, u:u + 1], ALU.add,
                                            ALU.mult).then_inc(normed, 1)
                dve.wait_ge(normed, 4 * i + 4)
            repeat(dve, TILES // 4, body)

        @block.tensor
        def _(pe):
            def body(i):
                for u in range(4):
                    pe.wait_ge(normed, 4 * i + u + 1)
                    wait(pe, stored, 4 * i + u - 1)
                    for c in range(CD):
                        last = nc.tensor.transpose(flipped[:, u % 2, c * P:(c + 1) * P], xn[:, u, c * P:(c + 1) * P], ident[:])
                    last.then_inc(turned, 1)
            repeat(pe, TILES // 4, body)

        @block.scalar
        def _(act):
            def body(i):
                act.wait_ge(centred, i + 1)
                for u in range(4):
                    wait(act, squared, 4 * i + u)
                    nc.scalar.activation(scratch[:], xin[:, u], ACT.Square, bias=neg_mean[:, u:u + 1],
                                         accum_out=squares[:, u:u + 1]).then_inc(squared, 1)
                act.wait_ge(squared, 4 * i + 4)
                nc.scalar.activation(deviation[:], squares[:], ACT.Sqrt, bias=eps[:], scale=1.0 / D).then_inc(rooted, 1)
                for u in range(4):
                    act.wait_ge(turned, 4 * i + u + 1)
                    nc.scalar.activation(
                        x_t[:, :, :, bass.ds((4 * i + u) * BT, BT)].rearrange("p c s b -> p c b s"),
                        flipped[:, u % 2].rearrange("p (c b s) -> p c b s", c=CD, b=BT), ACT.Copy).then_inc(stored, 1)
            repeat(act, TILES // 4, body)


def query_path(nc, packed, rope_q, x_t, w_vo, q_dram):
    with ExitStack() as ctx:
        sb = lambda n, s: ctx.enter_context(nc.sbuf_tensor(n, s, F32))
        sem = lambda n: ctx.enter_context(nc.semaphore(n))
        w = sb("b_w", [P, HG, W_ALL])
        table = sb("b_table", [P, 2, CQ, S])
        rot = sb("b_rot", [P, 2, CQ, SG, R])
        sin_part = sb("b_sin_part", [P, 2, CQ, SG, R])
        q_sb = sb("b_q", [P, 2, SG * B])
        m_sb = sb("b_m", [P, 2, SG * R])
        qr_sb = sb("b_qr", [R, 2, SG * B])
        staged = sb("b_staged", [P, 2, B, HG // 2, S])
        ps = ctx.enter_context(nc.psum_tensor("b_ps", [P, 8, D], F32))
        w_loaded = [sem(f"b_w_loaded{u}") for u in range(HG)]
        staged_out = [sem(f"b_staged_out{u}") for u in range(2)]
        table_loaded = sem("b_table_loaded")
        cos_ready, sin_ready, rot_ready = sem("b_cos_ready"), sem("b_sin_ready"), sem("b_rot_ready")
        a_done, a_stored = sem("b_a_done"), sem("b_a_stored")
        m_done, m_stored = sem("b_m_done"), sem("b_m_stored")
        qr_done, qr_stored = sem("b_qr_done"), sem("b_qr_stored")
        qc_done, qc_stored = sem("b_qc_done"), sem("b_qc_stored")
        STEPS = HG * NSG
        TURNS = H // HG
        LAST = TURNS * STEPS
        turn_steps = [(m // NSG, m % NSG, m) for m in range(STEPS)]
        q_out = q_dram.rearrange("b d h s -> d b (h s)")
        block = ctx.enter_context(nc.Block())

        def a_count(i, hh, g):
            return (NSG + 1) * (HG * i + hh) + g + 1

        @block.sync
        def _(sp):
            def load(i, hh):
                wait(sp, qc_done, NSG * (HG * (i - 1) + hh + 1))
                sp.dma_start(w[:, hh], packed[bass.ds(HG * i + hh, 1)].rearrange("h p n -> p (h n)")).then_inc(w_loaded[hh], 16)

            def store(i, pair):
                sp.wait_ge(qc_stored, STEPS * i + (pair + 1) * STEPS // 2)
                sp.dma_start(q_out[:, :, bass.ds((2 * i + pair) * HG // 2 * S, HG // 2 * S)],
                             staged[:, pair].rearrange("p b h s -> p b (h s)")).then_inc(staged_out[pair], 16)

            sp.dma_start(table[:], rope_q).then_inc(table_loaded, 16)
            for hh in range(HG):
                load(0, hh)
            with sp.Fori(0, TURNS - 1) as i:
                for pair in range(2):
                    load(i + 1, 2 * pair)
                    load(i + 1, 2 * pair + 1)
                    store(i, pair)
            for pair in range(2):
                store(TURNS - 1, pair)
            for pair in range(2):
                sp.wait_ge(staged_out[pair], 16 * TURNS)

        def rotated(engine, out, hh, g, column, which):
            weight = w[:, hh, column:column + CQ * R].rearrange("p (c r) -> p c r", c=CQ).unsqueeze(2)
            angle = table[:, which, :, g * SG:(g + 1) * SG].unsqueeze(3)
            shape = [P, CQ, SG, R]
            return engine.tensor_tensor(out, weight.to_broadcast(shape), angle.to_broadcast(shape), ALU.mult)

        @block.gpsimd
        def _(pool):
            pool.wait_ge(table_loaded, 16)

            def body(i):
                for hh, g, m in turn_steps:
                    n = STEPS * i + m
                    if g == 0:
                        pool.wait_ge(w_loaded[hh], 16 * (i + 1))
                    wait(pool, rot_ready, n - 1)
                    rotated(nc.gpsimd, sin_part[:, m % 2], hh, g, W_QR2, 1).then_inc(sin_ready, 1)
            repeat(pool, TURNS, body)

        @block.vector
        def _(dve):
            dve.wait_ge(table_loaded, 16)

            def store_m(n, slot):
                dve.wait_ge(m_done, n + 1)
                wait(dve, qr_done, n - 1)
                nc.vector.tensor_copy(m_sb[:, slot], ps[:, 2 + slot]).then_inc(m_stored, 1)

            def store_qc(n, m):
                hh, g = (m % STEPS) // NSG, m % NSG
                dve.wait_ge(qc_done, n + 1)
                out = staged[:, hh // 2, :, hh % 2, g * SG:(g + 1) * SG].rearrange("p b s -> p s b")
                nc.vector.tensor_copy(out, ps[:, 6 + m % 2].rearrange("p (s b) -> p s b", s=SG)).then_inc(qc_stored, 1)

            def body(i):
                first = isinstance(i, int)
                for hh, g, m in turn_steps:
                    n = STEPS * i + m
                    if g == 0:
                        dve.wait_ge(w_loaded[hh], 16 * (i + 1))
                    wait(dve, m_done, n - 1)
                    rotated(nc.vector, rot[:, m % 2], hh, g, W_QR, 0).then_inc(cos_ready, 1)
                    if m or not first:
                        store_m(n - 1, (m - 1) % 2)
                    dve.wait_ge(sin_ready, n + 1)
                    dve.wait_ge(cos_ready, n + 1)
                    nc.vector.tensor_tensor(rot[:, m % 2], rot[:, m % 2], sin_part[:, m % 2], ALU.add).then_inc(rot_ready, 1)
                    if m >= 3 or not first:
                        if (m - 3) % (STEPS // 2) == 0 and not (first and m == 3):
                            wait(dve, staged_out[(m - 3) // (STEPS // 2)], 16 * i)
                        store_qc(n - 3, m - 3)
            repeat(dve, TURNS, body)
            store_m(LAST - 1, (STEPS - 1) % 2)
            for lag in (3, 2, 1):
                store_qc(LAST - lag, STEPS - lag)

        @block.tensor
        def _(pe):
            def project_query(i, hh, g):
                if g == 0:
                    pe.wait_ge(w_loaded[hh], 16 * (i + 1))
                wait(pe, a_stored, a_count(i, hh, g) - 2)
                for c in range(CD):
                    last = nc.tensor.matmul(ps[:, (hh + g) % 2], w[:, hh, W_Q + c * P:W_Q + (c + 1) * P],
                                            x_t[:, c, g * SG:(g + 1) * SG].rearrange("p s b -> p (s b)"),
                                            start=c == 0, stop=c == CD - 1)
                last.then_inc(a_done, 1)

            def product_m(n, m, hh):
                pe.wait_ge(rot_ready, n + 1)
                wait(pe, m_stored, n - 1)
                for c in range(CQ):
                    last = nc.tensor.matmul(ps[:, 2 + m % 2], w[:, hh, W_KCQ + c * P:W_KCQ + (c + 1) * P],
                                            rot[:, m % 2, c].rearrange("p s r -> p (s r)"), start=c == 0, stop=c == CQ - 1)
                last.then_inc(m_done, 1)

            def output_weight(i, hh):
                pe.wait_ge(a_stored, a_count(i, hh, NSG) - 2)
                nc.tensor.matmul(ps[:, (hh + NSG) % 2], w[:, hh, W_KV:W_KV + P], w[:, hh, W_O:W_O + D],
                                 start=True, stop=True).then_inc(a_done, 1)

            def reduce_query(n, m, i):
                hh, g = (m % STEPS) // NSG, m % NSG
                pe.wait_ge(m_stored, n + 1)
                pe.wait_ge(a_stored, a_count(i if m >= 0 else i - 1, hh, g))
                wait(pe, qr_stored, n - 1)
                for s in range(SG):
                    last = nc.tensor.matmul(ps[0:R, 4 + m % 2, s * B:(s + 1) * B], m_sb[:, m % 2, s * R:(s + 1) * R],
                                            q_sb[:, m % 2, s * B:(s + 1) * B], start=True, stop=True)
                last.then_inc(qr_done, 1)

            def carry_query(n, m):
                hh = (m % STEPS) // NSG
                pe.wait_ge(qr_stored, n + 1)
                wait(pe, qc_stored, n - 1)
                nc.tensor.matmul(ps[:, 6 + m % 2], w[0:R, hh, W_KR:W_KR + DC], qr_sb[:, m % 2],
                                 start=True, stop=True).then_inc(qc_done, 1)

            def body(i):
                first = isinstance(i, int)
                for hh, g, m in turn_steps:
                    n = STEPS * i + m
                    project_query(i, hh, g)
                    product_m(n, m, hh)
                    if g == NSG - 1:
                        output_weight(i, hh)
                    if m >= 2 or not first:
                        carry_query(n - 2, m - 2)
                    if m >= 1 or not first:
                        reduce_query(n - 1, m - 1, i)
            repeat(pe, TURNS, body)
            carry_query(LAST - 2, STEPS - 2)
            reduce_query(LAST - 1, STEPS - 1, TURNS - 1)
            carry_query(LAST - 1, STEPS - 1)

        @block.scalar
        def _(act):
            def store_qr(n, m):
                act.wait_ge(qr_done, n + 1)
                wait(act, qc_done, n - 1)
                nc.scalar.activation(qr_sb[:, m % 2], ps[0:R, 4 + m % 2], ACT.Copy).then_inc(qr_stored, 1)

            def body(i):
                first = isinstance(i, int)
                for hh, g, m in turn_steps:
                    n = STEPS * i + m
                    act.wait_ge(a_done, a_count(i, hh, g))
                    wait(act, qr_done, n - 1)
                    nc.scalar.activation(q_sb[:, m % 2], ps[:, (hh + g) % 2], ACT.Copy).then_inc(a_stored, 1)
                    if g == NSG - 1:
                        act.wait_ge(a_done, a_count(i, hh, NSG))
                        nc.scalar.activation(w_vo[:, bass.ds(HG * i + hh, 1)].rearrange("p h n -> p (h n)"),
                                             ps[:, (hh + NSG) % 2], ACT.Copy).then_inc(a_stored, 1)
                    if m >= 1 or not first:
                        store_qr(n - 1, m - 1)
            repeat(act, TURNS, body)
            store_qr(LAST - 1, STEPS - 1)


def cross_attention(nc, cache_t, rope_kv, x, q_dram, w_vo, x1, stat, ident):
    with ExitStack() as ctx:
        sb = lambda n, s: ctx.enter_context(nc.sbuf_tensor(n, s, F32))
        sem = lambda n: ctx.enter_context(nc.semaphore(n))
        CH = H // HG
        STEPS = BT * CH
        table = sb("c_table", [P, 2, L])
        raw = sb("c_raw", [P, BT, L])
        swapped = sb("c_swapped", [P, BT, L])
        part = sb("c_part", [P, 2, L])
        kv_t = sb("c_kv_t", [P, BT, L])
        kv = sb("c_kv", [P, BT, 2, P])
        kv_end = sb("c_kv_end", [1, BT, P])
        q = sb("c_q", [P, BT, H * S])
        peak = sb("c_peak", [P, 4])
        total = sb("c_total", [P, 4])
        inverse = sb("c_inverse", [P, 4])
        e = sb("c_e", [P, 4, L])
        e_t = sb("c_e_t", [P, 2, 2, H * S])
        e_t_end = sb("c_e_t_end", [1, 2, H * S])
        mixed = sb("c_mixed", [P, H, BT, S])
        scratch = sb("c_scratch", [P, D])
        row_sum, neg_mean, squares = (sb(f"c_{n}", [P, 1]) for n in ("row_sum", "neg_mean", "squares"))
        sc_ps = ctx.enter_context(nc.psum_tensor("c_sc_ps", [P, 2, D], F32))
        et_ps = ctx.enter_context(nc.psum_tensor("c_et_ps", [P, 2, D], F32))
        mix_ps = ctx.enter_context(nc.psum_tensor("c_mix_ps", [P, 2, D], F32))
        out_ps = ctx.enter_context(nc.psum_tensor("c_out_ps", [P, D], F32))
        kv_ps = ctx.enter_context(nc.psum_tensor("c_kv_ps", [P, D], F32))
        table_loaded, x_loaded = sem("c_table_loaded"), sem("c_x_loaded")
        q_loaded = [sem(f"c_q_loaded{u}") for u in range(BT)]
        raw_loaded = [sem(f"c_raw_loaded{u}") for u in range(BT)]
        rotated_, kv_turned, kv_stored, pool_chained = sem("c_rotated"), sem("c_kv_turned"), sem("c_kv_stored"), sem("c_pool_chained")
        scored, peaked, exped, normed = sem("c_scored"), sem("c_peaked"), sem("c_exped"), sem("c_normed")
        turned, et_stored, mix_done, mix_stored = sem("c_turned"), sem("c_et_stored"), sem("c_mix_done"), sem("c_mix_stored")
        out_done, out_free, dve_chained = sem("c_out_done"), sem("c_out_free"), sem("c_dve_chained")
        centred, squared, kept = sem("c_centred"), sem("c_squared"), sem("c_kept")
        CHUNKS = B * CH
        block = ctx.enter_context(nc.Block())
        q_in = q_dram.rearrange("b d h s -> b d (h s)")

        @block.sync
        def _(sp):
            sp.dma_start(table[:], rope_kv).then_inc(table_loaded, 16)

            def body(i):
                for u in range(BT):
                    b = BT * i + u
                    wait(sp, rotated_, b - BT + 1)
                    at = bass.ds(b, 1)
                    sp.dma_start(raw[:, u], cache_t[at].rearrange("b d l -> d (b l)")).then_inc(raw_loaded[u], 16)
                    half = DC // 2
                    for lo, hi in ((0, half), (half, 0)):
                        sp.dma_start(swapped[lo:lo + half, u], cache_t[at, hi:hi + half].rearrange("b d l -> d (b l)")).then_inc(raw_loaded[u], 16)
                    wait(sp, scored, CH * (b - BT + 1))
                    sp.dma_start(q[:, u], q_in[at].rearrange("b d x -> d (b x)")).then_inc(q_loaded[u], 16)
                    if isinstance(i, int) and u == 0:
                        sp.dma_start(x1[:], x.rearrange("(t p) d -> p t d", p=P)).then_inc(x_loaded, 16)
            repeat(sp, TILES, body)

        @block.gpsimd
        def _(pool):
            pool.wait_ge(table_loaded, 16)

            def body(i):
                for u in range(BT):
                    b = BT * i + u
                    pool.wait_ge(raw_loaded[u], 48 * (i + 1))
                    nc.gpsimd.tensor_tensor(part[:, 0], raw[:, u], table[:, 0], ALU.mult).then_inc(pool_chained, 1)
                    nc.gpsimd.tensor_tensor(part[:, 1], swapped[:, u], table[:, 1], ALU.mult).then_inc(pool_chained, 1)
                    pool.wait_ge(pool_chained, 2 * b + 2)
                    wait(pool, scored, CH * (b - BT + 1))
                    wait(pool, kv_turned, b - BT + 1)
                    nc.gpsimd.tensor_tensor(kv_t[:, u], part[:, 0], part[:, 1], ALU.add).then_inc(rotated_, 1)
                    pool.wait_ge(rotated_, b + 1)
            repeat(pool, TILES, body)

        @block.vector
        def _(dve):
            def find_peak(n, j):
                dve.wait_ge(scored, n + 1)
                wait(dve, exped, n - 3)
                nc.vector.tensor_reduce(peak[:, j % 4:j % 4 + 1], sc_ps[:, j % 2, 0:L], AX_X, ALU.max,
                                        negate=True).then_inc(peaked, 1)

            def normalise(n, j):
                k = j % 4
                dve.wait_ge(exped, n + 1)
                nc.vector.reciprocal(inverse[:, k:k + 1], total[:, k:k + 1]).then_inc(dve_chained, 1)
                dve.wait_ge(dve_chained, n + 1)
                nc.vector.tensor_scalar(e[:, k], e[:, k], inverse[:, k:k + 1], None, ALU.mult).then_inc(normed, 1)

            def store_mixed(t, u):
                dve.wait_ge(mix_done, BT * t + u + 1)
                if u == 0:
                    wait(dve, out_done, t)
                nc.vector.tensor_copy(mixed[:, :, u], mix_ps[:, u % 2].rearrange("p (h s) -> p h s", h=H)).then_inc(mix_stored, 1)

            def add_out(t):
                dve.wait_ge(out_done, t + 1)
                row = x1[:, bass.ds(t, 1)].rearrange("p t d -> p (t d)")
                nc.vector.scalar_tensor_tensor(row, out_ps[:], 1.0, row, ALU.mult, ALU.add, accum_out=row_sum[:]).then_inc(out_free, 1)
                dve.wait_ge(out_free, t + 2)
                nc.vector.tensor_scalar(neg_mean[:], row_sum[:], -1.0 / D, None, ALU.mult).then_inc(centred, 1)

            def keep_moments(t):
                dve.wait_ge(squared, t + 1)
                nc.vector.tensor_copy(stat[:, 0, bass.ds(t, 1)], neg_mean[:])
                nc.vector.tensor_copy(stat[:, 1, bass.ds(t, 1)], squares[:]).then_inc(kept, 1)

            def body(i):
                first = isinstance(i, int)
                for j in range(STEPS):
                    n = STEPS * i + j
                    find_peak(n, j)
                    if j or not first:
                        normalise(n - 1, j - 1)
                    if j % CH == 2 and j > CH:
                        store_mixed(i, j // CH - 1)
                    if j == 2 and not first:
                        store_mixed(i - 1, BT - 1)
                    if j == 7 and not first:
                        add_out(i - 1)
                    if j == 12 and not first:
                        keep_moments(i - 1)
            dve.wait_ge(x_loaded, 16)
            dve.sem_inc(out_free, 1)
            dve.sem_inc(kept, 1)
            repeat(dve, TILES, body)
            normalise(CHUNKS - 1, STEPS - 1)
            store_mixed(TILES - 1, BT - 1)
            add_out(TILES - 1)
            keep_moments(TILES - 1)

        @block.scalar
        def _(act):
            def exponential(n, j):
                k = j % 4
                act.wait_ge(peaked, n + 1)
                wait(act, turned, n - 3)
                nc.scalar.activation(e[:, k], sc_ps[:, j % 2, 0:L], ACT.Exp, bias=peak[:, k:k + 1],
                                     accum_out=total[:, k:k + 1]).then_inc(exped, 1)

            def store_turned(n, b, j):
                u, c = (j // CH) % 2, j % CH
                act.wait_ge(turned, n + 1)
                if c == 0:
                    wait(act, mix_done, b - 1)
                nc.scalar.activation(e_t[:, u, :, c * P:(c + 1) * P], et_ps[:, j % 2, 0:2 * P].rearrange("p (k x) -> p k x", k=2), ACT.Copy)
                nc.scalar.activation(e_t_end[:, u, c * P:(c + 1) * P], et_ps[0:1, j % 2, 2 * P:3 * P], ACT.Copy).then_inc(et_stored, 1)

            def square_row(t):
                act.wait_ge(centred, t + 1)
                act.wait_ge(kept, t + 1)
                row = x1[:, bass.ds(t, 1)].rearrange("p t d -> p (t d)")
                nc.scalar.activation(scratch[:], row, ACT.Square, bias=neg_mean[:], accum_out=squares[:]).then_inc(squared, 1)

            def store_kv(b, u):
                act.wait_ge(kv_turned, b + 1)
                wait(act, mix_done, b - BT + 1)
                nc.scalar.activation(kv[:, u], kv_ps[:, 0:2 * P].rearrange("p (k x) -> p k x", k=2), ACT.Copy)
                nc.scalar.activation(kv_end[:, u], kv_ps[0:1, 2 * P:3 * P], ACT.Copy).then_inc(kv_stored, 1)

            def body(i):
                first = isinstance(i, int)
                for j in range(STEPS):
                    n, u = STEPS * i + j, j // CH
                    exponential(n, j)
                    if j or not first:
                        store_turned(n - 1, BT * i + (j - 1) // CH, (j - 1) % STEPS)
                    if j % CH == 1:
                        store_kv(BT * i + u, u)
                    if j == 9 and not first:
                        square_row(i - 1)
            repeat(act, TILES, body)
            store_turned(CHUNKS - 1, B - 1, STEPS - 1)
            square_row(TILES - 1)

        @block.tensor
        def _(pe):
            def score(n, b, t, j):
                u, c = j // CH, j % CH
                if c == 0:
                    pe.wait_ge(q_loaded[u], 16 * (t + 1))
                    pe.wait_ge(rotated_, b + 1)
                wait(pe, exped, n - 1)
                nc.tensor.matmul(sc_ps[:, j % 2, 0:L], q[:, u, c * P:(c + 1) * P], kv_t[:, u],
                                 start=True, stop=True).then_inc(scored, 1)

            def turn_kv(b, u):
                pe.wait_ge(rotated_, b + 1)
                wait(pe, kv_stored, b)
                for k in range(2):
                    nc.tensor.transpose(kv_ps[:, k * P:(k + 1) * P], kv_t[:, u, k * P:(k + 1) * P], ident[:])
                nc.tensor.transpose(kv_ps[0:1, 2 * P:3 * P], kv_t[:, u, 2 * P:L], ident[:]).then_inc(kv_turned, 1)

            def turn_weights(n, j):
                pe.wait_ge(normed, n + 1)
                wait(pe, et_stored, n - 1)
                for k in range(2):
                    nc.tensor.transpose(et_ps[:, j % 2, k * P:(k + 1) * P], e[:, j % 4, k * P:(k + 1) * P], ident[:])
                nc.tensor.transpose(et_ps[0:1, j % 2, 2 * P:3 * P], e[:, j % 4, 2 * P:L], ident[:]).then_inc(turned, 1)

            def mix(b, u):
                pe.wait_ge(et_stored, CH * (b + 1))
                pe.wait_ge(kv_stored, b + 1)
                wait(pe, mix_stored, b - 1)
                out = mix_ps[:, u % 2]
                for k in range(2):
                    nc.tensor.matmul(out, kv[:, u, k], e_t[:, u % 2, k], start=k == 0, stop=False)
                nc.tensor.matmul(out, kv_end[:, u], e_t_end[:, u % 2], start=False, stop=True).then_inc(mix_done, 1)

            def project(t, heads):
                if heads[0] == 0:
                    pe.wait_ge(mix_stored, BT * (t + 1))
                    pe.wait_ge(out_free, t + 1)
                for h in heads:
                    last = nc.tensor.matmul(out_ps[:], mixed[:, h].rearrange("p b s -> p (b s)"), w_vo[:, h],
                                            start=h == 0, stop=h == H - 1)
                if heads[-1] == H - 1:
                    last.then_inc(out_done, 1)

            shares = {3: range(0, 5), 4: range(5, 10), 5: range(10, H)}

            def body(i, first=False, final=False):
                for j in range(STEPS):
                    n, u = STEPS * i + j, j // CH
                    if not (final and j >= STEPS - 2):
                        ahead = (j + 2) % STEPS
                        t = i + (j + 2) // STEPS
                        score(n + 2, BT * t + ahead // CH, t, ahead)
                    if j % CH == 0:
                        turn_kv(BT * i + u, u)
                    if j in shares and not first:
                        project(i - 1, shares[j])
                    if j % CH == 1 and (j > CH or not first):
                        mix(BT * i + u - 1, (u - 1) % BT)
                    turn_weights(n, j)
            score(0, 0, 0, 0)
            score(1, 0, 0, 1)
            body(0, first=True)
            with pe.Fori(1, TILES - 1) as i:
                body(i)
            body(TILES - 1, final=True)
            mix(B - 1, BT - 1)
            project(TILES - 1, range(H))


def root_deviations(nc, stat, eps, name):
    with nc.semaphore(f"{name}_rooted") as rooted, nc.semaphore(f"{name}_inverted") as inverted, nc.Block() as block:
        @block.scalar
        def _(act):
            nc.scalar.activation(stat[:, 1], stat[:, 1], ACT.Sqrt, bias=eps[:], scale=1.0 / D).then_inc(rooted, 1)

        @block.vector
        def _(dve):
            dve.wait_ge(rooted, 1)
            nc.vector.reciprocal(stat[:, 1], stat[:, 1]).then_inc(inverted, 1)
            dve.wait_ge(inverted, 1)


MAGIC = 1.5 * 2.0 ** 23
TURN_HI = 6.28125
TURN_LO = 2 * PI - TURN_HI


def head_of(hh):
    chunk, k = divmod(hh, HG)
    return 8 * (chunk // 2) + 2 * k + chunk % 2


def holo_weights(nc, amp_nat, phase_nat, basis_t, basis_o, amp_o, phase_o, half_pi, basis, score_w, value_w, out_w):
    with ExitStack() as ctx:
        sb = lambda n, s: ctx.enter_context(nc.sbuf_tensor(n, s, F32))
        sem = lambda n: ctx.enter_context(nc.semaphore(n))
        NAT, OUT = CD * 3 * HARM, D
        amp = sb("h_amp", [P, NAT + OUT])
        phase = sb("h_phase", [P, NAT + OUT])
        turns = sb("h_turns", [P, NAT + OUT])
        bo = sb("h_bo", [P, CD, HARM])
        ps = ctx.enter_context(nc.psum_tensor("h_ps", [P, 8, 512], F32))
        loaded, cleared, stepped, cosined, weighed, multiplied, kept = (
            sem(f"h_{n}") for n in ("loaded", "cleared", "stepped", "cosined", "weighed", "multiplied", "kept"))
        block = ctx.enter_context(nc.Block())

        @block.sync
        def _(sp):
            sp.dma_start(phase[:, 0:NAT], phase_nat.rearrange("p t i -> p (t i)")).then_inc(loaded, 16)
            sp.wait_ge(cleared, 1)
            sp.dma_start(phase[0:HARM, NAT:], phase_o).then_inc(loaded, 16)
            sp.dma_start(amp[:, 0:NAT], amp_nat.rearrange("p t i -> p (t i)")).then_inc(loaded, 16)
            sp.wait_ge(cleared, 2)
            sp.dma_start(amp[0:HARM, NAT:], amp_o).then_inc(loaded, 16)
            sp.dma_start(bo[:], basis_o).then_inc(loaded, 16)
            sp.dma_start(basis[:], basis_t).then_inc(loaded, 16)
            sp.wait_ge(loaded, 96)

        @block.vector
        def _(dve):
            nc.vector.memset(phase[:, NAT:], 0.0).then_inc(cleared, 1)
            nc.vector.memset(amp[:, NAT:], 0.0).then_inc(cleared, 1)
            dve.wait_ge(loaded, 96)
            dve.wait_ge(cleared, 2)
            steps = (
                lambda: nc.vector.tensor_scalar(turns[:], phase[:], 1.0 / (2 * PI), MAGIC, ALU.mult, ALU.add),
                lambda: nc.vector.tensor_scalar(turns[:], turns[:], MAGIC, None, ALU.subtract),
                lambda: nc.vector.scalar_tensor_tensor(phase[:], turns[:], -TURN_HI, phase[:], ALU.mult, ALU.add),
                lambda: nc.vector.scalar_tensor_tensor(phase[:], turns[:], -TURN_LO, phase[:], ALU.mult, ALU.add),
            )
            for n, step in enumerate(steps):
                step().then_inc(stepped, 1)
                dve.wait_ge(stepped, n + 1)
            dve.wait_ge(cosined, 2)
            nc.vector.tensor_tensor(amp[:], amp[:], phase[:], ALU.mult).then_inc(weighed, 1)
            dve.wait_ge(weighed, 1)
            nc.vector.tensor_copy(out_w[:], amp[0:HARM, NAT:])
            dve.wait_ge(multiplied, 1)
            nc.vector.tensor_scalar(score_w[:].rearrange("p (t r) j -> p r t j", r=4),
                                    ps[0:HARM, 0:4, 0:4 * HARM].rearrange("p r (t j) -> p r t j", t=4),
                                    float(np.float32(1.0) / np.sqrt(np.float32(HD))), None, ALU.mult).then_inc(kept, 1)
            dve.wait_ge(kept, 1)

        @block.scalar
        def _(act):
            act.wait_ge(stepped, 4)
            nc.scalar.activation(phase[:], phase[:], ACT.Abs).then_inc(cosined, 1)
            act.wait_ge(cosined, 1)
            nc.scalar.activation(phase[:], phase[:], ACT.Sin, bias=half_pi[:], scale=-1.0).then_inc(cosined, 1)
            act.wait_ge(multiplied, 2)
            places = value_w[HARM:2 * HARM].rearrange("p (c cp k kp) j -> p c cp k kp j", c=2, cp=2, k=2)
            for r in range(4):
                for c in range(2):
                    nc.scalar.activation(places[:, c, r % 2, :, r // 2],
                                         ps[HARM:2 * HARM, 4 + r, c * 2 * HARM:(c + 1) * 2 * HARM].rearrange("p (k j) -> p k j", k=2), ACT.Copy)

        @block.tensor
        def _(pe):
            pe.wait_ge(weighed, 1)
            weights = amp[:, 0:NAT].rearrange("p (t w i) -> p t w i", t=CD, w=3)

            def rows(h):
                return slice(h % 4 * HD, h % 4 * HD + HD), h // 4

            for h in range(16):
                at, t = rows(h)
                last = nc.tensor.matmul(ps[0:HARM, h % 4, t * HARM:(t + 1) * HARM], weights[at, t, 0], weights[at, t, 1],
                                        start=True, stop=True)
            last.then_inc(multiplied, 1)
            for hh in range(16):
                h, c, k = head_of(hh), hh // 8, hh % 4 // 2
                at, t = rows(h)
                last = nc.tensor.matmul(ps[HARM:2 * HARM, 4 + h % 4, (2 * c + k) * HARM:(2 * c + k + 1) * HARM], weights[at, t, 2], bo[at, t],
                                        start=True, stop=True)
            last.then_inc(multiplied, 1)


def self_attention(nc, x1, stat, basis, score_w, value_w, out_w, ident):
    with ExitStack() as ctx:
        sb = lambda n, s: ctx.enter_context(nc.sbuf_tensor(n, s, F32))
        sem = lambda n: ctx.enter_context(nc.semaphore(n))
        HH = 16
        xn = sb("d_xn", [P, 2, D])
        xn_t = sb("d_xn_t", [P, CD, P])
        reduced = sb("d_reduced", [P, 2, 2, P])
        u_sb = sb("d_u", [P, 2, BT, HG, S])
        shifted = sb("d_shifted", [P, 2, HH, S])
        e = sb("d_e", [P, 2, HH, S])
        peak, total, inverse = (sb(f"d_{n}", [P, 2, HH]) for n in ("peak", "total", "inverse"))
        e_t = sb("d_e_t", [P, HH, P])
        z_sb = sb("d_z", [P, HH, HARM])
        ro_sb = sb("d_ro", [HARM, P])
        scratch = sb("d_scratch", [P, D])
        row_sum, neg_mean, squares = (sb(f"d_{n}", [P, 1]) for n in ("row_sum", "neg_mean", "squares"))
        ps = ctx.enter_context(nc.psum_tensor("d_ps", [P, 8, D], F32))
        T_BANK, R_BANK, U_BANK, S_BANK, P_BANK, Z_BANK = 0, 1, 2, 4, 5, 6
        fetched, normed, turned, turned_out = sem("d_fetched"), sem("d_normed"), sem("d_turned"), sem("d_turned_out")
        reduced_done, reduced_out = sem("d_reduced_done"), sem("d_reduced_out")
        u_done, u_out_a, u_out_d = sem("d_u_done"), sem("d_u_out_a"), sem("d_u_out_d")
        scored, peaked, shifted_out, exped, summed, inverted, weighed = (
            sem(f"d_{n}") for n in ("scored", "peaked", "shifted_out", "exped", "summed", "inverted", "weighed"))
        e_turned, e_out_a, e_out_d = sem("d_e_turned"), sem("d_e_out_a"), sem("d_e_out_d")
        z_done, z_out_a, z_out_d = sem("d_z_done"), sem("d_z_out_a"), sem("d_z_out_d")
        ro_done, ro_out, out_done, added = sem("d_ro_done"), sem("d_ro_out"), sem("d_out_done"), sem("d_added")
        centred, squared, kept, cleared = sem("d_centred"), sem("d_squared"), sem("d_kept"), sem("d_cleared")
        half_scored = sem("d_half_scored")
        TURNS = TILES // 2
        block = ctx.enter_context(nc.Block())

        def row_of(t):
            return x1[:, bass.ds(t, 1)].rearrange("p t d -> p (t d)")

        def copy_blocks(engine, batches):
            for b in batches:
                at = slice(b * S, (b + 1) * S)
                out, in_ = e_t[at, :, at], ps[at, P_BANK].rearrange("p (h s) -> p h s", h=HH)
                last = nc.vector.tensor_copy(out, in_) if engine == "dve" else nc.scalar.activation(out, in_, ACT.Copy)
            return last

        @block.gpsimd
        def _(pool):
            nc.gpsimd.memset(e_t[:], 0.0).then_inc(cleared, 1)

            def body(i):
                for v in range(2):
                    t = 2 * i + v
                    wait(pool, turned, t - 1)
                    nc.gpsimd.tensor_tensor(xn[:, v], row_of(t), stat[:, 0, bass.ds(t, 1)].to_broadcast([P, D]), ALU.add).then_inc(fetched, 1)
                    pool.wait_ge(fetched, t + 1)
                    nc.gpsimd.tensor_tensor(xn[:, v], xn[:, v], stat[:, 1, bass.ds(t, 1)].to_broadcast([P, D]), ALU.mult).then_inc(normed, 1)
            repeat(pool, TURNS, body)

        @block.tensor
        def _(pe):
            def turn_input(t, v):
                pe.wait_ge(normed, t + 1)
                wait(pe, turned_out, t)
                for c in range(CD):
                    last = nc.tensor.transpose(ps[:, T_BANK, c * P:(c + 1) * P], xn[:, v, c * P:(c + 1) * P], ident[:])
                last.then_inc(turned, 1)

            def reduce_input(t, v):
                pe.wait_ge(turned_out, t + 1)
                wait(pe, reduced_out, t)
                wait(pe, ro_out, t - 1)
                for m in range(2):
                    for c in range(CD):
                        last = nc.tensor.matmul(ps[:, R_BANK, m * P:(m + 1) * P], basis[:, c, m * P:(m + 1) * P], xn_t[:, c],
                                                start=c == 0, stop=c == CD - 1)
                last.then_inc(reduced_done, 1)

            def score_weights(t, v):
                pe.wait_ge(reduced_out, t + 1)
                wait(pe, u_out_a, t)
                wait(pe, u_out_d, t)
                for g in range(2):
                    for k in range(HG):
                        h = 8 * g + 2 * k
                        last = nc.tensor.matmul(ps[:, U_BANK + g, k * P:(k + 1) * P], score_w[:, h:h + 2].rearrange("p h j -> p (h j)"),
                                                reduced[0:HARM, v, 0], start=True, stop=True)
                last.then_inc(u_done, 1)

            def score(t, v):
                pe.wait_ge(u_out_a, t + 1)
                pe.wait_ge(u_out_d, t + 1)
                wait(pe, shifted_out, t)
                for parity in range(2):
                    if parity:
                        pe.wait_ge(half_scored, t + 1)
                    at = slice(parity * HARM, (parity + 1) * HARM)
                    for g in range(2):
                        for b in range(BT):
                            first = (2 * g + parity) * P + b * S
                            last = nc.tensor.matmul(ps[:, S_BANK, first:first + S], u_sb[at, g, b].rearrange("p k s -> p (k s)"),
                                                    reduced[at, v, 1, b * S:(b + 1) * S], start=True, stop=True)
                    last.then_inc(scored if parity else half_scored, 1)

            def value_weights(t, v):
                wait(pe, z_out_a, t)
                wait(pe, z_out_d, t)
                for g in range(2):
                    last = nc.tensor.matmul(ps[:, Z_BANK + g], reduced[HARM:2 * HARM, v, 0],
                                            value_w[HARM:2 * HARM, 8 * g:8 * g + 8].rearrange("p h j -> p (h j)"), start=True, stop=True)
                last.then_inc(z_done, 1)

            def turn_weights(t, v):
                pe.wait_ge(weighed, t + 1)
                wait(pe, added, t)
                for c in range(HG):
                    last = nc.tensor.transpose(ps[:, P_BANK, c * P:(c + 1) * P],
                                               e[:, v, 4 * c:4 * c + 4].rearrange("p b s -> p (b s)"), ident[:])
                last.then_inc(e_turned, 1)

            def mix(t):
                for done in (e_out_a, e_out_d, z_out_a, z_out_d):
                    pe.wait_ge(done, t + 1)
                for h in range(HH):
                    last = nc.tensor.matmul(ps[0:HARM, R_BANK, 2 * P:3 * P], z_sb[:, h], e_t[:, h], start=h == 0, stop=h == HH - 1)
                last.then_inc(ro_done, 1)

            def project(t):
                pe.wait_ge(ro_out, t + 1)
                nc.tensor.matmul(ps[:, P_BANK], ro_sb[:], out_w[:], start=True, stop=True).then_inc(out_done, 1)

            def step(t, v, first=False, last=False):
                if not last:
                    turn_input(t, v)
                if not first:
                    value_weights(t - 1, 1 - v)
                if not last:
                    reduce_input(t, v)
                if not first:
                    turn_weights(t - 1, 1 - v)
                if not last:
                    score_weights(t, v)
                if not first:
                    mix(t - 1)
                if not last:
                    score(t, v)
                if not first:
                    project(t - 1)

            step(0, 0, first=True)
            step(1, 1)
            with pe.Fori(1, TURNS) as i:
                step(2 * i, 0)
                step(2 * i + 1, 1)
            step(TILES, 0, last=True)

        @block.vector
        def _(dve):
            def shift(t, v):
                scores = ps[:, S_BANK].rearrange("p (h s) -> p h s", h=HH)
                dve.wait_ge(scored, t + 1)
                nc.vector.tensor_reduce(peak[:, v], scores, AX_X, ALU.max).then_inc(peaked, 1)
                dve.wait_ge(peaked, t + 1)
                nc.vector.tensor_tensor(shifted[:, v], scores, peak[:, v].unsqueeze(2).to_broadcast([P, HH, S]),
                                        ALU.subtract).then_inc(shifted_out, 1)

            def weigh(t, v):
                dve.wait_ge(exped, t + 1)
                nc.vector.tensor_reduce(total[:, v], e[:, v], AX_X, ALU.add).then_inc(summed, 1)
                dve.wait_ge(summed, t + 1)
                nc.vector.reciprocal(inverse[:, v], total[:, v]).then_inc(inverted, 1)
                dve.wait_ge(inverted, t + 1)
                nc.vector.tensor_tensor(e[:, v], e[:, v], inverse[:, v].unsqueeze(2).to_broadcast([P, HH, S]), ALU.mult).then_inc(weighed, 1)

            def step(t, v, first=False, last=False):
                if not first:
                    shift(t - 1, 1 - v)
                    dve.wait_ge(z_done, t)
                    wait(dve, ro_done, t - 1)
                    nc.vector.tensor_copy(z_sb[:, 0:8].rearrange("p h j -> p (h j)"), ps[:, Z_BANK]).then_inc(z_out_d, 1)
                    weigh(t - 1, 1 - v)
                    dve.wait_ge(e_turned, t)
                    copy_blocks("dve", (0, 1)).then_inc(e_out_d, 1)
                if not last:
                    dve.wait_ge(u_done, t + 1)
                    wait(dve, scored, t)
                    nc.vector.tensor_copy(u_sb[:, 1], ps[:, U_BANK + 1].rearrange("p (k b s) -> p b k s", k=HG, b=BT)).then_inc(u_out_d, 1)
                if not first:
                    dve.wait_ge(out_done, t)
                    nc.vector.scalar_tensor_tensor(row_of(t - 1), ps[:, P_BANK], 1.0, row_of(t - 1), ALU.mult, ALU.add,
                                                   accum_out=row_sum[:]).then_inc(added, 1)
                    dve.wait_ge(added, t)
                    nc.vector.tensor_scalar(neg_mean[:], row_sum[:], -1.0 / D, None, ALU.mult).then_inc(centred, 1)
                    dve.wait_ge(squared, t)
                    nc.vector.tensor_copy(stat[:, 0, bass.ds(t - 1, 1)], neg_mean[:])
                    nc.vector.tensor_copy(stat[:, 1, bass.ds(t - 1, 1)], squares[:]).then_inc(kept, 1)

            dve.wait_ge(cleared, 1)
            step(0, 0, first=True)
            step(1, 1)
            with dve.Fori(1, TURNS) as i:
                step(2 * i, 0)
                step(2 * i + 1, 1)
            step(TILES, 0, last=True)

        @block.scalar
        def _(act):
            def step(t, v, first=False, last=False):
                if not last:
                    act.wait_ge(turned, t + 1)
                    wait(act, reduced_done, t)
                    nc.scalar.activation(xn_t[:], ps[:, T_BANK].rearrange("p (c x) -> p c x", c=CD), ACT.Copy).then_inc(turned_out, 1)
                if not first:
                    act.wait_ge(shifted_out, t)
                    nc.scalar.activation(e[:, 1 - v], shifted[:, 1 - v], ACT.Exp).then_inc(exped, 1)
                    act.wait_ge(z_done, t)
                    wait(act, ro_done, t - 1)
                    nc.scalar.activation(z_sb[:, 8:16].rearrange("p h j -> p (h j)"), ps[:, Z_BANK + 1], ACT.Copy).then_inc(z_out_a, 1)
                if not last:
                    act.wait_ge(reduced_done, t + 1)
                    wait(act, scored, t - 1)
                    wait(act, z_done, t - 1)
                    nc.scalar.activation(reduced[:, v], ps[:, R_BANK, 0:2 * P].rearrange("p (m x) -> p m x", m=2), ACT.Copy).then_inc(reduced_out, 1)
                if not first:
                    act.wait_ge(e_turned, t)
                    copy_blocks("act", (2, 3)).then_inc(e_out_a, 1)
                if not last:
                    act.wait_ge(u_done, t + 1)
                    wait(act, scored, t)
                    nc.scalar.activation(u_sb[:, 0], ps[:, U_BANK].rearrange("p (k b s) -> p b k s", k=HG, b=BT), ACT.Copy).then_inc(u_out_a, 1)
                if not first:
                    act.wait_ge(ro_done, t)
                    wait(act, out_done, t - 1)
                    nc.scalar.activation(ro_sb[:], ps[0:HARM, R_BANK, 2 * P:3 * P], ACT.Copy).then_inc(ro_out, 1)
                    act.wait_ge(centred, t)
                    wait(act, kept, t - 1)
                    nc.scalar.activation(scratch[:], row_of(t - 1), ACT.Square, bias=neg_mean[:], accum_out=squares[:]).then_inc(squared, 1)

            act.wait_ge(cleared, 1)
            step(0, 0, first=True)
            step(1, 1)
            with act.Fori(1, TURNS) as i:
                step(2 * i, 0)
                step(2 * i + 1, 1)
            step(TILES, 0, last=True)


def fold_weights(nc, ent_in, ent_out, path, columns, rows, half_pi, ident, folded, bias, out_norm):
    LAYERS, PW, QUARTERS = 2, 2, 4
    PB, PH = LAYERS, LAYERS + LAYERS * PW
    with ExitStack() as ctx:
        sb = lambda n, s: ctx.enter_context(nc.sbuf_tensor(n, s, F32))
        sem = lambda n: ctx.enter_context(nc.semaphore(n))
        NR = LAYERS + 2 * LAYERS * PW + 2
        left = sb("f_left", [P, CF, D])
        right = sb("f_right", [P, CF, D])
        paths = sb("f_paths", [P, PW, CD, D])
        col = sb("f_col", [P, 8 * CD + LAYERS * CF])
        row = sb("f_row", [P, NR, D])
        turns = sb("f_turns", [P, LAYERS * PW, D])
        acc = sb("f_acc", [P, D])
        ones = sb("f_ones", [P, P])
        ps = ctx.enter_context(nc.psum_tensor("f_ps", [P, CD, D], F32))
        bias_ps = ctx.enter_context(nc.psum_tensor("f_bias_ps", [P, D], F32))
        small_loaded, quarter_loaded, paths_loaded = sem("f_small_loaded"), [sem(f"f_quarter_loaded{q}") for q in range(QUARTERS)], sem("f_paths_loaded")
        chained, cosined, multiplied, quarter_used, copied, pool_chained = (
            sem(f"f_{n}") for n in ("chained", "cosined", "multiplied", "quarter_used", "copied", "pool_chained"))
        accumulated, spread, modulated, stage_done = sem("f_accumulated"), sem("f_spread"), sem("f_modulated"), sem("f_stage_done")
        block = ctx.enter_context(nc.Block())
        KQ = CF // QUARTERS
        GAIN, OFFSET, ENT_B = 0, 4 * CD, 8 * CD
        MODS = slice(PH, PH + LAYERS * PW)

        @block.sync
        def _(sp):
            for l in range(LAYERS):
                for q in range(QUARTERS):
                    at = slice(q * KQ, (q + 1) * KQ)
                    if l:
                        sp.wait_ge(quarter_used, q + 1)
                        sp.wait_ge(accumulated, l * CF)
                    sp.dma_start(left[:, at], ent_in[l, :, at]).then_inc(quarter_loaded[q], 16)
                    sp.dma_start(right[:, at], ent_out[l, :, at]).then_inc(quarter_loaded[q], 16)
                    if l == 0 and q == 0:
                        sp.dma_start(col[:], columns).then_inc(small_loaded, 16)
                        sp.dma_start(row[:].rearrange("p r d -> p (r d)"), rows.rearrange("(o r) d -> o (r d)", o=1).to_broadcast([P, NR * D])).then_inc(small_loaded, 16)
                if l:
                    sp.wait_ge(pool_chained, 1 + 3 * l)
                sp.dma_start(paths[:], path[l]).then_inc(paths_loaded, 16)
            sp.wait_ge(paths_loaded, 16 * LAYERS)

        @block.gpsimd
        def _(pool):
            nc.gpsimd.memset(ones[:], 1.0).then_inc(pool_chained, 1)
            for l in range(LAYERS):
                pool.wait_ge(paths_loaded, 16 * (l + 1))
                pool.wait_ge(modulated, 1)
                for p in range(PW):
                    mod = row[:, PH + l * PW + p].unsqueeze(1).to_broadcast([P, CD, D])
                    nc.gpsimd.tensor_tensor(paths[:, p], paths[:, p], mod, ALU.mult).then_inc(pool_chained, 1)
                pool.wait_ge(pool_chained, 1 + 3 * l + 2)
                nc.gpsimd.tensor_tensor(folded[:, 2 * l + 1], paths[:, 0], paths[:, 1], ALU.add).then_inc(pool_chained, 1)
                pool.wait_ge(pool_chained, 1 + 3 * l + 3)

        @block.tensor
        def _(pe):
            pe.wait_ge(pool_chained, 1)
            for l in range(LAYERS):
                for q in range(QUARTERS):
                    pe.wait_ge(quarter_loaded[q], 32 * (l + 1))
                    for k in range(q * KQ, (q + 1) * KQ):
                        for m in range(CD):
                            if l and k == 0:
                                pe.wait_ge(copied, CD * l)
                            last = nc.tensor.matmul(ps[:, m], left[:, k, m * P:(m + 1) * P], right[:, k], start=k == 0, stop=k == CF - 1)
                    last.then_inc(quarter_used, 1)
                for part in range(2):
                    pe.wait_ge(stage_done, 2 * l + part + 1)
                    nc.tensor.matmul(bias_ps[:], ones[:], acc[:], start=True, stop=True).then_inc(spread, 1)

        @block.scalar
        def _(act):
            act.wait_ge(chained, 5)
            nc.scalar.activation(turns[:], row[:, MODS], ACT.Abs).then_inc(cosined, 1)
            act.wait_ge(cosined, 1)
            nc.scalar.activation(row[:, MODS], turns[:], ACT.Sin, bias=half_pi[:], scale=-1.0).then_inc(cosined, 1)
            for l in range(LAYERS):
                act.wait_ge(quarter_used, QUARTERS * (l + 1))
                for m in range(CD):
                    nc.scalar.activation(folded[:, 2 * l, m], ps[:, m], ACT.Copy).then_inc(copied, 1)

        @block.vector
        def _(dve):
            count = [0]

            def link(instruction):
                count[0] += 1
                instruction.then_inc(chained, 1)
                dve.wait_ge(chained, count[0])

            dve.wait_ge(small_loaded, 32)
            phases = row[:, MODS]
            link(nc.vector.tensor_scalar(phases, phases, PI / 4, None, ALU.subtract))
            link(nc.vector.tensor_scalar(turns[:], phases, 1.0 / (2 * PI), MAGIC, ALU.mult, ALU.add))
            link(nc.vector.tensor_scalar(turns[:], turns[:], MAGIC, None, ALU.subtract))
            flat = lambda a: a.rearrange("p r d -> p (r d)")
            link(nc.vector.scalar_tensor_tensor(flat(phases), flat(turns[:]), -TURN_HI, flat(phases), ALU.mult, ALU.add))
            link(nc.vector.scalar_tensor_tensor(flat(phases), flat(turns[:]), -TURN_LO, flat(phases), ALU.mult, ALU.add))
            dve.wait_ge(cosined, 2)
            nc.vector.tensor_scalar(phases, phases, float(np.sqrt(2.0)), None, ALU.mult).then_inc(modulated, 1)
            dve.wait_ge(modulated, 1)
            nc.vector.tensor_copy(out_norm[:], row[:, NR - 2:NR])
            dve.wait_ge(pool_chained, 1)
            for l in range(LAYERS):
                for part in range(2):
                    j = 2 * l + part
                    if j:
                        dve.wait_ge(spread, j)
                    if part == 0:
                        for k in range(CF):
                            if k % KQ == 0:
                                dve.wait_ge(quarter_loaded[k // KQ], 32 * (l + 1))
                            at = col[:, ENT_B + l * CF + k:ENT_B + l * CF + k + 1]
                            step = (nc.vector.tensor_scalar(acc[:], right[:, k], at, None, ALU.mult) if k == 0 else
                                    nc.vector.scalar_tensor_tensor(acc[:], right[:, k], at, acc[:], ALU.mult, ALU.add))
                            step.then_inc(accumulated, 1)
                            dve.wait_ge(accumulated, l * CF + k + 1)
                        dve.wait_ge(copied, CD * (l + 1))
                    else:
                        link(nc.vector.memset(acc[:], 0.0))
                        dve.wait_ge(pool_chained, 1 + 3 * (l + 1))
                    for m in range(CD):
                        square = folded[:, j, m, m * P:(m + 1) * P]
                        link(nc.vector.tensor_tensor(square, square, ident[:], ALU.add))
                        link(nc.vector.scalar_tensor_tensor(acc[:], folded[:, j, m], col[:, OFFSET + j * CD + m:OFFSET + j * CD + m + 1],
                                                            acc[:], ALU.mult, ALU.add))
                        last = nc.vector.tensor_scalar(folded[:, j, m], folded[:, j, m], col[:, GAIN + j * CD + m:GAIN + j * CD + m + 1], None, ALU.mult)
                    last.then_inc(stage_done, 1)
                    dve.wait_ge(spread, j + 1)
                    if part == 0:
                        link(nc.vector.tensor_tensor(bias[:, j], bias_ps[:], row[:, l], ALU.add))
                    else:
                        link(nc.vector.tensor_copy(bias[:, j], bias_ps[:]))
                        for p in range(PW):
                            r = l * PW + p
                            link(nc.vector.tensor_tensor(turns[:, r], row[:, PB + r], row[:, PH + r], ALU.mult))
                            link(nc.vector.tensor_tensor(bias[:, j], bias[:, j], turns[:, r], ALU.add))


def feed_forward(nc, x2, stat, gate_w, gate_b, folded, bias, out_norm, eps, half_pi, ident, out):
    with ExitStack() as ctx:
        sb = lambda n, s: ctx.enter_context(nc.sbuf_tensor(n, s, F32))
        sem = lambda n: ctx.enter_context(nc.semaphore(n))
        G, STEPS = 4, 4
        UNITS, TURNS = G * STEPS, TILES // G
        T = G * P
        weights = sb("e_weights", [P, 2, CD, D])
        gb = sb("e_gb", [P, 2, CD])
        minus_quarter = sb("e_minus_quarter", [P, 1])
        xn = sb("e_xn", [P, G, D])
        xn_t = sb("e_xn_t", [P, CD, T])
        angle = sb("e_angle", [P, CD, T])
        sigma = sb("e_sigma", [P, CD, T])
        h_t = sb("e_h_t", [P, 2, CD, T])
        y = sb("e_y", [P, G, D])
        result = sb("e_result", [P, G, D])
        total, neg_mean, squares, deviation, rstd = (sb(f"e_{n}", [P, G]) for n in ("total", "neg_mean", "squares", "deviation", "rstd"))
        scratch = sb("e_scratch", [P, D])
        turn_ps = ctx.enter_context(nc.psum_tensor("e_turn_ps", [P, 2, D], F32))
        mm_ps = ctx.enter_context(nc.psum_tensor("e_mm_ps", [P, 4, D], F32))
        loaded, preset = sem("e_loaded"), sem("e_preset")
        fetched, normed, x_turned, x_turned_out = sem("e_fetched"), sem("e_normed"), sem("e_x_turned"), sem("e_x_turned_out")
        gated, angled, folded_angle, sined, sigmad, h_ready = (
            sem(f"e_{n}") for n in ("gated", "angled", "folded_angle", "sined", "sigmad", "h_ready"))
        multiplied, biased, centred, squared, rooted, inverted, y_normed, y_turned, y_out = (
            sem(f"e_{n}") for n in ("multiplied", "biased", "centred", "squared", "rooted", "inverted", "y_normed", "y_turned", "y_out"))
        gained, summed, stored = sem("e_gained"), sem("e_summed"), sem("e_stored")
        block = ctx.enter_context(nc.Block())
        out_tiles = out.rearrange("(i u p) d -> i p u d", u=G, p=P)
        MM = UNITS - G

        def row_of(t):
            return x2[:, bass.ds(t, 1)].rearrange("p t d -> p (t d)")

        @block.sync
        def _(sp):
            sp.dma_start(weights[:], gate_w).then_inc(loaded, 16)
            sp.dma_start(gb[:], gate_b).then_inc(loaded, 16)

            def body(i):
                sp.wait_ge(summed, G * (i + 1))
                sp.dma_start(out_tiles[bass.ds(i, 1)].rearrange("i p u d -> p (i u) d"), result[:]).then_inc(stored, 16)
            repeat(sp, TURNS, body)
            sp.wait_ge(stored, 16 * TURNS)

        @block.gpsimd
        def _(pool):
            nc.gpsimd.memset(minus_quarter[:], -PI / 4).then_inc(preset, 1)

            def body(i):
                for u in range(G):
                    t = G * i + u
                    wait(pool, x_turned, t - G + 1)
                    nc.gpsimd.tensor_tensor(xn[:, u], row_of(t), stat[:, 0, bass.ds(t, 1)].to_broadcast([P, D]), ALU.add).then_inc(fetched, 1)
                    pool.wait_ge(fetched, t + 1)
                    nc.gpsimd.tensor_tensor(xn[:, u], xn[:, u], stat[:, 1, bass.ds(t, 1)].to_broadcast([P, D]), ALU.mult).then_inc(normed, 1)
                for u in range(G):
                    t = G * i + u
                    done = 2 * t
                    pool.wait_ge(y_normed, UNITS * i + MM + u + 1)
                    nc.gpsimd.tensor_tensor(y[:, u], y[:, u], out_norm[:, 0], ALU.mult).then_inc(gained, 1)
                    pool.wait_ge(gained, done + 1)
                    nc.gpsimd.tensor_tensor(y[:, u], y[:, u], out_norm[:, 1], ALU.add).then_inc(gained, 1)
            repeat(pool, TURNS, body)

        RING = 2 * CD + UNITS

        @block.tensor
        def _(pe):
            def turn_input(t, u):
                pe.wait_ge(normed, t + 1)
                wait(pe, x_turned_out, t - 1)
                for c in range(CD):
                    last = nc.tensor.transpose(turn_ps[:, u % 2, c * P:(c + 1) * P], xn[:, u, c * P:(c + 1) * P], ident[:])
                last.then_inc(x_turned, 1)

            def free_bank(i, r):
                before = r - 4
                if before < 0:
                    before += RING
                    i = i - 1
                if isinstance(i, int) and i < 0:
                    return
                if before < CD:
                    pe.wait_ge(angled, CD * i + before + 1)
                elif before < 2 * CD:
                    pe.wait_ge(sigmad, CD * i + before - CD + 1)
                else:
                    pe.wait_ge(biased, UNITS * i + before - 2 * CD + 1)

            def gate(i, r):
                free_bank(i, r)
                which, f = divmod(r, CD)
                for c in range(CD):
                    last = nc.tensor.matmul(mm_ps[:, r % 4], weights[:, which, c, f * P:(f + 1) * P], xn_t[:, c], start=c == 0, stop=c == CD - 1)
                last.then_inc(gated, 1)

            def multiply(i, q):
                j, u = divmod(q, G)
                if q == 0:
                    pe.wait_ge(h_ready, CD * (i + 1))
                if j:
                    pe.wait_ge(y_out, MM * i + q - G + 1)
                free_bank(i, 2 * CD + q)
                for c in range(CD):
                    last = nc.tensor.matmul(mm_ps[:, q % 4], h_t[:, j % 2, c, u * P:(u + 1) * P], folded[:, j, c], start=c == 0, stop=c == CD - 1)
                last.then_inc(multiplied, 1)

            def turn_y(i, q):
                pe.wait_ge(y_normed, UNITS * i + q + 1)
                if q >= 2:
                    pe.wait_ge(y_out, MM * i + q - 1)
                for c in range(CD):
                    last = nc.tensor.transpose(turn_ps[:, q % 2, c * P:(c + 1) * P], y[:, q % G, c * P:(c + 1) * P], ident[:])
                last.then_inc(y_turned, 1)

            pe.wait_ge(loaded, 32)

            def body(i):
                for u in range(G):
                    turn_input(G * i + u, u)
                pe.wait_ge(x_turned_out, G * (i + 1))
                for r in range(2 * CD):
                    gate(i, r)
                for q in range(UNITS):
                    multiply(i, q)
                    if 2 <= q < MM + 2:
                        turn_y(i, q - 2)
            repeat(pe, TURNS, body)

        @block.scalar
        def _(act):
            act.wait_ge(loaded, 32)
            act.wait_ge(preset, 1)

            def body(i):
                for u in range(G):
                    t = G * i + u
                    act.wait_ge(x_turned, t + 1)
                    if u == 0:
                        wait(act, gated, 2 * CD * i)
                    nc.scalar.activation(xn_t[:, :, u * P:(u + 1) * P], turn_ps[:, u % 2].rearrange("p (c x) -> p c x", c=CD), ACT.Copy).then_inc(x_turned_out, 1)
                for f in range(CD):
                    act.wait_ge(gated, 2 * CD * i + f + 1)
                    if f == 0:
                        wait(act, h_ready, CD * i)
                    nc.scalar.activation(angle[:, f], mm_ps[:, f], ACT.Tanh, bias=gb[:, 0, f:f + 1]).then_inc(angled, 1)
                act.wait_ge(angled, CD * (i + 1))
                nc.scalar.activation(angle[:], angle[:], ACT.Abs, bias=minus_quarter[:], scale=PI).then_inc(folded_angle, 1)
                act.wait_ge(folded_angle, i + 1)
                nc.scalar.activation(angle[:], angle[:], ACT.Sin, bias=half_pi[:], scale=-1.0).then_inc(sined, 1)
                for f in range(CD):
                    act.wait_ge(gated, 2 * CD * i + CD + f + 1)
                    nc.scalar.activation(sigma[:, f], mm_ps[:, f], ACT.Sigmoid, bias=gb[:, 1, f:f + 1]).then_inc(sigmad, 1)
                for q in range(UNITS):
                    u = q % G
                    n = UNITS * i + q
                    act.wait_ge(centred, n + 1)
                    wait(act, rooted, n)
                    nc.scalar.activation(scratch[:], y[:, u], ACT.Square, bias=neg_mean[:, u:u + 1], accum_out=squares[:, u:u + 1]).then_inc(squared, 1)
                    act.wait_ge(squared, n + 1)
                    nc.scalar.activation(deviation[:, u:u + 1], squares[:, u:u + 1], ACT.Sqrt, bias=eps[:], scale=1.0 / D).then_inc(rooted, 1)
                    if 3 <= q < MM + 3:
                        store_turned(i, q - 3)

            def store_turned(i, q):
                j, u = divmod(q, G)
                act.wait_ge(y_turned, MM * i + q + 1)
                if j:
                    act.wait_ge(multiplied, UNITS * i + G * j)
                nc.scalar.activation(h_t[:, (j + 1) % 2, :, u * P:(u + 1) * P], turn_ps[:, q % 2].rearrange("p (c x) -> p c x", c=CD), ACT.Copy).then_inc(y_out, 1)

            repeat(act, TURNS, body)

        @block.vector
        def _(dve):
            def take(i, q):
                j, u = divmod(q, G)
                n = UNITS * i + q
                dve.wait_ge(multiplied, n + 1)
                if q >= G:
                    dve.wait_ge(y_turned, MM * i + q - G + 1)
                else:
                    wait(dve, summed, G * (i - 1) + u + 1)
                nc.vector.scalar_tensor_tensor(y[:, u], mm_ps[:, q % 4], 1.0, bias[:, j], ALU.mult, ALU.add, accum_out=total[:, u:u + 1]).then_inc(biased, 1)
                dve.wait_ge(biased, n + 1)
                nc.vector.tensor_scalar(neg_mean[:, u:u + 1], total[:, u:u + 1], -1.0 / D, None, ALU.mult).then_inc(centred, 1)

            def normalise(i, q):
                u, n = q % G, UNITS * i + q
                dve.wait_ge(rooted, n + 1)
                nc.vector.reciprocal(rstd[:, u:u + 1], deviation[:, u:u + 1]).then_inc(inverted, 1)
                dve.wait_ge(inverted, n + 1)
                nc.vector.tensor_scalar(y[:, u], y[:, u], neg_mean[:, u:u + 1], rstd[:, u:u + 1], ALU.add, ALU.mult).then_inc(y_normed, 1)

            def body(i):
                dve.wait_ge(sined, i + 1)
                dve.wait_ge(sigmad, CD * i + 1)
                if not isinstance(i, int):
                    dve.wait_ge(multiplied, UNITS * i - G)
                for f in range(CD):
                    dve.wait_ge(sigmad, CD * i + f + 1)
                    nc.vector.scalar_tensor_tensor(h_t[:, 0, f], angle[:, f], float(np.sqrt(2.0)), sigma[:, f], ALU.mult, ALU.mult).then_inc(h_ready, 1)
                for q in range(UNITS):
                    take(i, q)
                    if q:
                        normalise(i, q - 1)
                normalise(i, UNITS - 1)
                wait(dve, stored, 16 * i)
                for u in range(G):
                    dve.wait_ge(gained, 2 * (G * i + u + 1))
                    nc.vector.scalar_tensor_tensor(result[:, u], y[:, u], 1.0, row_of(G * i + u), ALU.mult, ALU.add).then_inc(summed, 1)
            repeat(dve, TURNS, body)


def perceiver_block(nc, x, cache_t, packed, rope_q, rope_kv, amp_nat, phase_nat, basis_t, basis_o, amp_o, phase_o,
                    ent_in, ent_out, path, columns, rows, gate_w, gate_b, out):
    q_dram = nc.dram_tensor("carried_queries", (B, DC, H, S), F32, kind="Internal").ap()
    with ExitStack() as ctx:
        sb = lambda n, s: ctx.enter_context(nc.sbuf_tensor(n, s, F32))
        ident = sb("ident", [P, P])
        stat = sb("stat", [P, 2, TILES])
        eps = sb("eps", [P, 1])
        half_pi = sb("half_pi", [P, 1])
        ready = ctx.enter_context(nc.semaphore("ident_ready"))
        with nc.Block() as block:
            @block.gpsimd
            def _(pool):
                nc.gpsimd.memset(ident[:], 0.0).then_inc(ready, 1)
                nc.gpsimd.memset(eps[:], EPS).then_inc(ready, 1)
                nc.gpsimd.memset(half_pi[:], PI / 2).then_inc(ready, 1)
                pool.wait_ge(ready, 3)
                nc.gpsimd.affine_select(out=ident[:], in_=ident[:], compare_op=ALU.not_equal, fill=1.0,
                                        base=0, pattern=[[-1, P]], channel_multiplier=1).then_inc(ready, 1)
                pool.wait_ge(ready, 4)
        basis, score_w, value_w, out_w = (sb("basis", [P, CD, 2 * P]), sb("score_w", [HARM, 16, HARM]),
                                          sb("value_w", [P, 16, HARM]), sb("out_w", [HARM, D]))
        holo_weights(nc, amp_nat, phase_nat, basis_t, basis_o, amp_o, phase_o, half_pi, basis, score_w, value_w, out_w)
        stream, product = sb("stream", [P, TILES * D]), sb("product", [P, H * D])
        x_t = stream[:].rearrange("p (c s b) -> p c s b", c=CD, s=S)
        w_vo = product[:].rearrange("p (h d) -> p h d", h=H)
        normalise_input(nc, x, x_t, ident, eps)
        query_path(nc, packed, rope_q, x_t, w_vo, q_dram)
        x1 = stream[:].rearrange("p (t d) -> p t d", t=TILES)
        cross_attention(nc, cache_t, rope_kv, x, q_dram, w_vo, x1, stat, ident)
        root_deviations(nc, stat, eps, "x1")
        self_attention(nc, x1, stat, basis, score_w, value_w, out_w, ident)
        root_deviations(nc, stat, eps, "x2")
        folded = product[:].rearrange("p (j c d) -> p j c d", j=4, c=CD)
        bias, out_norm = sb("bias", [P, 4, D]), sb("out_norm", [P, 2, D])
        fold_weights(nc, ent_in, ent_out, path, columns, rows, half_pi, ident, folded, bias, out_norm)
        feed_forward(nc, x1, stat, gate_w, gate_b, folded, bias, out_norm, eps, half_pi, ident, out)


def rope_tables(length, dim):
    inv = (1.0 / 10000.0 ** (np.arange(0, dim, 2, dtype=np.float32) / np.float32(dim))).astype(np.float32)
    f = np.arange(length, dtype=np.float32)[:, None] * inv[None, :]
    sin = np.repeat(np.sin(f.astype(np.float64)).astype(np.float32), 2, axis=-1)
    cos = np.repeat(np.cos(f.astype(np.float64)).astype(np.float32), 2, axis=-1)
    return sin, cos


def kernel(**inputs):
    import concourse.bacc as bacc
    from concourse.bass_utils import run_bass_kernel_spmd

    g = {name.replace("L0_", ""): np.asarray(a) for name, a in inputs.items()}
    sin_q, cos_q = rope_tables(S, DQ)
    sin_k, cos_k = rope_tables(L, DC)
    sign_q = np.where(np.arange(DQ) < DQ // 2, np.float32(1), np.float32(-1))
    swap_q = (np.arange(DQ) + DQ // 2) % DQ
    rope_q = np.stack([cos_q.T, (sin_q[:, swap_q] * sign_q).T]).reshape(2, CQ, P, S).transpose(2, 0, 1, 3)
    sign_k = np.where(np.arange(DC) < DC // 2, np.float32(-1), np.float32(1))
    rope_kv = np.stack([cos_k.T, (sin_k * sign_k).T], axis=1)

    w_qr = g["xattn_W_qr"]
    w_qr2 = np.concatenate([w_qr[:, DQ // 2:], w_qr[:, :DQ // 2]], axis=1)
    rows = lambda a, c: a.reshape(H, c, P, -1).transpose(0, 2, 1, 3).reshape(H, P, -1)
    w_kr = np.zeros((H, P, P), np.float32)
    w_kr[:, :R] = g["xattn_W_kr"].transpose(0, 2, 1)
    packed = np.concatenate([
        rows(g["xattn_Wq"].reshape(H, K, D).transpose(0, 2, 1), CD),
        rows(g["xattn_w_kc_q"].transpose(0, 2, 1), CQ),
        rows(w_qr, CQ), rows(w_qr2, CQ), w_kr, g["xattn_w_kc_kv"],
        g["xattn_Wo"].T.reshape(H, K, D)], axis=2)

    by_row = lambda a: a.reshape(CD, P, -1).transpose(1, 0, 2)
    three = lambda kind: by_row(np.concatenate([g[f"attn_{kind}_{n}"] for n in "qkv"], axis=1))

    column = lambda a: a.reshape(-1, P).T
    gains = [np.ones(D, np.float32), g["ffn_ln3_g"][0], g["ffn_ln4_g"][0], g["ffn_ln3_g"][1]]
    offsets = [np.zeros(D, np.float32), g["ffn_ln3_b"][0], g["ffn_ln4_b"][0], g["ffn_ln3_b"][1]]
    columns = np.concatenate([column(a) for a in (*gains, *offsets, *g["ffn_ent_b"])], axis=1)
    rows_ = np.concatenate([g["ffn_ent_pb"], g["ffn_path_b"].reshape(-1, D), g["ffn_phase"].reshape(-1, D),
                            g["ffn_ln4_g"][1:], g["ffn_ln4_b"][1:]])
    ent = lambda a: a.reshape(2, CF, P, D).transpose(0, 2, 1, 3)

    arrays = {
        "x": g["x"].reshape(B * S, D), "cache_t": g["ctx_512"].transpose(0, 2, 1), "packed": packed,
        "rope_q": rope_q, "rope_kv": rope_kv,
        "amp_nat": three("amp"), "phase_nat": three("phase"),
        "basis_t": by_row(np.concatenate([g[f"attn_basis_{n}"].T for n in "qvkk"], axis=1)),
        "basis_o": by_row(g["attn_basis_o"].T), "amp_o": g["attn_amp_o"].T, "phase_o": g["attn_phase_o"].T,
        "ent_in": ent(g["ffn_ent_w"].transpose(0, 2, 1)), "ent_out": ent(g["ffn_ent_pw"]),
        "path": g["ffn_path_w"].reshape(2, 2, CD, P, D).transpose(0, 3, 1, 2, 4),
        "columns": columns, "rows": rows_,
        "gate_w": np.stack([by_row(g["ffn_ph_w"]), by_row(g["ffn_amp_w"])], axis=1),
        "gate_b": np.stack([column(g["ffn_ph_b"]), column(g["ffn_amp_b"])], axis=1),
    }
    arrays = {name: np.ascontiguousarray(a) for name, a in arrays.items()}
    nc = bacc.Bacc("TRN2", target_bir_lowering=False, num_devices=1)
    args = [nc.dram_tensor(name, a.shape, mybir.dt.from_np(a.dtype), kind="ExternalInput").ap() for name, a in arrays.items()]
    out = nc.dram_tensor("out", (B * S, D), F32, kind="ExternalOutput").ap()
    perceiver_block(nc, *args, out)
    result = run_bass_kernel_spmd(nc, [arrays], core_ids=[0])
    return result.results[0]["out"].reshape(B, S, D)
```

```python
from contextlib import ExitStack

import numpy as np
import concourse.bass as bass
from concourse import mybir

ALU = mybir.AluOpType
ACT = mybir.ActivationFunctionType
F32 = mybir.dt.float32
F32R = mybir.dt.float32r
AX_X = mybir.AxisListType.X

P = 128
B, S, D = 64, 32, 512
L, DC = 257, 128
H, K = 16, 128
DQ, R = 384, 64
HARM, HD = 64, 32
FE = 2048
TILES = B * S // P
BT = P // S
CD, CQ, CF = D // P, DQ // P, FE // P
SG = 8
NSG = S // SG
HG = 4
EPS = 1e-5
PI = float(np.pi)

W_Q, W_KCQ, W_QR, W_QR2, W_KR, W_KV, W_O, W_ALL = np.cumsum([0, D, DQ, CQ * R, CQ * R, P, P, D]).tolist()


def wait(engine, sem, value):
    if isinstance(value, int) and value <= 0:
        return
    engine.wait_ge(sem, value)


def repeat(engine, count, body):
    body(0)
    with engine.Fori(1, count) as i:
        body(i)


def repeat_to_last(engine, count, body):
    body(0)
    with engine.Fori(1, count - 1) as i:
        body(i)
    body(count - 1, final=True)


def multiply_parts(nc, out, left, right, start, stop):
    nc.tensor.matmul(out, left[0], right[0], start=start, stop=False)
    nc.tensor.matmul(out, left[0], right[1], start=False, stop=False)
    return nc.tensor.matmul(out, left[1], right[0], start=False, stop=stop)


def low_part(nc, low, value, high):
    return nc.vector.tensor_tensor(low, value, high.bitcast(F32), ALU.subtract)


class Chain:

    def __init__(self, engine, sem, per_turn=0):
        self.engine, self.sem, self.per_turn, self.base, self.n = engine, sem, per_turn, 0, 0

    def turn(self, i):
        if not isinstance(i, int) or i > 0:
            assert self.n == self.per_turn, self.n
        self.base, self.n = i * self.per_turn, 0

    def __call__(self, instruction):
        self.n += 1
        instruction.then_inc(self.sem, 1)
        self.engine.wait_ge(self.sem, self.base + self.n)


def normalise_input(nc, x, x_t, ident, eps):
    with ExitStack() as ctx:
        sb = lambda n, s: ctx.enter_context(nc.sbuf_tensor(n, s, F32))
        sem = lambda n: ctx.enter_context(nc.semaphore(n))
        xin = sb("a_xin", [P, 4, D])
        xn = sb("a_xn", [P, 4, D])
        total, neg_mean, squares, deviation, rstd = (
            sb(f"a_{n}", [P, 4]) for n in ("total", "neg_mean", "squares", "deviation", "rstd"))
        scratch = sb("a_scratch", [P, D])
        flipped = ctx.enter_context(nc.psum_tensor("a_flipped", [P, 2, D], F32))
        x_loaded = [sem(f"a_x_loaded{u}") for u in range(4)]
        normed, turned, stored, chained = sem("a_normed"), sem("a_turned"), sem("a_stored"), sem("a_chained")
        centred, squared, rooted, rounded = sem("a_centred"), sem("a_squared"), sem("a_rooted"), sem("a_rounded")
        x_tiles = x.rearrange("(t p) d -> t p d", p=P)

        def placed(part, t):
            return part[:, :, :, bass.ds(t * BT, BT)].rearrange("p c s b -> p c b s")

        def by_batch(u):
            return flipped[:, u % 2].rearrange("p (c b s) -> p c b s", c=CD, b=BT)

        block = ctx.enter_context(nc.Block())

        @block.sync
        def _(sp):
            def body(i):
                for u in range(4):
                    wait(sp, normed, 4 * i + u - 3)
                    sp.dma_start(xin[:, u], x_tiles[bass.ds(4 * i + u, 1)].rearrange("t p d -> p (t d)")).then_inc(x_loaded[u], 16)
            repeat(sp, TILES // 4, body)

        @block.vector
        def _(dve):
            chain = Chain(dve, chained, 5)

            def body(i):
                chain.turn(i)
                for u in range(4):
                    dve.wait_ge(x_loaded[u], 16 * (i + 1))
                    chain(nc.vector.tensor_reduce(total[:, u:u + 1], xin[:, u], AX_X, ALU.add))
                nc.vector.tensor_scalar(neg_mean[:], total[:], -1.0 / D, None, ALU.mult).then_inc(centred, 1)
                dve.wait_ge(rooted, i + 1)
                chain(nc.vector.reciprocal(rstd[:], deviation[:]))
                for u in range(4):
                    wait(dve, turned, 4 * i + u - 3)
                    nc.vector.tensor_scalar(xn[:, u], xin[:, u], neg_mean[:, u:u + 1], rstd[:, u:u + 1], ALU.add,
                                            ALU.mult).then_inc(normed, 1)
                for u in range(4):
                    dve.wait_ge(rounded, 4 * i + u + 1)
                    low_part(nc, placed(x_t[1], 4 * i + u), by_batch(u), placed(x_t[0], 4 * i + u)).then_inc(stored, 1)
            repeat(dve, TILES // 4, body)

        @block.tensor
        def _(pe):
            def body(i):
                for u in range(4):
                    pe.wait_ge(normed, 4 * i + u + 1)
                    wait(pe, stored, 4 * i + u - 1)
                    for c in range(CD):
                        last = nc.tensor.transpose(flipped[:, u % 2, c * P:(c + 1) * P], xn[:, u, c * P:(c + 1) * P], ident[:])
                    last.then_inc(turned, 1)
            repeat(pe, TILES // 4, body)

        @block.scalar
        def _(act):
            def body(i):
                act.wait_ge(centred, i + 1)
                for u in range(4):
                    wait(act, squared, 4 * i + u)
                    nc.scalar.activation(scratch[:], xin[:, u], ACT.Square, bias=neg_mean[:, u:u + 1],
                                         accum_out=squares[:, u:u + 1]).then_inc(squared, 1)
                act.wait_ge(squared, 4 * i + 4)
                nc.scalar.activation(deviation[:], squares[:], ACT.Sqrt, bias=eps[:], scale=1.0 / D).then_inc(rooted, 1)
                for u in range(4):
                    act.wait_ge(turned, 4 * i + u + 1)
                    nc.scalar.activation(placed(x_t[0], 4 * i + u), by_batch(u), ACT.Copy).then_inc(rounded, 1)
            repeat(act, TILES // 4, body)


def query_path(nc, packed, rope_q, x_t, w_vo_dram, q_dram):
    with ExitStack() as ctx:
        sb = lambda n, s: ctx.enter_context(nc.sbuf_tensor(n, s, F32))
        sem = lambda n: ctx.enter_context(nc.semaphore(n))
        pair = lambda n, s: [ctx.enter_context(nc.sbuf_tensor(f"{n}_{part}", s, F32R)) for part in ("high", "low")]
        w = sb("b_w", [P, HG, W_ALL])
        w_parts = pair("b_w_parts", [P, 2, W_QR])
        table = sb("b_table", [P, 2, CQ, S])
        rot = sb("b_rot", [P, 2, CQ, SG, R])
        rot_parts = pair("b_rot_parts", [P, 2, CQ, SG, R])
        sin_part = sb("b_sin_part", [P, 2, CQ, SG, R])
        q_sb = sb("b_q", [P, 2, SG * B])
        m_sb = sb("b_m", [P, 2, SG * R])
        qr_sb = sb("b_qr", [R, 2, SG * B])
        w_vo = sb("b_w_vo", [P, 2, D])
        staged = sb("b_staged", [P, 2, B, HG // 2, S])
        ps = ctx.enter_context(nc.psum_tensor("b_ps", [P, 8, D], F32))
        w_loaded = [sem(f"b_w_loaded{u}") for u in range(HG)]
        staged_out = [sem(f"b_staged_out{u}") for u in range(2)]
        w_vo_out = [sem(f"b_w_vo_out{u}") for u in range(2)]
        table_loaded = sem("b_table_loaded")
        cos_ready, sin_ready, rot_summed, rot_rounded, rot_ready = (
            sem(f"b_{n}") for n in ("cos_ready", "sin_ready", "rot_summed", "rot_rounded", "rot_ready"))
        w_rounded, w_split = sem("b_w_rounded"), sem("b_w_split")
        a_done, a_stored = sem("b_a_done"), sem("b_a_stored")
        m_done, m_stored = sem("b_m_done"), sem("b_m_stored")
        qr_done, qr_stored = sem("b_qr_done"), sem("b_qr_stored")
        qc_done, qc_stored = sem("b_qc_done"), sem("b_qc_stored")
        STEPS = HG * NSG
        TURNS = H // HG
        LAST = TURNS * STEPS
        turn_steps = [(m // NSG, m % NSG, m) for m in range(STEPS)]
        q_out = q_dram.rearrange("b d h s -> d b (h s)")
        block = ctx.enter_context(nc.Block())

        def a_count(i, hh, g):
            return (NSG + 1) * (HG * i + hh) + g + 1

        @block.sync
        def _(sp):
            def load(i, hh):
                wait(sp, qc_done, NSG * (HG * (i - 1) + hh + 1))
                sp.dma_start(w[:, hh], packed[bass.ds(HG * i + hh, 1)].rearrange("h p n -> p (h n)")).then_inc(w_loaded[hh], 16)

            def store(i, pair):
                sp.wait_ge(qc_stored, STEPS * i + (pair + 1) * STEPS // 2)
                sp.dma_start(q_out[:, :, bass.ds((2 * i + pair) * HG // 2 * S, HG // 2 * S)],
                             staged[:, pair].rearrange("p b h s -> p b (h s)")).then_inc(staged_out[pair], 16)

            def store_weights(i, hh):
                sp.wait_ge(a_stored, a_count(i, hh, NSG))
                sp.dma_start(w_vo_dram[:, bass.ds(HG * i + hh, 1)].rearrange("p h n -> p (h n)"), w_vo[:, hh % 2]).then_inc(w_vo_out[hh % 2], 16)

            sp.dma_start(table[:], rope_q).then_inc(table_loaded, 16)
            for hh in range(HG):
                load(0, hh)
            with sp.Fori(0, TURNS - 1) as i:
                for pair in range(2):
                    for hh in (2 * pair, 2 * pair + 1):
                        store_weights(i, hh)
                        load(i + 1, hh)
                    store(i, pair)
            for pair in range(2):
                for hh in (2 * pair, 2 * pair + 1):
                    store_weights(TURNS - 1, hh)
                store(TURNS - 1, pair)
            for pair in range(2):
                sp.wait_ge(staged_out[pair], 16 * TURNS)
                sp.wait_ge(w_vo_out[pair], 16 * 2 * TURNS)

        def rotated(engine, out, hh, g, column, which):
            weight = w[:, hh, column:column + CQ * R].rearrange("p (c r) -> p c r", c=CQ).unsqueeze(2)
            angle = table[:, which, :, g * SG:(g + 1) * SG].unsqueeze(3)
            shape = [P, CQ, SG, R]
            return engine.tensor_tensor(out, weight.to_broadcast(shape), angle.to_broadcast(shape), ALU.mult)

        @block.gpsimd
        def _(pool):
            pool.wait_ge(table_loaded, 16)

            def body(i):
                for hh, g, m in turn_steps:
                    n = STEPS * i + m
                    if g == 0:
                        pool.wait_ge(w_loaded[hh], 16 * (i + 1))
                    wait(pool, rot_summed, n - 1)
                    rotated(nc.gpsimd, sin_part[:, m % 2], hh, g, W_QR2, 1).then_inc(sin_ready, 1)
            repeat(pool, TURNS, body)

        @block.vector
        def _(dve):
            def store_m(n, slot):
                dve.wait_ge(m_done, n + 1)
                wait(dve, qr_done, n - 1)
                nc.vector.tensor_copy(m_sb[:, slot], ps[:, 2 + slot]).then_inc(m_stored, 1)

            def split_weights(head, hh):
                dve.wait_ge(w_rounded, head + 1)
                low_part(nc, w_parts[1][:, hh % 2], w[:, hh, 0:W_QR], w_parts[0][:, hh % 2]).then_inc(w_split, 1)

            def cos_part(i, n, m):
                hh, g = m // NSG, m % NSG
                if g == 0:
                    dve.wait_ge(w_loaded[hh], 16 * (i + 1))
                wait(dve, rot_ready, n - 1)
                rotated(nc.vector, rot[:, m % 2], hh, g, W_QR, 0).then_inc(cos_ready, 1)

            def add_sin_part(n, m):
                dve.wait_ge(sin_ready, n + 1)
                dve.wait_ge(cos_ready, n + 1)
                nc.vector.tensor_tensor(rot[:, m % 2], rot[:, m % 2], sin_part[:, m % 2], ALU.add).then_inc(rot_summed, 1)

            dve.wait_ge(table_loaded, 16)
            cos_part(0, 0, 0)
            add_sin_part(0, 0)
            split_weights(0, 0)

            def body(i, final=False):
                first = isinstance(i, int) and i == 0
                for hh, g, m in turn_steps:
                    n = STEPS * i + m
                    more = not (final and m == STEPS - 1)
                    if more:
                        cos_part(i + (m + 1) // STEPS, n + 1, (m + 1) % STEPS)
                    if m or not first:
                        store_m(n - 1, (m - 1) % 2)
                    dve.wait_ge(rot_rounded, n + 1)
                    low_part(nc, rot_parts[1][:, m % 2], rot[:, m % 2], rot_parts[0][:, m % 2]).then_inc(rot_ready, 1)
                    if more:
                        add_sin_part(n + 1, (m + 1) % 2)
                    if g == 2 and not (final and hh == HG - 1):
                        split_weights(HG * i + hh + 1, (hh + 1) % HG)
            repeat_to_last(dve, TURNS, body)
            store_m(LAST - 1, (STEPS - 1) % 2)

        @block.tensor
        def _(pe):
            def project_query(i, hh, g):
                if g == 0:
                    pe.wait_ge(w_split, HG * i + hh + 1)
                wait(pe, a_stored, a_count(i, hh, g) - 2)
                for c in range(CD):
                    last = multiply_parts(nc, ps[:, (hh + g) % 2], [a[:, hh % 2, W_Q + c * P:W_Q + (c + 1) * P] for a in w_parts],
                                          [a[:, c, g * SG:(g + 1) * SG].rearrange("p s b -> p (s b)") for a in x_t],
                                          c == 0, c == CD - 1)
                last.then_inc(a_done, 1)

            def product_m(n, m, hh):
                pe.wait_ge(rot_ready, n + 1)
                wait(pe, m_stored, n - 1)
                for c in range(CQ):
                    last = multiply_parts(nc, ps[:, 2 + m % 2], [a[:, hh % 2, W_KCQ + c * P:W_KCQ + (c + 1) * P] for a in w_parts],
                                          [a[:, m % 2, c].rearrange("p s r -> p (s r)") for a in rot_parts], c == 0, c == CQ - 1)
                last.then_inc(m_done, 1)

            def output_weight(i, hh):
                pe.wait_ge(a_stored, a_count(i, hh, NSG) - 2)
                nc.tensor.matmul(ps[:, (hh + NSG) % 2], w[:, hh, W_KV:W_KV + P], w[:, hh, W_O:W_O + D],
                                 start=True, stop=True).then_inc(a_done, 1)

            def reduce_query(n, m, i):
                hh, g = (m % STEPS) // NSG, m % NSG
                pe.wait_ge(m_stored, n + 1)
                pe.wait_ge(a_stored, a_count(i if m >= 0 else i - 1, hh, g))
                wait(pe, qr_stored, n - 1)
                for s in range(SG):
                    last = nc.tensor.matmul(ps[0:R, 4 + m % 2, s * B:(s + 1) * B], m_sb[:, m % 2, s * R:(s + 1) * R],
                                            q_sb[:, m % 2, s * B:(s + 1) * B], start=True, stop=True)
                last.then_inc(qr_done, 1)

            def carry_query(n, m):
                hh = (m % STEPS) // NSG
                pe.wait_ge(qr_stored, n + 1)
                wait(pe, qc_stored, n - 1)
                nc.tensor.matmul(ps[:, 6 + m % 2], w[0:R, hh, W_KR:W_KR + DC], qr_sb[:, m % 2],
                                 start=True, stop=True).then_inc(qc_done, 1)

            def body(i):
                first = isinstance(i, int)
                for hh, g, m in turn_steps:
                    n = STEPS * i + m
                    project_query(i, hh, g)
                    product_m(n, m, hh)
                    if g == NSG - 1:
                        output_weight(i, hh)
                    if m >= 2 or not first:
                        carry_query(n - 2, m - 2)
                    if m >= 1 or not first:
                        reduce_query(n - 1, m - 1, i)
            repeat(pe, TURNS, body)
            carry_query(LAST - 2, STEPS - 2)
            reduce_query(LAST - 1, STEPS - 1, TURNS - 1)
            carry_query(LAST - 1, STEPS - 1)

        @block.scalar
        def _(act):
            def store_qr(n, m):
                act.wait_ge(qr_done, n + 1)
                wait(act, qc_done, n - 1)
                nc.scalar.activation(qr_sb[:, m % 2], ps[0:R, 4 + m % 2], ACT.Copy).then_inc(qr_stored, 1)

            def store_qc(n, m):
                hh, g = (m % STEPS) // NSG, m % NSG
                act.wait_ge(qc_done, n + 1)
                out = staged[:, hh // 2, :, hh % 2, g * SG:(g + 1) * SG].rearrange("p b s -> p s b")
                nc.scalar.activation(out, ps[:, 6 + m % 2].rearrange("p (s b) -> p s b", s=SG), ACT.Copy).then_inc(qc_stored, 1)

            def round_weights(i, head, hh):
                act.wait_ge(w_loaded[hh], 16 * (i + 1))
                wait(act, m_done, NSG * (head - 1))
                nc.scalar.activation(w_parts[0][:, hh % 2], w[:, hh, 0:W_QR], ACT.Copy).then_inc(w_rounded, 1)

            def round_rotated(n, m):
                act.wait_ge(rot_summed, n + 1)
                wait(act, m_done, n - 1)
                nc.scalar.activation(rot_parts[0][:, m % 2], rot[:, m % 2], ACT.Copy).then_inc(rot_rounded, 1)

            round_weights(0, 0, 0)
            round_rotated(0, 0)

            def body(i, final=False):
                first = isinstance(i, int) and i == 0
                for hh, g, m in turn_steps:
                    n = STEPS * i + m
                    act.wait_ge(a_done, a_count(i, hh, g))
                    wait(act, qr_done, n - 1)
                    nc.scalar.activation(q_sb[:, m % 2], ps[:, (hh + g) % 2], ACT.Copy).then_inc(a_stored, 1)
                    if g == NSG - 1:
                        act.wait_ge(a_done, a_count(i, hh, NSG))
                        if hh >= 2 or not first:
                            act.wait_ge(w_vo_out[hh % 2], 16 * (2 * i + hh // 2))
                        nc.scalar.activation(w_vo[:, hh % 2], ps[:, (hh + NSG) % 2], ACT.Copy).then_inc(a_stored, 1)
                    if m >= 3 or not first:
                        if (m - 3) % (STEPS // 2) == 0 and not (first and m == 3):
                            wait(act, staged_out[(m - 3) // (STEPS // 2)], 16 * i)
                        store_qc(n - 3, m - 3)
                    if not (final and m == STEPS - 1):
                        round_rotated(n + 1, m + 1)
                    if g == 1 and not (final and hh == HG - 1):
                        round_weights(i + (hh + 1) // HG, HG * i + hh + 1, (hh + 1) % HG)
                    if m >= 1 or not first:
                        store_qr(n - 1, m - 1)
            repeat_to_last(act, TURNS, body)
            store_qr(LAST - 1, STEPS - 1)
            for lag in (3, 2, 1):
                store_qc(LAST - lag, STEPS - lag)


def cross_attention(nc, cache_t, rope_kv, x, q_dram, w_vo_dram, x1, stat, ident):
    with ExitStack() as ctx:
        sb = lambda n, s, dtype=F32: ctx.enter_context(nc.sbuf_tensor(n, s, dtype))
        pair = lambda n, s: [sb(f"{n}_{part}", s, F32R) for part in ("high", "low")]
        sem = lambda n: ctx.enter_context(nc.semaphore(n))
        CH = H // HG
        STEPS = BT * CH
        table = sb("c_table", [P, 2, L])
        raw = sb("c_raw", [P, BT, L])
        swapped = sb("c_swapped", [P, BT, L])
        part = sb("c_part", [P, 2, L])
        kv_t = sb("c_kv_t", [P, BT, L])
        kv = sb("c_kv", [P, BT, 2, P])
        kv_end = sb("c_kv_end", [1, BT, P])
        q = sb("c_q", [P, BT, H * S])
        peak = sb("c_peak", [P, 4])
        total = sb("c_total", [P, 4])
        inverse = sb("c_inverse", [P, 4])
        e = sb("c_e", [P, 4, L])
        e_t = sb("c_e_t", [P, 2, 2, H * S])
        e_t_end = sb("c_e_t_end", [1, 2, H * S])
        mixed = pair("c_mixed", [P, H, BT, S])
        w_vo = pair("c_w_vo", [P, H, D])
        w_vo_raw = sb("c_w_vo_raw", [P, 4, D])
        scratch = sb("c_scratch", [P, D])
        row_sum, neg_mean, squares = (sb(f"c_{n}", [P, 1]) for n in ("row_sum", "neg_mean", "squares"))
        sc_ps = ctx.enter_context(nc.psum_tensor("c_sc_ps", [P, 2, D], F32))
        et_ps = ctx.enter_context(nc.psum_tensor("c_et_ps", [P, 2, D], F32))
        mix_ps = ctx.enter_context(nc.psum_tensor("c_mix_ps", [P, 2, D], F32))
        out_ps = ctx.enter_context(nc.psum_tensor("c_out_ps", [P, D], F32))
        kv_ps = ctx.enter_context(nc.psum_tensor("c_kv_ps", [P, D], F32))
        table_loaded, x_loaded = sem("c_table_loaded"), sem("c_x_loaded")
        q_loaded = [sem(f"c_q_loaded{u}") for u in range(BT)]
        raw_loaded = [sem(f"c_raw_loaded{u}") for u in range(BT)]
        rotated_, kv_turned, kv_stored, pool_chained = sem("c_rotated"), sem("c_kv_turned"), sem("c_kv_stored"), sem("c_pool_chained")
        scored, peaked, exped, normed = sem("c_scored"), sem("c_peaked"), sem("c_exped"), sem("c_normed")
        turned, et_stored, mix_done, mix_stored = sem("c_turned"), sem("c_et_stored"), sem("c_mix_done"), sem("c_mix_stored")
        out_done, out_free, dve_chained = sem("c_out_done"), sem("c_out_free"), sem("c_dve_chained")
        w_vo_loaded, w_vo_rounded, w_vo_split, mix_rounded = (
            sem(f"c_{n}") for n in ("w_vo_loaded", "w_vo_rounded", "w_vo_split", "mix_rounded"))
        centred, squared, kept = sem("c_centred"), sem("c_squared"), sem("c_kept")
        CHUNKS = B * CH
        block = ctx.enter_context(nc.Block())
        q_in = q_dram.rearrange("b d h s -> b d (h s)")

        @block.sync
        def _(sp):
            sp.dma_start(table[:], rope_kv).then_inc(table_loaded, 16)

            def body(i):
                for u in range(BT):
                    b = BT * i + u
                    wait(sp, rotated_, b - BT + 1)
                    at = bass.ds(b, 1)
                    sp.dma_start(raw[:, u], cache_t[at].rearrange("b d l -> d (b l)")).then_inc(raw_loaded[u], 16)
                    half = DC // 2
                    for lo, hi in ((0, half), (half, 0)):
                        sp.dma_start(swapped[lo:lo + half, u], cache_t[at, hi:hi + half].rearrange("b d l -> d (b l)")).then_inc(raw_loaded[u], 16)
                    wait(sp, scored, CH * (b - BT + 1))
                    sp.dma_start(q[:, u], q_in[at].rearrange("b d x -> d (b x)")).then_inc(q_loaded[u], 16)
            body(0)
            for k in range(H // 4):
                wait(sp, w_vo_split, k)
                sp.dma_start(w_vo_raw[:], w_vo_dram[:, 4 * k:4 * k + 4]).then_inc(w_vo_loaded, 16)
            sp.dma_start(x1[:], x.rearrange("(t p) d -> p t d", p=P)).then_inc(x_loaded, 16)
            with sp.Fori(1, TILES) as i:
                body(i)

        @block.gpsimd
        def _(pool):
            pool.wait_ge(table_loaded, 16)

            def body(i):
                for u in range(BT):
                    b = BT * i + u
                    pool.wait_ge(raw_loaded[u], 48 * (i + 1))
                    nc.gpsimd.tensor_tensor(part[:, 0], raw[:, u], table[:, 0], ALU.mult).then_inc(pool_chained, 1)
                    nc.gpsimd.tensor_tensor(part[:, 1], swapped[:, u], table[:, 1], ALU.mult).then_inc(pool_chained, 1)
                    pool.wait_ge(pool_chained, 2 * b + 2)
                    wait(pool, scored, CH * (b - BT + 1))
                    wait(pool, kv_turned, b - BT + 1)
                    nc.gpsimd.tensor_tensor(kv_t[:, u], part[:, 0], part[:, 1], ALU.add).then_inc(rotated_, 1)
                    pool.wait_ge(rotated_, b + 1)
            repeat(pool, TILES, body)

        @block.vector
        def _(dve):
            def find_peak(n, j):
                dve.wait_ge(scored, n + 1)
                wait(dve, exped, n - 3)
                nc.vector.tensor_reduce(peak[:, j % 4:j % 4 + 1], sc_ps[:, j % 2, 0:L], AX_X, ALU.max,
                                        negate=True).then_inc(peaked, 1)

            def normalise(n, j):
                k = j % 4
                dve.wait_ge(exped, n + 1)
                nc.vector.reciprocal(inverse[:, k:k + 1], total[:, k:k + 1]).then_inc(dve_chained, 1)
                dve.wait_ge(dve_chained, n + 1)
                nc.vector.tensor_scalar(e[:, k], e[:, k], inverse[:, k:k + 1], None, ALU.mult).then_inc(normed, 1)

            def store_mixed(t, u):
                dve.wait_ge(mix_rounded, BT * t + u + 1)
                low_part(nc, mixed[1][:, :, u], mix_ps[:, u % 2].rearrange("p (h s) -> p h s", h=H), mixed[0][:, :, u]).then_inc(mix_stored, 1)

            def add_out(t):
                if isinstance(t, int):
                    dve.wait_ge(x_loaded, 16)
                dve.wait_ge(out_done, t + 1)
                row = x1[:, bass.ds(t, 1)].rearrange("p t d -> p (t d)")
                nc.vector.scalar_tensor_tensor(row, out_ps[:], 1.0, row, ALU.mult, ALU.add, accum_out=row_sum[:]).then_inc(out_free, 1)
                dve.wait_ge(out_free, t + 2)
                nc.vector.tensor_scalar(neg_mean[:], row_sum[:], -1.0 / D, None, ALU.mult).then_inc(centred, 1)

            def keep_moments(t):
                dve.wait_ge(squared, t + 1)
                nc.vector.tensor_copy(stat[:, 0, bass.ds(t, 1)], neg_mean[:])
                nc.vector.tensor_copy(stat[:, 1, bass.ds(t, 1)], squares[:]).then_inc(kept, 1)

            def body(i):
                first = isinstance(i, int)
                for j in range(STEPS):
                    n = STEPS * i + j
                    find_peak(n, j)
                    if j or not first:
                        normalise(n - 1, j - 1)
                    if j in stores:
                        back, u = stores[j]
                        if not (first and back):
                            store_mixed(i - back, u)
                    if j == 13 and not first:
                        add_out(i - 1)
                    if j == 15 and not first:
                        keep_moments(i - 1)
                    if first and j % CH == 3:
                        k = j // CH
                        dve.wait_ge(w_vo_rounded, k + 1)
                        low_part(nc, w_vo[1][:, 4 * k:4 * k + 4], w_vo_raw[:], w_vo[0][:, 4 * k:4 * k + 4]).then_inc(w_vo_split, 1)
            stores = {14: (0, 0), 15: (0, 1), 2: (1, 2), 5: (1, 3)}
            dve.sem_inc(out_free, 1)
            dve.sem_inc(kept, 1)
            repeat(dve, TILES, body)
            normalise(CHUNKS - 1, STEPS - 1)
            store_mixed(TILES - 1, BT - 2)
            store_mixed(TILES - 1, BT - 1)
            add_out(TILES - 1)
            keep_moments(TILES - 1)

        @block.scalar
        def _(act):
            def exponential(n, j):
                k = j % 4
                act.wait_ge(peaked, n + 1)
                wait(act, turned, n - 3)
                nc.scalar.activation(e[:, k], sc_ps[:, j % 2, 0:L], ACT.Exp, bias=peak[:, k:k + 1],
                                     accum_out=total[:, k:k + 1]).then_inc(exped, 1)

            def store_turned(n, b, j):
                u, c = (j // CH) % 2, j % CH
                act.wait_ge(turned, n + 1)
                if c == 0:
                    wait(act, mix_done, b - 1)
                nc.scalar.activation(e_t[:, u, :, c * P:(c + 1) * P], et_ps[:, j % 2, 0:2 * P].rearrange("p (k x) -> p k x", k=2), ACT.Copy)
                nc.scalar.activation(e_t_end[:, u, c * P:(c + 1) * P], et_ps[0:1, j % 2, 2 * P:3 * P], ACT.Copy).then_inc(et_stored, 1)

            def square_row(t):
                act.wait_ge(centred, t + 1)
                act.wait_ge(kept, t + 1)
                row = x1[:, bass.ds(t, 1)].rearrange("p t d -> p (t d)")
                nc.scalar.activation(scratch[:], row, ACT.Square, bias=neg_mean[:], accum_out=squares[:]).then_inc(squared, 1)

            def store_kv(b, u):
                act.wait_ge(kv_turned, b + 1)
                wait(act, mix_done, b - BT + 1)
                nc.scalar.activation(kv[:, u], kv_ps[:, 0:2 * P].rearrange("p (k x) -> p k x", k=2), ACT.Copy)
                nc.scalar.activation(kv_end[:, u], kv_ps[0:1, 2 * P:3 * P], ACT.Copy).then_inc(kv_stored, 1)

            def round_mixed(t, u):
                act.wait_ge(mix_done, BT * t + u + 1)
                if u == 0:
                    wait(act, out_done, t)
                nc.scalar.activation(mixed[0][:, :, u], mix_ps[:, u % 2].rearrange("p (h s) -> p h s", h=H), ACT.Copy).then_inc(mix_rounded, 1)

            def body(i):
                first = isinstance(i, int)
                for j in range(STEPS):
                    n, u = STEPS * i + j, j // CH
                    exponential(n, j)
                    if j >= 2 or not first:
                        store_turned(n - 2, BT * i + (j - 2) // CH, (j - 2) % STEPS)
                    if j % CH == 1:
                        store_kv(BT * i + u, u)
                    if j in rounds:
                        back, u = rounds[j]
                        if not (first and back):
                            round_mixed(i - back, u)
                    if j == 14 and not first:
                        square_row(i - 1)
                    if first and j % CH == 3:
                        k = j // CH
                        act.wait_ge(w_vo_loaded, 16 * (k + 1))
                        nc.scalar.activation(w_vo[0][:, 4 * k:4 * k + 4], w_vo_raw[:], ACT.Copy).then_inc(w_vo_rounded, 1)
            rounds = {12: (0, 0), 13: (0, 1), 0: (1, 2), 4: (1, 3)}
            repeat(act, TILES, body)
            store_turned(CHUNKS - 2, B - 1, STEPS - 2)
            store_turned(CHUNKS - 1, B - 1, STEPS - 1)
            round_mixed(TILES - 1, BT - 2)
            round_mixed(TILES - 1, BT - 1)
            square_row(TILES - 1)

        @block.tensor
        def _(pe):
            def score(n, b, t, j):
                u, c = j // CH, j % CH
                if c == 0:
                    pe.wait_ge(q_loaded[u], 16 * (t + 1))
                    pe.wait_ge(rotated_, b + 1)
                wait(pe, exped, n - 1)
                nc.tensor.matmul(sc_ps[:, j % 2, 0:L], q[:, u, c * P:(c + 1) * P], kv_t[:, u],
                                 start=True, stop=True).then_inc(scored, 1)

            def turn_kv(b, u):
                pe.wait_ge(rotated_, b + 1)
                wait(pe, kv_stored, b)
                for k in range(2):
                    nc.tensor.transpose(kv_ps[:, k * P:(k + 1) * P], kv_t[:, u, k * P:(k + 1) * P], ident[:])
                nc.tensor.transpose(kv_ps[0:1, 2 * P:3 * P], kv_t[:, u, 2 * P:L], ident[:]).then_inc(kv_turned, 1)

            def turn_weights(n, j):
                pe.wait_ge(normed, n + 1)
                wait(pe, et_stored, n - 1)
                for k in range(2):
                    nc.tensor.transpose(et_ps[:, j % 2, k * P:(k + 1) * P], e[:, j % 4, k * P:(k + 1) * P], ident[:])
                nc.tensor.transpose(et_ps[0:1, j % 2, 2 * P:3 * P], e[:, j % 4, 2 * P:L], ident[:]).then_inc(turned, 1)

            def mix(b, u):
                pe.wait_ge(et_stored, CH * (b + 1))
                pe.wait_ge(kv_stored, b + 1)
                wait(pe, mix_stored, b - 1)
                out = mix_ps[:, u % 2]
                for k in range(2):
                    nc.tensor.matmul(out, kv[:, u, k], e_t[:, u % 2, k], start=k == 0, stop=False)
                nc.tensor.matmul(out, kv_end[:, u], e_t_end[:, u % 2], start=False, stop=True).then_inc(mix_done, 1)

            def project(t, heads):
                if heads[0] == 0:
                    pe.wait_ge(w_vo_split, H // 4)
                    pe.wait_ge(mix_stored, BT * (t + 1))
                    pe.wait_ge(out_free, t + 1)
                for h in heads:
                    last = multiply_parts(nc, out_ps[:], [a[:, h].rearrange("p b s -> p (b s)") for a in mixed],
                                          [w[:, h] for w in w_vo], h == 0, h == H - 1)
                if heads[-1] == H - 1:
                    last.then_inc(out_done, 1)

            shares = {5: range(0, 3), 7: range(3, 6), 8: range(6, 9), 9: range(9, 12), 11: range(12, H)}

            def body(i, first=False, final=False):
                for j in range(STEPS):
                    n, u = STEPS * i + j, j // CH
                    if not (final and j >= STEPS - 2):
                        ahead = (j + 2) % STEPS
                        t = i + (j + 2) // STEPS
                        score(n + 2, BT * t + ahead // CH, t, ahead)
                    if j % CH == 0:
                        turn_kv(BT * i + u, u)
                    if j in shares and not first:
                        project(i - 1, shares[j])
                    if j % CH == 2 and (j > CH or not first):
                        mix(BT * i + u - 1, (u - 1) % BT)
                    if j or not first:
                        turn_weights(n - 1, (j - 1) % STEPS)
            score(0, 0, 0, 0)
            score(1, 0, 0, 1)
            body(0, first=True)
            with pe.Fori(1, TILES - 1) as i:
                body(i)
            body(TILES - 1, final=True)
            turn_weights(CHUNKS - 1, STEPS - 1)
            mix(B - 1, BT - 1)
            project(TILES - 1, range(H))


def root_deviations(nc, stat, eps, name):
    with nc.semaphore(f"{name}_rooted") as rooted, nc.semaphore(f"{name}_inverted") as inverted, nc.Block() as block:
        @block.scalar
        def _(act):
            nc.scalar.activation(stat[:, 1], stat[:, 1], ACT.Sqrt, bias=eps[:], scale=1.0 / D).then_inc(rooted, 1)

        @block.vector
        def _(dve):
            dve.wait_ge(rooted, 1)
            nc.vector.reciprocal(stat[:, 1], stat[:, 1]).then_inc(inverted, 1)
            dve.wait_ge(inverted, 1)


MAGIC = 1.5 * 2.0 ** 23
TURN_HI = 6.28125
TURN_LO = 2 * PI - TURN_HI


def head_of(hh):
    chunk, k = divmod(hh, HG)
    return 8 * (chunk // 2) + 2 * k + chunk % 2


def holo_weights(nc, amp_nat, phase_nat, basis_t, basis_o, amp_o, phase_o, half_pi, basis, score_w, value_w, out_w):
    with ExitStack() as ctx:
        sb = lambda n, s: ctx.enter_context(nc.sbuf_tensor(n, s, F32))
        sem = lambda n: ctx.enter_context(nc.semaphore(n))
        NAT, OUT = CD * 3 * HARM, D
        amp = sb("h_amp", [P, NAT + OUT])
        phase = sb("h_phase", [P, NAT + OUT])
        turns = sb("h_turns", [P, NAT + OUT])
        bo = sb("h_bo", [P, CD, HARM])
        ps = ctx.enter_context(nc.psum_tensor("h_ps", [P, 8, 512], F32))
        loaded, cleared, stepped, cosined, weighed, multiplied, kept = (
            sem(f"h_{n}") for n in ("loaded", "cleared", "stepped", "cosined", "weighed", "multiplied", "kept"))
        block = ctx.enter_context(nc.Block())

        @block.sync
        def _(sp):
            sp.dma_start(phase[:, 0:NAT], phase_nat.rearrange("p t i -> p (t i)")).then_inc(loaded, 16)
            sp.wait_ge(cleared, 1)
            sp.dma_start(phase[0:HARM, NAT:], phase_o).then_inc(loaded, 16)
            sp.dma_start(amp[:, 0:NAT], amp_nat.rearrange("p t i -> p (t i)")).then_inc(loaded, 16)
            sp.wait_ge(cleared, 2)
            sp.dma_start(amp[0:HARM, NAT:], amp_o).then_inc(loaded, 16)
            sp.dma_start(bo[:], basis_o).then_inc(loaded, 16)
            sp.dma_start(basis[:], basis_t).then_inc(loaded, 16)
            sp.wait_ge(loaded, 96)

        @block.vector
        def _(dve):
            nc.vector.memset(phase[:, NAT:], 0.0).then_inc(cleared, 1)
            nc.vector.memset(amp[:, NAT:], 0.0).then_inc(cleared, 1)
            dve.wait_ge(loaded, 96)
            dve.wait_ge(cleared, 2)
            steps = (
                lambda: nc.vector.tensor_scalar(turns[:], phase[:], 1.0 / (2 * PI), MAGIC, ALU.mult, ALU.add),
                lambda: nc.vector.tensor_scalar(turns[:], turns[:], MAGIC, None, ALU.subtract),
                lambda: nc.vector.scalar_tensor_tensor(phase[:], turns[:], -TURN_HI, phase[:], ALU.mult, ALU.add),
                lambda: nc.vector.scalar_tensor_tensor(phase[:], turns[:], -TURN_LO, phase[:], ALU.mult, ALU.add),
            )
            for n, step in enumerate(steps):
                step().then_inc(stepped, 1)
                dve.wait_ge(stepped, n + 1)
            dve.wait_ge(cosined, 2)
            nc.vector.tensor_tensor(amp[:], amp[:], phase[:], ALU.mult).then_inc(weighed, 1)
            dve.wait_ge(weighed, 1)
            nc.vector.tensor_copy(out_w[:], amp[0:HARM, NAT:])
            dve.wait_ge(multiplied, 1)
            nc.vector.tensor_scalar(score_w[:].rearrange("p (t r) j -> p r t j", r=4),
                                    ps[0:HARM, 0:4, 0:4 * HARM].rearrange("p r (t j) -> p r t j", t=4),
                                    float(np.float32(1.0) / np.sqrt(np.float32(HD))), None, ALU.mult).then_inc(kept, 1)
            dve.wait_ge(kept, 1)

        @block.scalar
        def _(act):
            act.wait_ge(stepped, 4)
            nc.scalar.activation(phase[:], phase[:], ACT.Abs).then_inc(cosined, 1)
            act.wait_ge(cosined, 1)
            nc.scalar.activation(phase[:], phase[:], ACT.Sin, bias=half_pi[:], scale=-1.0).then_inc(cosined, 1)
            act.wait_ge(multiplied, 2)
            places = value_w[HARM:2 * HARM].rearrange("p (c cp k kp) j -> p c cp k kp j", c=2, cp=2, k=2)
            for r in range(4):
                for c in range(2):
                    nc.scalar.activation(places[:, c, r % 2, :, r // 2],
                                         ps[HARM:2 * HARM, 4 + r, c * 2 * HARM:(c + 1) * 2 * HARM].rearrange("p (k j) -> p k j", k=2), ACT.Copy)

        @block.tensor
        def _(pe):
            pe.wait_ge(weighed, 1)
            weights = amp[:, 0:NAT].rearrange("p (t w i) -> p t w i", t=CD, w=3)

            def rows(h):
                return slice(h % 4 * HD, h % 4 * HD + HD), h // 4

            for h in range(16):
                at, t = rows(h)
                last = nc.tensor.matmul(ps[0:HARM, h % 4, t * HARM:(t + 1) * HARM], weights[at, t, 0], weights[at, t, 1],
                                        start=True, stop=True)
            last.then_inc(multiplied, 1)
            for hh in range(16):
                h, c, k = head_of(hh), hh // 8, hh % 4 // 2
                at, t = rows(h)
                last = nc.tensor.matmul(ps[HARM:2 * HARM, 4 + h % 4, (2 * c + k) * HARM:(2 * c + k + 1) * HARM], weights[at, t, 2], bo[at, t],
                                        start=True, stop=True)
            last.then_inc(multiplied, 1)


def self_attention(nc, x1, stat, basis, score_w, value_w, out_w, ident):
    with ExitStack() as ctx:
        sb = lambda n, s: ctx.enter_context(nc.sbuf_tensor(n, s, F32))
        sem = lambda n: ctx.enter_context(nc.semaphore(n))
        HH = 16
        xn = sb("d_xn", [P, 2, D])
        xn_t = sb("d_xn_t", [P, CD, P])
        reduced = sb("d_reduced", [P, 2, 2, P])
        u_sb = sb("d_u", [P, 2, BT, HG, S])
        shifted = sb("d_shifted", [P, 2, HH, S])
        e = sb("d_e", [P, 2, HH, S])
        peak, total, inverse = (sb(f"d_{n}", [P, 2, HH]) for n in ("peak", "total", "inverse"))
        e_t = sb("d_e_t", [P, HH, P])
        z_sb = sb("d_z", [P, HH, HARM])
        ro_sb = sb("d_ro", [HARM, P])
        scratch = sb("d_scratch", [P, D])
        row_sum, neg_mean, squares = (sb(f"d_{n}", [P, 1]) for n in ("row_sum", "neg_mean", "squares"))
        ps = ctx.enter_context(nc.psum_tensor("d_ps", [P, 8, D], F32))
        T_BANK, R_BANK, U_BANK, S_BANK, P_BANK, Z_BANK = 0, 1, 2, 4, 5, 6
        fetched, normed, turned, turned_out = sem("d_fetched"), sem("d_normed"), sem("d_turned"), sem("d_turned_out")
        reduced_done, reduced_out = sem("d_reduced_done"), sem("d_reduced_out")
        u_done, u_out_a, u_out_d = sem("d_u_done"), sem("d_u_out_a"), sem("d_u_out_d")
        scored, peaked, shifted_out, exped, summed, inverted, weighed = (
            sem(f"d_{n}") for n in ("scored", "peaked", "shifted_out", "exped", "summed", "inverted", "weighed"))
        e_turned, e_out_a, e_out_d = sem("d_e_turned"), sem("d_e_out_a"), sem("d_e_out_d")
        z_done, z_out_a, z_out_d = sem("d_z_done"), sem("d_z_out_a"), sem("d_z_out_d")
        ro_done, ro_out, out_done, added = sem("d_ro_done"), sem("d_ro_out"), sem("d_out_done"), sem("d_added")
        centred, squared, kept, cleared = sem("d_centred"), sem("d_squared"), sem("d_kept"), sem("d_cleared")
        half_scored = sem("d_half_scored")
        TURNS = TILES // 2
        block = ctx.enter_context(nc.Block())

        def row_of(t):
            return x1[:, bass.ds(t, 1)].rearrange("p t d -> p (t d)")

        def copy_blocks(engine, batches):
            for b in batches:
                at = slice(b * S, (b + 1) * S)
                out, in_ = e_t[at, :, at], ps[at, P_BANK].rearrange("p (h s) -> p h s", h=HH)
                last = nc.vector.tensor_copy(out, in_) if engine == "dve" else nc.scalar.activation(out, in_, ACT.Copy)
            return last

        @block.gpsimd
        def _(pool):
            nc.gpsimd.memset(e_t[:], 0.0).then_inc(cleared, 1)

            def body(i):
                for v in range(2):
                    t = 2 * i + v
                    wait(pool, turned, t - 1)
                    nc.gpsimd.tensor_tensor(xn[:, v], row_of(t), stat[:, 0, bass.ds(t, 1)].to_broadcast([P, D]), ALU.add).then_inc(fetched, 1)
                    pool.wait_ge(fetched, t + 1)
                    nc.gpsimd.tensor_tensor(xn[:, v], xn[:, v], stat[:, 1, bass.ds(t, 1)].to_broadcast([P, D]), ALU.mult).then_inc(normed, 1)
            repeat(pool, TURNS, body)

        @block.tensor
        def _(pe):
            def turn_input(t, v):
                pe.wait_ge(normed, t + 1)
                wait(pe, turned_out, t)
                for c in range(CD):
                    last = nc.tensor.transpose(ps[:, T_BANK, c * P:(c + 1) * P], xn[:, v, c * P:(c + 1) * P], ident[:])
                last.then_inc(turned, 1)

            def reduce_input(t, v):
                pe.wait_ge(turned_out, t + 1)
                wait(pe, reduced_out, t)
                wait(pe, ro_out, t - 1)
                for m in range(2):
                    for c in range(CD):
                        last = nc.tensor.matmul(ps[:, R_BANK, m * P:(m + 1) * P], basis[:, c, m * P:(m + 1) * P], xn_t[:, c],
                                                start=c == 0, stop=c == CD - 1)
                last.then_inc(reduced_done, 1)

            def score_weights(t, v):
                pe.wait_ge(reduced_out, t + 1)
                wait(pe, u_out_a, t)
                wait(pe, u_out_d, t)
                for g in range(2):
                    for k in range(HG):
                        h = 8 * g + 2 * k
                        last = nc.tensor.matmul(ps[:, U_BANK + g, k * P:(k + 1) * P], score_w[:, h:h + 2].rearrange("p h j -> p (h j)"),
                                                reduced[0:HARM, v, 0], start=True, stop=True)
                last.then_inc(u_done, 1)

            def score(t, v):
                pe.wait_ge(u_out_a, t + 1)
                pe.wait_ge(u_out_d, t + 1)
                wait(pe, shifted_out, t)
                for parity in range(2):
                    if parity:
                        pe.wait_ge(half_scored, t + 1)
                    at = slice(parity * HARM, (parity + 1) * HARM)
                    for g in range(2):
                        for b in range(BT):
                            first = (2 * g + parity) * P + b * S
                            last = nc.tensor.matmul(ps[:, S_BANK, first:first + S], u_sb[at, g, b].rearrange("p k s -> p (k s)"),
                                                    reduced[at, v, 1, b * S:(b + 1) * S], start=True, stop=True)
                    last.then_inc(scored if parity else half_scored, 1)

            def value_weights(t, v):
                wait(pe, z_out_a, t)
                wait(pe, z_out_d, t)
                for g in range(2):
                    last = nc.tensor.matmul(ps[:, Z_BANK + g], reduced[HARM:2 * HARM, v, 0],
                                            value_w[HARM:2 * HARM, 8 * g:8 * g + 8].rearrange("p h j -> p (h j)"), start=True, stop=True)
                last.then_inc(z_done, 1)

            def turn_weights(t, v):
                pe.wait_ge(weighed, t + 1)
                wait(pe, added, t)
                for c in range(HG):
                    last = nc.tensor.transpose(ps[:, P_BANK, c * P:(c + 1) * P],
                                               e[:, v, 4 * c:4 * c + 4].rearrange("p b s -> p (b s)"), ident[:])
                last.then_inc(e_turned, 1)

            def mix(t):
                for done in (e_out_a, e_out_d, z_out_a, z_out_d):
                    pe.wait_ge(done, t + 1)
                for h in range(HH):
                    last = nc.tensor.matmul(ps[0:HARM, R_BANK, 2 * P:3 * P], z_sb[:, h], e_t[:, h], start=h == 0, stop=h == HH - 1)
                last.then_inc(ro_done, 1)

            def project(t):
                pe.wait_ge(ro_out, t + 1)
                nc.tensor.matmul(ps[:, P_BANK], ro_sb[:], out_w[:], start=True, stop=True).then_inc(out_done, 1)

            def step(t, v, first=False, last=False):
                if not last:
                    turn_input(t, v)
                if not first:
                    value_weights(t - 1, 1 - v)
                if not last:
                    reduce_input(t, v)
                if not first:
                    turn_weights(t - 1, 1 - v)
                if not last:
                    score_weights(t, v)
                if not first:
                    mix(t - 1)
                if not last:
                    score(t, v)
                if not first:
                    project(t - 1)

            step(0, 0, first=True)
            step(1, 1)
            with pe.Fori(1, TURNS) as i:
                step(2 * i, 0)
                step(2 * i + 1, 1)
            step(TILES, 0, last=True)

        @block.vector
        def _(dve):
            def shift(t, v):
                scores = ps[:, S_BANK].rearrange("p (h s) -> p h s", h=HH)
                dve.wait_ge(scored, t + 1)
                nc.vector.tensor_reduce(peak[:, v], scores, AX_X, ALU.max).then_inc(peaked, 1)
                dve.wait_ge(peaked, t + 1)
                nc.vector.tensor_tensor(shifted[:, v], scores, peak[:, v].unsqueeze(2).to_broadcast([P, HH, S]),
                                        ALU.subtract).then_inc(shifted_out, 1)

            def weigh(t, v):
                dve.wait_ge(exped, t + 1)
                nc.vector.tensor_reduce(total[:, v], e[:, v], AX_X, ALU.add).then_inc(summed, 1)
                dve.wait_ge(summed, t + 1)
                nc.vector.reciprocal(inverse[:, v], total[:, v]).then_inc(inverted, 1)
                dve.wait_ge(inverted, t + 1)
                nc.vector.tensor_tensor(e[:, v], e[:, v], inverse[:, v].unsqueeze(2).to_broadcast([P, HH, S]), ALU.mult).then_inc(weighed, 1)

            def step(t, v, first=False, last=False):
                if not first:
                    shift(t - 1, 1 - v)
                    dve.wait_ge(z_done, t)
                    wait(dve, ro_done, t - 1)
                    nc.vector.tensor_copy(z_sb[:, 0:8].rearrange("p h j -> p (h j)"), ps[:, Z_BANK]).then_inc(z_out_d, 1)
                    weigh(t - 1, 1 - v)
                    dve.wait_ge(e_turned, t)
                    copy_blocks("dve", (0, 1)).then_inc(e_out_d, 1)
                if not last:
                    dve.wait_ge(u_done, t + 1)
                    wait(dve, scored, t)
                    nc.vector.tensor_copy(u_sb[:, 1], ps[:, U_BANK + 1].rearrange("p (k b s) -> p b k s", k=HG, b=BT)).then_inc(u_out_d, 1)
                if not first:
                    dve.wait_ge(out_done, t)
                    nc.vector.scalar_tensor_tensor(row_of(t - 1), ps[:, P_BANK], 1.0, row_of(t - 1), ALU.mult, ALU.add,
                                                   accum_out=row_sum[:]).then_inc(added, 1)
                    dve.wait_ge(added, t)
                    nc.vector.tensor_scalar(neg_mean[:], row_sum[:], -1.0 / D, None, ALU.mult).then_inc(centred, 1)
                    dve.wait_ge(squared, t)
                    nc.vector.tensor_copy(stat[:, 0, bass.ds(t - 1, 1)], neg_mean[:])
                    nc.vector.tensor_copy(stat[:, 1, bass.ds(t - 1, 1)], squares[:]).then_inc(kept, 1)

            dve.wait_ge(cleared, 1)
            step(0, 0, first=True)
            step(1, 1)
            with dve.Fori(1, TURNS) as i:
                step(2 * i, 0)
                step(2 * i + 1, 1)
            step(TILES, 0, last=True)

        @block.scalar
        def _(act):
            def step(t, v, first=False, last=False):
                if not last:
                    act.wait_ge(turned, t + 1)
                    wait(act, reduced_done, t)
                    nc.scalar.activation(xn_t[:], ps[:, T_BANK].rearrange("p (c x) -> p c x", c=CD), ACT.Copy).then_inc(turned_out, 1)
                if not first:
                    act.wait_ge(shifted_out, t)
                    nc.scalar.activation(e[:, 1 - v], shifted[:, 1 - v], ACT.Exp).then_inc(exped, 1)
                    act.wait_ge(z_done, t)
                    wait(act, ro_done, t - 1)
                    nc.scalar.activation(z_sb[:, 8:16].rearrange("p h j -> p (h j)"), ps[:, Z_BANK + 1], ACT.Copy).then_inc(z_out_a, 1)
                if not last:
                    act.wait_ge(reduced_done, t + 1)
                    wait(act, scored, t - 1)
                    wait(act, z_done, t - 1)
                    nc.scalar.activation(reduced[:, v], ps[:, R_BANK, 0:2 * P].rearrange("p (m x) -> p m x", m=2), ACT.Copy).then_inc(reduced_out, 1)
                if not first:
                    act.wait_ge(e_turned, t)
                    copy_blocks("act", (2, 3)).then_inc(e_out_a, 1)
                if not last:
                    act.wait_ge(u_done, t + 1)
                    wait(act, scored, t)
                    nc.scalar.activation(u_sb[:, 0], ps[:, U_BANK].rearrange("p (k b s) -> p b k s", k=HG, b=BT), ACT.Copy).then_inc(u_out_a, 1)
                if not first:
                    act.wait_ge(ro_done, t)
                    wait(act, out_done, t - 1)
                    nc.scalar.activation(ro_sb[:], ps[0:HARM, R_BANK, 2 * P:3 * P], ACT.Copy).then_inc(ro_out, 1)
                    act.wait_ge(centred, t)
                    wait(act, kept, t - 1)
                    nc.scalar.activation(scratch[:], row_of(t - 1), ACT.Square, bias=neg_mean[:], accum_out=squares[:]).then_inc(squared, 1)

            act.wait_ge(cleared, 1)
            step(0, 0, first=True)
            step(1, 1)
            with act.Fori(1, TURNS) as i:
                step(2 * i, 0)
                step(2 * i + 1, 1)
            step(TILES, 0, last=True)


def fold_weights(nc, ent_in, ent_out, path, columns, rows, half_pi, ident, folded, bias, out_norm):
    LAYERS, PW, QUARTERS = 2, 2, 4
    PB, PH = LAYERS, LAYERS + LAYERS * PW
    with ExitStack() as ctx:
        sb = lambda n, s: ctx.enter_context(nc.sbuf_tensor(n, s, F32))
        sem = lambda n: ctx.enter_context(nc.semaphore(n))
        NR = LAYERS + 2 * LAYERS * PW + 2
        left = sb("f_left", [P, CF // 2, D])
        right = sb("f_right", [P, CF // 2, D])
        raw = sb("f_raw", [P, CD, D])
        turns = raw[:, 0:LAYERS * PW]
        paths = sb("f_paths", [P, PW, CD, D])
        col = sb("f_col", [P, 8 * CD + LAYERS * CF])
        row = sb("f_row", [P, NR, D])
        acc = sb("f_acc", [P, D])
        ones = sb("f_ones", [P, P])
        ps = ctx.enter_context(nc.psum_tensor("f_ps", [P, CD, D], F32))
        bias_ps = ctx.enter_context(nc.psum_tensor("f_bias_ps", [P, D], F32))
        small_loaded, quarter_loaded, paths_loaded = sem("f_small_loaded"), [sem(f"f_quarter_loaded{q}") for q in range(2)], sem("f_paths_loaded")
        chained, cosined, multiplied, quarter_used, copied, pool_chained = (
            sem(f"f_{n}") for n in ("chained", "cosined", "multiplied", "quarter_used", "copied", "pool_chained"))
        accumulated, spread, modulated, gained, rounded, split = (
            sem(f"f_{n}") for n in ("accumulated", "spread", "modulated", "gained", "rounded", "split"))
        block = ctx.enter_context(nc.Block())
        KQ = CF // QUARTERS
        GAIN, OFFSET, ENT_B = 0, 4 * CD, 8 * CD
        MODS = slice(PH, PH + LAYERS * PW)

        @block.sync
        def _(sp):
            for l in range(LAYERS):
                for q in range(QUARTERS):
                    at = slice(q * KQ, (q + 1) * KQ)
                    slot = slice(q % 2 * KQ, (q % 2 + 1) * KQ)
                    turn = QUARTERS * l + q
                    if turn >= 2:
                        sp.wait_ge(quarter_used, turn - 1)
                        sp.wait_ge(accumulated, (turn - 1) * KQ)
                    sp.dma_start(left[:, slot], ent_in[l, :, at]).then_inc(quarter_loaded[q % 2], 16)
                    sp.dma_start(right[:, slot], ent_out[l, :, at]).then_inc(quarter_loaded[q % 2], 16)
                    if l == 0 and q == 0:
                        sp.dma_start(col[:], columns).then_inc(small_loaded, 16)
                        sp.dma_start(row[:].rearrange("p r d -> p (r d)"), rows.rearrange("(o r) d -> o (r d)", o=1).to_broadcast([P, NR * D])).then_inc(small_loaded, 16)
                if l:
                    sp.wait_ge(pool_chained, 1 + 3 * l)
                sp.dma_start(paths[:], path[l]).then_inc(paths_loaded, 16)
            sp.wait_ge(paths_loaded, 16 * LAYERS)

        @block.gpsimd
        def _(pool):
            nc.gpsimd.memset(ones[:], 1.0).then_inc(pool_chained, 1)
            pool.wait_ge(modulated, 1)
            for l in range(LAYERS):
                pool.wait_ge(paths_loaded, 16 * (l + 1))
                for p in range(PW):
                    mod = row[:, PH + l * PW + p].unsqueeze(1).to_broadcast([P, CD, D])
                    nc.gpsimd.tensor_tensor(paths[:, p], paths[:, p], mod, ALU.mult).then_inc(pool_chained, 1)
                pool.wait_ge(pool_chained, 1 + 3 * l + 2)
                pool.wait_ge(split, CD * (2 * l + 1))
                nc.gpsimd.tensor_tensor(raw[:], paths[:, 0], paths[:, 1], ALU.add).then_inc(pool_chained, 1)

        @block.tensor
        def _(pe):
            pe.wait_ge(pool_chained, 1)
            for l in range(LAYERS):
                for q in range(QUARTERS):
                    pe.wait_ge(quarter_loaded[q % 2], 32 * (2 * l + q // 2 + 1))
                    for k in range(q * KQ, (q + 1) * KQ):
                        slot = k % (2 * KQ)
                        for m in range(CD):
                            if l and k == 0:
                                pe.wait_ge(copied, CD * l)
                            last = nc.tensor.matmul(ps[:, m], left[:, slot, m * P:(m + 1) * P], right[:, slot], start=k == 0, stop=k == CF - 1)
                    last.then_inc(quarter_used, 1)
                for part in range(2):
                    pe.wait_ge(gained, CD * (2 * l + part + 1))
                    nc.tensor.matmul(bias_ps[:], ones[:], acc[:], start=True, stop=True).then_inc(spread, 1)

        @block.scalar
        def _(act):
            act.wait_ge(chained, 5)
            nc.scalar.activation(turns, row[:, MODS], ACT.Abs).then_inc(cosined, 1)
            act.wait_ge(cosined, 1)
            nc.scalar.activation(row[:, MODS], turns, ACT.Sin, bias=half_pi[:], scale=-1.0).then_inc(cosined, 1)
            act.wait_ge(cosined, 2)
            for j in range(2 * LAYERS):
                if j % 2 == 0:
                    act.wait_ge(quarter_used, QUARTERS * (j // 2 + 1))
                    if j:
                        act.wait_ge(split, CD * j)
                    for m in range(CD):
                        nc.scalar.activation(raw[:, m], ps[:, m], ACT.Copy).then_inc(copied, 1)
                for m in range(CD):
                    act.wait_ge(gained, CD * j + m + 1)
                    nc.scalar.activation(folded[0][:, j, m], raw[:, m], ACT.Copy).then_inc(rounded, 1)

        @block.vector
        def _(dve):
            count = [0]

            def link(instruction):
                count[0] += 1
                instruction.then_inc(chained, 1)
                dve.wait_ge(chained, count[0])

            dve.wait_ge(small_loaded, 32)
            phases = row[:, MODS]
            link(nc.vector.tensor_scalar(phases, phases, PI / 4, None, ALU.subtract))
            link(nc.vector.tensor_scalar(turns, phases, 1.0 / (2 * PI), MAGIC, ALU.mult, ALU.add))
            link(nc.vector.tensor_scalar(turns, turns, MAGIC, None, ALU.subtract))
            flat = lambda a: a.rearrange("p r d -> p (r d)")
            link(nc.vector.scalar_tensor_tensor(flat(phases), flat(turns), -TURN_HI, flat(phases), ALU.mult, ALU.add))
            link(nc.vector.scalar_tensor_tensor(flat(phases), flat(turns), -TURN_LO, flat(phases), ALU.mult, ALU.add))
            dve.wait_ge(cosined, 2)
            nc.vector.tensor_scalar(phases, phases, float(np.sqrt(2.0)), None, ALU.mult).then_inc(modulated, 1)
            dve.wait_ge(modulated, 1)
            nc.vector.tensor_copy(out_norm[:], row[:, NR - 2:NR])
            dve.wait_ge(pool_chained, 1)
            for l in range(LAYERS):
                for part in range(2):
                    j = 2 * l + part
                    if j:
                        dve.wait_ge(spread, j)
                    if part == 0:
                        for k in range(CF):
                            if k % KQ == 0:
                                q = k // KQ
                                dve.wait_ge(quarter_loaded[q % 2], 32 * (2 * l + q // 2 + 1))
                            slot = k % (2 * KQ)
                            at = col[:, ENT_B + l * CF + k:ENT_B + l * CF + k + 1]
                            step = (nc.vector.tensor_scalar(acc[:], right[:, slot], at, None, ALU.mult) if k == 0 else
                                    nc.vector.scalar_tensor_tensor(acc[:], right[:, slot], at, acc[:], ALU.mult, ALU.add))
                            step.then_inc(accumulated, 1)
                            dve.wait_ge(accumulated, l * CF + k + 1)
                        dve.wait_ge(copied, CD * (l + 1))
                    else:
                        link(nc.vector.memset(acc[:], 0.0))
                        dve.wait_ge(pool_chained, 1 + 3 * (l + 1))
                    for m in range(CD):
                        square = raw[:, m, m * P:(m + 1) * P]
                        link(nc.vector.tensor_tensor(square, square, ident[:], ALU.add))
                        link(nc.vector.scalar_tensor_tensor(acc[:], raw[:, m], col[:, OFFSET + j * CD + m:OFFSET + j * CD + m + 1],
                                                            acc[:], ALU.mult, ALU.add))
                        nc.vector.tensor_scalar(raw[:, m], raw[:, m], col[:, GAIN + j * CD + m:GAIN + j * CD + m + 1], None, ALU.mult).then_inc(gained, 1)
                    for m in range(CD):
                        dve.wait_ge(rounded, CD * j + m + 1)
                        low_part(nc, folded[1][:, j, m], raw[:, m], folded[0][:, j, m]).then_inc(split, 1)
                    dve.wait_ge(spread, j + 1)
                    if part == 0:
                        link(nc.vector.tensor_tensor(bias[:, j], bias_ps[:], row[:, l], ALU.add))
                    else:
                        link(nc.vector.tensor_copy(bias[:, j], bias_ps[:]))
                        for p in range(PW):
                            r = l * PW + p
                            link(nc.vector.tensor_tensor(row[:, PB + r], row[:, PB + r], row[:, PH + r], ALU.mult))
                            link(nc.vector.tensor_tensor(bias[:, j], bias[:, j], row[:, PB + r], ALU.add))


def feed_forward(nc, x2, stat, gate_w, gate_b, folded, bias, out_norm, eps, half_pi, ident, out):
    with ExitStack() as ctx:
        sb = lambda n, s, dtype=F32: ctx.enter_context(nc.sbuf_tensor(n, s, dtype))
        pair = lambda n, s: [sb(f"{n}_{part}", s, F32R) for part in ("high", "low")]
        sem = lambda n: ctx.enter_context(nc.semaphore(n))
        G, STEPS = 4, 4
        UNITS, TURNS = G * STEPS, TILES // G
        T = G * P
        weights = pair("e_weights", [P, 2, CD, D])
        gb = sb("e_gb", [P, 2, CD])
        minus_quarter = sb("e_minus_quarter", [P, 1])
        xn = sb("e_xn", [P, G, D])
        xn_t = pair("e_xn_t", [P, CD, T])
        angle = sb("e_angle", [P, CD, T])
        sigma = sb("e_sigma", [P, CD, T])
        h_t = pair("e_h_t", [P, CD, T])
        y = sb("e_y", [P, G, D])
        total, neg_mean, squares, deviation, rstd = (sb(f"e_{n}", [P, G]) for n in ("total", "neg_mean", "squares", "deviation", "rstd"))
        scratch = sb("e_scratch", [P, D])
        turn_ps = ctx.enter_context(nc.psum_tensor("e_turn_ps", [P, 2, D], F32))
        mm_ps = ctx.enter_context(nc.psum_tensor("e_mm_ps", [P, 4, D], F32))
        loaded, preset = sem("e_loaded"), sem("e_preset")
        fetched, normed, x_turned, x_turned_out = sem("e_fetched"), sem("e_normed"), sem("e_x_turned"), sem("e_x_turned_out")
        gated, angled, folded_angle, sined, sigmad, h_ready = (
            sem(f"e_{n}") for n in ("gated", "angled", "folded_angle", "sined", "sigmad", "h_ready"))
        multiplied, biased, centred, squared, rooted, inverted, y_normed, y_turned, y_out = (
            sem(f"e_{n}") for n in ("multiplied", "biased", "centred", "squared", "rooted", "inverted", "y_normed", "y_turned", "y_out"))
        weights_rounded, weights_split, x_split, h_rounded, h_split, y_split = (
            sem(f"e_{n}") for n in ("weights_rounded", "weights_split", "x_split", "h_rounded", "h_split", "y_split"))
        gained, summed, stored = sem("e_gained"), sem("e_summed"), sem("e_stored")
        block = ctx.enter_context(nc.Block())
        out_tiles = out.rearrange("(i u p) d -> i p u d", u=G, p=P)
        MM = UNITS - G
        next_inputs = {UNITS - 3: (0,), UNITS - 2: (1, 2), UNITS - 1: (3,)}
        taken_inputs = {UNITS - 2: (0,), UNITS - 1: (1, 2, 3)}

        def row_of(t):
            return x2[:, bass.ds(t, 1)].rearrange("p t d -> p (t d)")

        @block.sync
        def _(sp):
            sp.dma_start(angle[:], gate_w[:, 0]).then_inc(loaded, 16)
            sp.dma_start(sigma[:], gate_w[:, 1]).then_inc(loaded, 16)
            sp.dma_start(gb[:], gate_b).then_inc(loaded, 16)

            def body(i):
                sp.wait_ge(summed, G * (i + 1))
                sp.dma_start(out_tiles[bass.ds(i, 1)].rearrange("i p u d -> p (i u) d"), y[:]).then_inc(stored, 16)
            repeat(sp, TURNS, body)
            sp.wait_ge(stored, 16 * TURNS)

        @block.gpsimd
        def _(pool):
            nc.gpsimd.memset(minus_quarter[:], -PI / 4).then_inc(preset, 1)

            def normalise_tiles(i):
                for u in range(G):
                    t = G * i + u
                    wait(pool, x_turned, t - G + 1)
                    nc.gpsimd.tensor_tensor(xn[:, u], row_of(t), stat[:, 0, bass.ds(t, 1)].to_broadcast([P, D]), ALU.add).then_inc(fetched, 1)
                    pool.wait_ge(fetched, t + 1)
                    nc.gpsimd.tensor_tensor(xn[:, u], xn[:, u], stat[:, 1, bass.ds(t, 1)].to_broadcast([P, D]), ALU.mult).then_inc(normed, 1)

            def body(i, final=False):
                if not final:
                    normalise_tiles(i + 1)
                for u in range(G):
                    t = G * i + u
                    done = 2 * t
                    pool.wait_ge(y_normed, UNITS * i + MM + u + 1)
                    nc.gpsimd.tensor_tensor(y[:, u], y[:, u], out_norm[:, 0], ALU.mult).then_inc(gained, 1)
                    pool.wait_ge(gained, done + 1)
                    nc.gpsimd.tensor_tensor(y[:, u], y[:, u], out_norm[:, 1], ALU.add).then_inc(gained, 1)
            normalise_tiles(0)
            repeat_to_last(pool, TURNS, body)

        RING = 2 * CD + UNITS

        @block.tensor
        def _(pe):
            def turn_input(t, u, i=None):
                pe.wait_ge(normed, t + 1)
                if u >= 2:
                    pe.wait_ge(x_split, t - 1)
                elif i is not None:
                    pe.wait_ge(y_split, MM * (i + 1) - 1 + u)
                for c in range(CD):
                    last = nc.tensor.transpose(turn_ps[:, u % 2, c * P:(c + 1) * P], xn[:, u, c * P:(c + 1) * P], ident[:])
                last.then_inc(x_turned, 1)

            def free_bank(i, r):
                before = r - 4
                if before < 0:
                    before += RING
                    i = i - 1
                if isinstance(i, int) and i < 0:
                    return
                if before < CD:
                    pe.wait_ge(angled, CD * i + before + 1)
                elif before < 2 * CD:
                    pe.wait_ge(sigmad, CD * i + before - CD + 1)
                else:
                    pe.wait_ge(biased, UNITS * i + before - 2 * CD + 1)

            def gate(i, r):
                free_bank(i, r)
                which, f = divmod(r, CD)
                for c in range(CD):
                    last = multiply_parts(nc, mm_ps[:, r % 4], [w[:, which, c, f * P:(f + 1) * P] for w in weights],
                                          [a[:, c] for a in xn_t], c == 0, c == CD - 1)
                last.then_inc(gated, 1)

            def multiply(i, q):
                j, u = divmod(q, G)
                if q == 0:
                    pe.wait_ge(h_split, CD * (i + 1))
                if j:
                    pe.wait_ge(y_split, MM * i + q - G + 1)
                free_bank(i, 2 * CD + q)
                for c in range(CD):
                    last = multiply_parts(nc, mm_ps[:, q % 4], [a[:, c, u * P:(u + 1) * P] for a in h_t],
                                          [w[:, j, c] for w in folded], c == 0, c == CD - 1)
                last.then_inc(multiplied, 1)

            def turn_y(i, q):
                pe.wait_ge(y_normed, UNITS * i + q + 1)
                if q >= 2:
                    pe.wait_ge(y_split, MM * i + q - 1)
                for c in range(CD):
                    last = nc.tensor.transpose(turn_ps[:, q % 2, c * P:(c + 1) * P], y[:, q % G, c * P:(c + 1) * P], ident[:])
                last.then_inc(y_turned, 1)

            pe.wait_ge(weights_split, 2)

            for u in range(G):
                turn_input(u, u)

            def body(i, final=False):
                pe.wait_ge(x_split, G * (i + 1))
                for r in range(2 * CD):
                    gate(i, r)
                for q in range(UNITS):
                    multiply(i, q)
                    if 2 <= q < MM + 2:
                        turn_y(i, q - 2)
                    if q in next_inputs and not final:
                        for u in next_inputs[q]:
                            turn_input(G * (i + 1) + u, u, i)
            repeat_to_last(pe, TURNS, body)

        @block.scalar
        def _(act):
            act.wait_ge(loaded, 48)
            for which, raw in enumerate((angle, sigma)):
                nc.scalar.activation(weights[0][:, which], raw[:], ACT.Copy).then_inc(weights_rounded, 1)
            act.wait_ge(preset, 1)
            act.wait_ge(weights_split, 2)

            def round_input(i, u):
                act.wait_ge(x_turned, G * i + u + 1)
                if u == 0:
                    wait(act, gated, 2 * CD * i)
                nc.scalar.activation(xn_t[0][:, :, u * P:(u + 1) * P], turn_ps[:, u % 2].rearrange("p (c x) -> p c x", c=CD), ACT.Copy).then_inc(x_turned_out, 1)

            for u in range(G):
                round_input(0, u)

            def body(i, final=False):
                for f in range(CD):
                    act.wait_ge(gated, 2 * CD * i + f + 1)
                    if f == 0:
                        wait(act, h_split, CD * i)
                    nc.scalar.activation(angle[:, f], mm_ps[:, f], ACT.Tanh, bias=gb[:, 0, f:f + 1]).then_inc(angled, 1)
                act.wait_ge(angled, CD * (i + 1))
                nc.scalar.activation(angle[:], angle[:], ACT.Abs, bias=minus_quarter[:], scale=PI).then_inc(folded_angle, 1)
                act.wait_ge(folded_angle, i + 1)
                nc.scalar.activation(angle[:], angle[:], ACT.Sin, bias=half_pi[:], scale=-1.0).then_inc(sined, 1)
                for f in range(CD):
                    act.wait_ge(gated, 2 * CD * i + CD + f + 1)
                    nc.scalar.activation(sigma[:, f], mm_ps[:, f], ACT.Sigmoid, bias=gb[:, 1, f:f + 1]).then_inc(sigmad, 1)
                for f in range(CD):
                    act.wait_ge(h_ready, CD * i + f + 1)
                    if f == 0:
                        wait(act, multiplied, UNITS * i)
                    nc.scalar.activation(h_t[0][:, f], angle[:, f], ACT.Copy).then_inc(h_rounded, 1)
                for q in range(UNITS):
                    u = q % G
                    n = UNITS * i + q
                    if 3 <= q < MM + 3:
                        store_turned(i, q - 3)
                    if q in taken_inputs and not final:
                        for v in taken_inputs[q]:
                            round_input(i + 1, v)
                    act.wait_ge(centred, n + 1)
                    wait(act, rooted, n)
                    nc.scalar.activation(scratch[:], y[:, u], ACT.Square, bias=neg_mean[:, u:u + 1], accum_out=squares[:, u:u + 1]).then_inc(squared, 1)
                    act.wait_ge(squared, n + 1)
                    nc.scalar.activation(deviation[:, u:u + 1], squares[:, u:u + 1], ACT.Sqrt, bias=eps[:], scale=1.0 / D).then_inc(rooted, 1)

            def store_turned(i, q):
                j, u = divmod(q, G)
                act.wait_ge(y_turned, MM * i + q + 1)
                act.wait_ge(multiplied, UNITS * i + q + 1)
                nc.scalar.activation(h_t[0][:, :, u * P:(u + 1) * P], turn_ps[:, q % 2].rearrange("p (c x) -> p c x", c=CD), ACT.Copy).then_inc(y_out, 1)

            repeat_to_last(act, TURNS, body)

        @block.vector
        def _(dve):
            def take(i, q):
                j, u = divmod(q, G)
                n = UNITS * i + q
                dve.wait_ge(multiplied, n + 1)
                if q >= G:
                    dve.wait_ge(y_turned, MM * i + q - G + 1)
                else:
                    wait(dve, stored, 16 * i)
                nc.vector.scalar_tensor_tensor(y[:, u], mm_ps[:, q % 4], 1.0, bias[:, j], ALU.mult, ALU.add, accum_out=total[:, u:u + 1]).then_inc(biased, 1)
                dve.wait_ge(biased, n + 1)
                nc.vector.tensor_scalar(neg_mean[:, u:u + 1], total[:, u:u + 1], -1.0 / D, None, ALU.mult).then_inc(centred, 1)

            def normalise(i, q):
                u, n = q % G, UNITS * i + q
                dve.wait_ge(rooted, n + 1)
                nc.vector.reciprocal(rstd[:, u:u + 1], deviation[:, u:u + 1]).then_inc(inverted, 1)
                dve.wait_ge(inverted, n + 1)
                nc.vector.tensor_scalar(y[:, u], y[:, u], neg_mean[:, u:u + 1], rstd[:, u:u + 1], ALU.add, ALU.mult).then_inc(y_normed, 1)

            def split_turned(i, q):
                u = q % G
                at = slice(u * P, (u + 1) * P)
                dve.wait_ge(y_out, MM * i + q + 1)
                low_part(nc, h_t[1][:, :, at], turn_ps[:, q % 2].rearrange("p (c x) -> p c x", c=CD), h_t[0][:, :, at]).then_inc(y_split, 1)

            dve.wait_ge(loaded, 48)
            for which, raw in enumerate((angle, sigma)):
                dve.wait_ge(weights_rounded, which + 1)
                low_part(nc, weights[1][:, which], raw[:], weights[0][:, which]).then_inc(weights_split, 1)

            def split_input(i, u):
                at = slice(u * P, (u + 1) * P)
                dve.wait_ge(x_turned_out, G * i + u + 1)
                low_part(nc, xn_t[1][:, :, at], turn_ps[:, u % 2].rearrange("p (c x) -> p c x", c=CD), xn_t[0][:, :, at]).then_inc(x_split, 1)

            for u in range(G):
                split_input(0, u)

            def body(i, final=False):
                dve.wait_ge(sined, i + 1)
                for f in range(CD):
                    dve.wait_ge(sigmad, CD * i + f + 1)
                    nc.vector.scalar_tensor_tensor(angle[:, f], angle[:, f], float(np.sqrt(2.0)), sigma[:, f], ALU.mult, ALU.mult).then_inc(h_ready, 1)
                for f in range(CD):
                    dve.wait_ge(h_rounded, CD * i + f + 1)
                    low_part(nc, h_t[1][:, f], angle[:, f], h_t[0][:, f]).then_inc(h_split, 1)
                for q in range(UNITS):
                    if 3 <= q < MM + 3:
                        split_turned(i, q - 3)
                    if q in taken_inputs and not final:
                        for v in taken_inputs[q]:
                            split_input(i + 1, v)
                    take(i, q)
                    if q:
                        normalise(i, q - 1)
                normalise(i, UNITS - 1)
                for u in range(G):
                    dve.wait_ge(gained, 2 * (G * i + u + 1))
                    nc.vector.scalar_tensor_tensor(y[:, u], y[:, u], 1.0, row_of(G * i + u), ALU.mult, ALU.add).then_inc(summed, 1)
            repeat_to_last(dve, TURNS, body)


def perceiver_block(nc, x, cache_t, packed, rope_q, rope_kv, amp_nat, phase_nat, basis_t, basis_o, amp_o, phase_o,
                    ent_in, ent_out, path, columns, rows, gate_w, gate_b, out):
    q_dram = nc.dram_tensor("carried_queries", (B, DC, H, S), F32, kind="Internal").ap()
    w_vo_dram = nc.dram_tensor("output_weights", (P, H, D), F32, kind="Internal").ap()
    with ExitStack() as ctx:
        sb = lambda n, s: ctx.enter_context(nc.sbuf_tensor(n, s, F32))
        ident = sb("ident", [P, P])
        stat = sb("stat", [P, 2, TILES])
        eps = sb("eps", [P, 1])
        half_pi = sb("half_pi", [P, 1])
        ready = ctx.enter_context(nc.semaphore("ident_ready"))
        with nc.Block() as block:
            @block.gpsimd
            def _(pool):
                nc.gpsimd.memset(ident[:], 0.0).then_inc(ready, 1)
                nc.gpsimd.memset(eps[:], EPS).then_inc(ready, 1)
                nc.gpsimd.memset(half_pi[:], PI / 2).then_inc(ready, 1)
                pool.wait_ge(ready, 3)
                nc.gpsimd.affine_select(out=ident[:], in_=ident[:], compare_op=ALU.not_equal, fill=1.0,
                                        base=0, pattern=[[-1, P]], channel_multiplier=1).then_inc(ready, 1)
                pool.wait_ge(ready, 4)
        with ExitStack() as scope:
            x_t = [scope.enter_context(nc.sbuf_tensor(f"x_t_{part}", [P, CD, S, B], F32R)) for part in ("high", "low")]
            normalise_input(nc, x, x_t, ident, eps)
            query_path(nc, packed, rope_q, x_t, w_vo_dram, q_dram)
        x1 = sb("x1", [P, TILES, D])
        cross_attention(nc, cache_t, rope_kv, x, q_dram, w_vo_dram, x1, stat, ident)
        root_deviations(nc, stat, eps, "x1")
        with ExitStack() as scope:
            basis, score_w, value_w, out_w = (scope.enter_context(nc.sbuf_tensor(n, shape, F32)) for n, shape in (
                ("basis", [P, CD, 2 * P]), ("score_w", [HARM, 16, HARM]), ("value_w", [P, 16, HARM]), ("out_w", [HARM, D])))
            holo_weights(nc, amp_nat, phase_nat, basis_t, basis_o, amp_o, phase_o, half_pi, basis, score_w, value_w, out_w)
            self_attention(nc, x1, stat, basis, score_w, value_w, out_w, ident)
        root_deviations(nc, stat, eps, "x2")
        folded = [ctx.enter_context(nc.sbuf_tensor(f"folded_{part}", [P, 4, CD, D], F32R)) for part in ("high", "low")]
        bias, out_norm = sb("bias", [P, 4, D]), sb("out_norm", [P, 2, D])
        fold_weights(nc, ent_in, ent_out, path, columns, rows, half_pi, ident, folded, bias, out_norm)
        feed_forward(nc, x1, stat, gate_w, gate_b, folded, bias, out_norm, eps, half_pi, ident, out)


def rope_tables(length, dim):
    inv = (1.0 / 10000.0 ** (np.arange(0, dim, 2, dtype=np.float32) / np.float32(dim))).astype(np.float32)
    f = np.arange(length, dtype=np.float32)[:, None] * inv[None, :]
    sin = np.repeat(np.sin(f.astype(np.float64)).astype(np.float32), 2, axis=-1)
    cos = np.repeat(np.cos(f.astype(np.float64)).astype(np.float32), 2, axis=-1)
    return sin, cos


def kernel(**inputs):
    import concourse.bacc as bacc
    from concourse.bass_utils import run_bass_kernel_spmd

    g = {name.replace("L0_", ""): np.asarray(a) for name, a in inputs.items()}
    sin_q, cos_q = rope_tables(S, DQ)
    sin_k, cos_k = rope_tables(L, DC)
    sign_q = np.where(np.arange(DQ) < DQ // 2, np.float32(1), np.float32(-1))
    swap_q = (np.arange(DQ) + DQ // 2) % DQ
    rope_q = np.stack([cos_q.T, (sin_q[:, swap_q] * sign_q).T]).reshape(2, CQ, P, S).transpose(2, 0, 1, 3)
    sign_k = np.where(np.arange(DC) < DC // 2, np.float32(-1), np.float32(1))
    rope_kv = np.stack([cos_k.T, (sin_k * sign_k).T], axis=1)

    w_qr = g["xattn_W_qr"]
    w_qr2 = np.concatenate([w_qr[:, DQ // 2:], w_qr[:, :DQ // 2]], axis=1)
    rows = lambda a, c: a.reshape(H, c, P, -1).transpose(0, 2, 1, 3).reshape(H, P, -1)
    w_kr = np.zeros((H, P, P), np.float32)
    w_kr[:, :R] = g["xattn_W_kr"].transpose(0, 2, 1)
    packed = np.concatenate([
        rows(g["xattn_Wq"].reshape(H, K, D).transpose(0, 2, 1), CD),
        rows(g["xattn_w_kc_q"].transpose(0, 2, 1), CQ),
        rows(w_qr, CQ), rows(w_qr2, CQ), w_kr, g["xattn_w_kc_kv"],
        g["xattn_Wo"].T.reshape(H, K, D)], axis=2)

    by_row = lambda a: a.reshape(CD, P, -1).transpose(1, 0, 2)
    three = lambda kind: by_row(np.concatenate([g[f"attn_{kind}_{n}"] for n in "qkv"], axis=1))

    column = lambda a: a.reshape(-1, P).T
    gains = [np.ones(D, np.float32), g["ffn_ln3_g"][0], g["ffn_ln4_g"][0], g["ffn_ln3_g"][1]]
    offsets = [np.zeros(D, np.float32), g["ffn_ln3_b"][0], g["ffn_ln4_b"][0], g["ffn_ln3_b"][1]]
    columns = np.concatenate([column(a) for a in (*gains, *offsets, *g["ffn_ent_b"])], axis=1)
    rows_ = np.concatenate([g["ffn_ent_pb"], g["ffn_path_b"].reshape(-1, D), g["ffn_phase"].reshape(-1, D),
                            g["ffn_ln4_g"][1:], g["ffn_ln4_b"][1:]])
    ent = lambda a: a.reshape(2, CF, P, D).transpose(0, 2, 1, 3)

    arrays = {
        "x": g["x"].reshape(B * S, D), "cache_t": g["ctx_512"].transpose(0, 2, 1), "packed": packed,
        "rope_q": rope_q, "rope_kv": rope_kv,
        "amp_nat": three("amp"), "phase_nat": three("phase"),
        "basis_t": by_row(np.concatenate([g[f"attn_basis_{n}"].T for n in "qvkk"], axis=1)),
        "basis_o": by_row(g["attn_basis_o"].T), "amp_o": g["attn_amp_o"].T, "phase_o": g["attn_phase_o"].T,
        "ent_in": ent(g["ffn_ent_w"].transpose(0, 2, 1)), "ent_out": ent(g["ffn_ent_pw"]),
        "path": g["ffn_path_w"].reshape(2, 2, CD, P, D).transpose(0, 3, 1, 2, 4),
        "columns": columns, "rows": rows_,
        "gate_w": np.stack([by_row(g["ffn_ph_w"]), by_row(g["ffn_amp_w"])], axis=1),
        "gate_b": np.stack([column(g["ffn_ph_b"]), column(g["ffn_amp_b"])], axis=1),
    }
    arrays = {name: np.ascontiguousarray(a) for name, a in arrays.items()}
    nc = bacc.Bacc("TRN2", target_bir_lowering=False, num_devices=1)
    args = [nc.dram_tensor(name, a.shape, mybir.dt.from_np(a.dtype), kind="ExternalInput").ap() for name, a in arrays.items()]
    out = nc.dram_tensor("out", (B * S, D), F32, kind="ExternalOutput").ap()
    perceiver_block(nc, *args, out)
    result = run_bass_kernel_spmd(nc, [arrays], core_ids=[0])
    return result.results[0]["out"].reshape(B, S, D)
```

```python
from contextlib import ExitStack

import numpy as np
import concourse.bass as bass
from concourse import mybir

ALU = mybir.AluOpType
ACT = mybir.ActivationFunctionType
F32 = mybir.dt.float32
F32R = mybir.dt.float32r
AX_X = mybir.AxisListType.X

P = 128
B, S, D = 64, 32, 512
L, DC = 257, 128
H, K = 16, 128
DQ, R = 384, 64
HARM, HD = 64, 32
FE = 2048
TILES = B * S // P
BT = P // S
CD, CQ, CF = D // P, DQ // P, FE // P
SG = 8
NSG = S // SG
HG = 4
EPS = 1e-5
PI = float(np.pi)

W_Q, W_KCQ, W_QR, W_QR2, W_KR, W_KV, W_O, W_ALL = np.cumsum([0, D, DQ, CQ * R, CQ * R, P, P, D]).tolist()


def wait(engine, sem, value):
    if isinstance(value, int) and value <= 0:
        return
    engine.wait_ge(sem, value)


def repeat(engine, count, body):
    body(0)
    with engine.Fori(1, count) as i:
        body(i)


def repeat_to_last(engine, count, body):
    body(0)
    with engine.Fori(1, count - 1) as i:
        body(i)
    body(count - 1, final=True)


def multiply_parts(nc, out, left, right, start, stop):
    nc.tensor.matmul(out, left[0], right[0], start=start, stop=False)
    nc.tensor.matmul(out, left[0], right[1], start=False, stop=False)
    return nc.tensor.matmul(out, left[1], right[0], start=False, stop=stop)


def low_part(nc, low, value, high):
    return nc.vector.tensor_tensor(low, value, high.bitcast(F32), ALU.subtract)


def normalise_input(nc, x, x_t, ident, eps, heads):
    with ExitStack() as ctx:
        sb = lambda n, s: ctx.enter_context(nc.sbuf_tensor(n, s, F32))
        used = []

        def sem(name):
            handle = ctx.enter_context(nc.semaphore(name))
            used.append(handle.num)
            return handle

        xin = sb("a_xin", [P, 2, 4, D])
        xn = sb("a_xn", [P, 4, D])
        total, neg_mean, squares, deviation, rstd = (
            sb(f"a_{n}", [P, 2, 4]) for n in ("total", "neg_mean", "squares", "deviation", "rstd"))
        scratch = sb("a_scratch", [P, D])
        flipped = ctx.enter_context(nc.psum_tensor("a_flipped", [P, 2, D], F32))
        x_loaded = [[sem(f"a_x_loaded{w}{u}") for u in range(4)] for w in range(2)]
        normed, turned, stored, chained, inverted = (
            sem(f"a_{n}") for n in ("normed", "turned", "stored", "chained", "inverted"))
        centred, squared, rooted, rounded = sem("a_centred"), sem("a_squared"), sem("a_rooted"), sem("a_rounded")
        x_tiles = x.rearrange("(t p) d -> t p d", p=P)

        def placed(part, t):
            return part[:, :, :, bass.ds(t * BT, BT)].rearrange("p c s b -> p c b s")

        def by_batch(u):
            return flipped[:, u % 2].rearrange("p (c b s) -> p c b s", c=CD, b=BT)

        block = ctx.enter_context(nc.Block())

        TURNS = TILES // 4

        def in_pairs(engine, step):
            step(0, 0, 0)
            step(1, 1, 0)
            with engine.Fori(1, TURNS // 2) as pair:
                step(2 * pair, 0, pair)
                step(2 * pair + 1, 1, pair)
            step(TURNS, 0, TURNS // 2, last=True)

        @block.sync
        def _(sp):
            def step(i, w, pair, last=False):
                if last:
                    return
                for u in range(4):
                    wait(sp, normed, 4 * (i - 2) + u + 1)
                    sp.dma_start(xin[:, w, u], x_tiles[bass.ds(4 * i + u, 1)].rearrange("t p d -> p (t d)")).then_inc(x_loaded[w][u], 16)
            in_pairs(sp, step)
            heads.first(sp)

        @block.vector
        def _(dve):
            def step(i, w, pair, last=False):
                if not last:
                    for u in range(4):
                        dve.wait_ge(x_loaded[w][u], 16 * (pair + 1))
                        nc.vector.tensor_reduce(total[:, w, u:u + 1], xin[:, w, u], AX_X, ALU.add).then_inc(chained, 1)
                    dve.wait_ge(chained, 4 * (i + 1))
                    nc.vector.tensor_scalar(neg_mean[:, w], total[:, w], -1.0 / D, None, ALU.mult).then_inc(centred, 1)
                if not isinstance(i, int) or i > 0:
                    normalise(i - 1, 1 - w)

            def normalise(i, w):
                dve.wait_ge(rooted, i + 1)
                nc.vector.reciprocal(rstd[:, w], deviation[:, w]).then_inc(inverted, 1)
                dve.wait_ge(inverted, i + 1)
                for u in range(4):
                    wait(dve, turned, 4 * (i - 1) + u + 1)
                    nc.vector.tensor_scalar(xn[:, u], xin[:, w, u], neg_mean[:, w, u:u + 1], rstd[:, w, u:u + 1], ALU.add,
                                            ALU.mult).then_inc(normed, 1)
                for u in range(4):
                    dve.wait_ge(rounded, 4 * i + u + 1)
                    low_part(nc, placed(x_t[1], 4 * i + u), by_batch(u), placed(x_t[0], 4 * i + u)).then_inc(stored, 1)
            in_pairs(dve, step)

        @block.tensor
        def _(pe):
            def body(i):
                for u in range(4):
                    pe.wait_ge(normed, 4 * i + u + 1)
                    wait(pe, stored, 4 * i + u - 1)
                    for c in range(CD):
                        last = nc.tensor.transpose(flipped[:, u % 2, c * P:(c + 1) * P], xn[:, u, c * P:(c + 1) * P], ident[:])
                    last.then_inc(turned, 1)
            repeat(pe, TILES // 4, body)

        @block.scalar
        def _(act):
            def step(i, w, pair, last=False):
                if not last:
                    act.wait_ge(centred, i + 1)
                    for u in range(4):
                        wait(act, squared, 4 * i + u)
                        nc.scalar.activation(scratch[:], xin[:, w, u], ACT.Square, bias=neg_mean[:, w, u:u + 1],
                                             accum_out=squares[:, w, u:u + 1]).then_inc(squared, 1)
                    act.wait_ge(squared, 4 * i + 4)
                    nc.scalar.activation(deviation[:, w], squares[:, w], ACT.Sqrt, bias=eps[:], scale=1.0 / D).then_inc(rooted, 1)
                if not isinstance(i, int) or i > 0:
                    for u in range(4):
                        act.wait_ge(turned, 4 * (i - 1) + u + 1)
                        nc.scalar.activation(placed(x_t[0], 4 * (i - 1) + u), by_batch(u), ACT.Copy).then_inc(rounded, 1)
            in_pairs(act, step)
    return used


class HeadWeights:

    def __init__(self, nc, ctx, packed, rope_q):
        sb = lambda n, s: ctx.enter_context(nc.sbuf_tensor(n, s, F32))
        self.packed, self.rope_q = packed, rope_q
        self.w = sb("b_w", [P, HG, W_ALL])
        self.table = sb("b_table", [P, 2, CQ, S])
        self.w_loaded = [ctx.enter_context(nc.semaphore(f"b_w_loaded{u}")) for u in range(HG)]
        self.table_loaded = ctx.enter_context(nc.semaphore("b_table_loaded"))

    def load(self, sp, i, hh):
        sp.dma_start(self.w[:, hh], self.packed[bass.ds(HG * i + hh, 1)].rearrange("h p n -> p (h n)")).then_inc(self.w_loaded[hh], 16)

    def first(self, sp):
        sp.dma_start(self.table[:], self.rope_q).then_inc(self.table_loaded, 16)
        for hh in range(HG):
            self.load(sp, 0, hh)


def query_path(nc, heads, x_t, w_vo_dram, q_dram):
    with ExitStack() as ctx:
        sb = lambda n, s: ctx.enter_context(nc.sbuf_tensor(n, s, F32))
        used = []

        def sem(name):
            handle = ctx.enter_context(nc.semaphore(name))
            used.append(handle.num)
            return handle

        pair = lambda n, s: [ctx.enter_context(nc.sbuf_tensor(f"{n}_{part}", s, F32R)) for part in ("high", "low")]
        w, table, w_loaded, table_loaded = heads.w, heads.table, heads.w_loaded, heads.table_loaded
        w_parts = pair("b_w_parts", [P, 2, W_QR])
        rot = sb("b_rot", [P, 2, CQ, SG, R])
        rot_parts = pair("b_rot_parts", [P, 2, CQ, SG, R])
        sin_part = sb("b_sin_part", [P, 2, CQ, SG, R])
        q_sb = sb("b_q", [P, 2, SG * B])
        m_sb = sb("b_m", [P, 2, SG * R])
        qr_sb = sb("b_qr", [R, 2, SG * B])
        w_vo = sb("b_w_vo", [P, 2, D])
        staged = sb("b_staged", [P, 2, B, HG // 2, S])
        ps = ctx.enter_context(nc.psum_tensor("b_ps", [P, 8, D], F32))
        staged_out = [sem(f"b_staged_out{u}") for u in range(2)]
        w_vo_out = [sem(f"b_w_vo_out{u}") for u in range(2)]
        cos_ready, sin_ready, rot_summed, rot_rounded, rot_ready = (
            sem(f"b_{n}") for n in ("cos_ready", "sin_ready", "rot_summed", "rot_rounded", "rot_ready"))
        w_rounded, w_split = sem("b_w_rounded"), sem("b_w_split")
        a_done, a_stored = sem("b_a_done"), sem("b_a_stored")
        m_done, m_stored = sem("b_m_done"), sem("b_m_stored")
        qr_done, qr_stored = sem("b_qr_done"), sem("b_qr_stored")
        qc_done, qc_stored = sem("b_qc_done"), sem("b_qc_stored")
        STEPS = HG * NSG
        TURNS = H // HG
        LAST = TURNS * STEPS
        turn_steps = [(m // NSG, m % NSG, m) for m in range(STEPS)]
        q_out = q_dram.rearrange("b d h s -> d b (h s)")
        block = ctx.enter_context(nc.Block())

        def a_count(i, hh, g):
            return (NSG + 1) * (HG * i + hh) + g + 1

        @block.sync
        def _(sp):
            def load(i, hh):
                wait(sp, qc_done, NSG * (HG * (i - 1) + hh + 1))
                heads.load(sp, i, hh)

            def store(i, pair):
                sp.wait_ge(qc_stored, STEPS * i + (pair + 1) * STEPS // 2)
                sp.dma_start(q_out[:, :, bass.ds((2 * i + pair) * HG // 2 * S, HG // 2 * S)],
                             staged[:, pair].rearrange("p b h s -> p b (h s)")).then_inc(staged_out[pair], 16)

            def store_weights(i, hh):
                sp.wait_ge(a_stored, a_count(i, hh, NSG))
                sp.dma_start(w_vo_dram[:, bass.ds(HG * i + hh, 1)].rearrange("p h n -> p (h n)"), w_vo[:, hh % 2]).then_inc(w_vo_out[hh % 2], 16)

            with sp.Fori(0, TURNS - 1) as i:
                for pair in range(2):
                    for hh in (2 * pair, 2 * pair + 1):
                        store_weights(i, hh)
                        load(i + 1, hh)
                    store(i, pair)
            for pair in range(2):
                for hh in (2 * pair, 2 * pair + 1):
                    store_weights(TURNS - 1, hh)
                store(TURNS - 1, pair)
            for pair in range(2):
                sp.wait_ge(staged_out[pair], 16 * TURNS)
                sp.wait_ge(w_vo_out[pair], 16 * 2 * TURNS)

        def rotated(engine, out, hh, g, column, which):
            weight = w[:, hh, column:column + CQ * R].rearrange("p (c r) -> p c r", c=CQ).unsqueeze(2)
            angle = table[:, which, :, g * SG:(g + 1) * SG].unsqueeze(3)
            shape = [P, CQ, SG, R]
            return engine.tensor_tensor(out, weight.to_broadcast(shape), angle.to_broadcast(shape), ALU.mult)

        @block.gpsimd
        def _(pool):
            pool.wait_ge(table_loaded, 16)

            def body(i):
                for hh, g, m in turn_steps:
                    n = STEPS * i + m
                    if g == 0:
                        pool.wait_ge(w_loaded[hh], 16 * (i + 1))
                    wait(pool, rot_summed, n - 1)
                    rotated(nc.gpsimd, sin_part[:, m % 2], hh, g, W_QR2, 1).then_inc(sin_ready, 1)
            repeat(pool, TURNS, body)

        @block.vector
        def _(dve):
            def store_m(n, slot):
                dve.wait_ge(m_done, n + 1)
                wait(dve, qr_done, n - 1)
                nc.vector.tensor_copy(m_sb[:, slot], ps[:, 2 + slot]).then_inc(m_stored, 1)

            def split_weights(head, hh):
                dve.wait_ge(w_rounded, head + 1)
                low_part(nc, w_parts[1][:, hh % 2], w[:, hh, 0:W_QR], w_parts[0][:, hh % 2]).then_inc(w_split, 1)

            def cos_part(i, n, m):
                hh, g = m // NSG, m % NSG
                if g == 0:
                    dve.wait_ge(w_loaded[hh], 16 * (i + 1))
                wait(dve, rot_ready, n - 1)
                rotated(nc.vector, rot[:, m % 2], hh, g, W_QR, 0).then_inc(cos_ready, 1)

            def add_sin_part(n, m):
                dve.wait_ge(sin_ready, n + 1)
                dve.wait_ge(cos_ready, n + 1)
                nc.vector.tensor_tensor(rot[:, m % 2], rot[:, m % 2], sin_part[:, m % 2], ALU.add).then_inc(rot_summed, 1)

            dve.wait_ge(table_loaded, 16)
            cos_part(0, 0, 0)
            add_sin_part(0, 0)
            split_weights(0, 0)

            def body(i, final=False):
                first = isinstance(i, int) and i == 0
                for hh, g, m in turn_steps:
                    n = STEPS * i + m
                    more = not (final and m == STEPS - 1)
                    if more:
                        cos_part(i + (m + 1) // STEPS, n + 1, (m + 1) % STEPS)
                    if m or not first:
                        store_m(n - 1, (m - 1) % 2)
                    dve.wait_ge(rot_rounded, n + 1)
                    low_part(nc, rot_parts[1][:, m % 2], rot[:, m % 2], rot_parts[0][:, m % 2]).then_inc(rot_ready, 1)
                    if more:
                        add_sin_part(n + 1, (m + 1) % 2)
                    if g == 2 and not (final and hh == HG - 1):
                        split_weights(HG * i + hh + 1, (hh + 1) % HG)
            repeat_to_last(dve, TURNS, body)
            store_m(LAST - 1, (STEPS - 1) % 2)

        @block.tensor
        def _(pe):
            def project_query(i, hh, g):
                if g == 0:
                    pe.wait_ge(w_split, HG * i + hh + 1)
                wait(pe, a_stored, a_count(i, hh, g) - 2)
                for c in range(CD):
                    last = multiply_parts(nc, ps[:, (hh + g) % 2], [a[:, hh % 2, W_Q + c * P:W_Q + (c + 1) * P] for a in w_parts],
                                          [a[:, c, g * SG:(g + 1) * SG].rearrange("p s b -> p (s b)") for a in x_t],
                                          c == 0, c == CD - 1)
                last.then_inc(a_done, 1)

            def product_m(n, m, hh):
                pe.wait_ge(rot_ready, n + 1)
                wait(pe, m_stored, n - 1)
                for c in range(CQ):
                    last = multiply_parts(nc, ps[:, 2 + m % 2], [a[:, hh % 2, W_KCQ + c * P:W_KCQ + (c + 1) * P] for a in w_parts],
                                          [a[:, m % 2, c].rearrange("p s r -> p (s r)") for a in rot_parts], c == 0, c == CQ - 1)
                last.then_inc(m_done, 1)

            def output_weight(i, hh):
                pe.wait_ge(a_stored, a_count(i, hh, NSG) - 2)
                nc.tensor.matmul(ps[:, (hh + NSG) % 2], w[:, hh, W_KV:W_KV + P], w[:, hh, W_O:W_O + D],
                                 start=True, stop=True).then_inc(a_done, 1)

            def reduce_query(n, m, i):
                hh, g = (m % STEPS) // NSG, m % NSG
                pe.wait_ge(m_stored, n + 1)
                pe.wait_ge(a_stored, a_count(i if m >= 0 else i - 1, hh, g))
                wait(pe, qr_stored, n - 1)
                for s in range(SG):
                    last = nc.tensor.matmul(ps[0:R, 4 + m % 2, s * B:(s + 1) * B], m_sb[:, m % 2, s * R:(s + 1) * R],
                                            q_sb[:, m % 2, s * B:(s + 1) * B], start=True, stop=True)
                last.then_inc(qr_done, 1)

            def carry_query(n, m):
                hh = (m % STEPS) // NSG
                pe.wait_ge(qr_stored, n + 1)
                wait(pe, qc_stored, n - 1)
                nc.tensor.matmul(ps[:, 6 + m % 2], w[0:R, hh, W_KR:W_KR + DC], qr_sb[:, m % 2],
                                 start=True, stop=True).then_inc(qc_done, 1)

            def body(i):
                first = isinstance(i, int)
                for hh, g, m in turn_steps:
                    n = STEPS * i + m
                    project_query(i, hh, g)
                    product_m(n, m, hh)
                    if g == NSG - 1:
                        output_weight(i, hh)
                    if m >= 2 or not first:
                        carry_query(n - 2, m - 2)
                    if m >= 1 or not first:
                        reduce_query(n - 1, m - 1, i)
            repeat(pe, TURNS, body)
            carry_query(LAST - 2, STEPS - 2)
            reduce_query(LAST - 1, STEPS - 1, TURNS - 1)
            carry_query(LAST - 1, STEPS - 1)

        @block.scalar
        def _(act):
            def store_qr(n, m):
                act.wait_ge(qr_done, n + 1)
                wait(act, qc_done, n - 1)
                nc.scalar.activation(qr_sb[:, m % 2], ps[0:R, 4 + m % 2], ACT.Copy).then_inc(qr_stored, 1)

            def store_qc(n, m):
                hh, g = (m % STEPS) // NSG, m % NSG
                act.wait_ge(qc_done, n + 1)
                out = staged[:, hh // 2, :, hh % 2, g * SG:(g + 1) * SG].rearrange("p b s -> p s b")
                nc.scalar.activation(out, ps[:, 6 + m % 2].rearrange("p (s b) -> p s b", s=SG), ACT.Copy).then_inc(qc_stored, 1)

            def round_weights(i, head, hh):
                act.wait_ge(w_loaded[hh], 16 * (i + 1))
                wait(act, m_done, NSG * (head - 1))
                nc.scalar.activation(w_parts[0][:, hh % 2], w[:, hh, 0:W_QR], ACT.Copy).then_inc(w_rounded, 1)

            def round_rotated(n, m):
                act.wait_ge(rot_summed, n + 1)
                wait(act, m_done, n - 1)
                nc.scalar.activation(rot_parts[0][:, m % 2], rot[:, m % 2], ACT.Copy).then_inc(rot_rounded, 1)

            round_weights(0, 0, 0)
            round_rotated(0, 0)

            def body(i, final=False):
                first = isinstance(i, int) and i == 0
                for hh, g, m in turn_steps:
                    n = STEPS * i + m
                    act.wait_ge(a_done, a_count(i, hh, g))
                    wait(act, qr_done, n - 1)
                    nc.scalar.activation(q_sb[:, m % 2], ps[:, (hh + g) % 2], ACT.Copy).then_inc(a_stored, 1)
                    if g == NSG - 1:
                        act.wait_ge(a_done, a_count(i, hh, NSG))
                        if hh >= 2 or not first:
                            act.wait_ge(w_vo_out[hh % 2], 16 * (2 * i + hh // 2))
                        nc.scalar.activation(w_vo[:, hh % 2], ps[:, (hh + NSG) % 2], ACT.Copy).then_inc(a_stored, 1)
                    if m >= 3 or not first:
                        if (m - 3) % (STEPS // 2) == 0 and not (first and m == 3):
                            wait(act, staged_out[(m - 3) // (STEPS // 2)], 16 * i)
                        store_qc(n - 3, m - 3)
                    if not (final and m == STEPS - 1):
                        round_rotated(n + 1, m + 1)
                    if g == 1 and not (final and hh == HG - 1):
                        round_weights(i + (hh + 1) // HG, HG * i + hh + 1, (hh + 1) % HG)
                    if m >= 1 or not first:
                        store_qr(n - 1, m - 1)
            repeat_to_last(act, TURNS, body)
            store_qr(LAST - 1, STEPS - 1)
            for lag in (3, 2, 1):
                store_qc(LAST - lag, STEPS - lag)
    return used


def cross_attention(nc, cache_t, rope_kv, x, q_dram, w_vo_dram, x1, stat, ident, left_counted):
    with ExitStack() as ctx:
        sb = lambda n, s, dtype=F32: ctx.enter_context(nc.sbuf_tensor(n, s, dtype))
        pair = lambda n, s: [sb(f"{n}_{part}", s, F32R) for part in ("high", "low")]
        sem = lambda n: ctx.enter_context(nc.semaphore(n))
        CH = H // HG
        STEPS = BT * CH
        table = sb("c_table", [P, 2, L])
        raw = sb("c_raw", [P, BT, L])
        swapped = sb("c_swapped", [P, BT, L])
        part = sb("c_part", [P, 2, L])
        kv_t = sb("c_kv_t", [P, BT, L])
        kv = sb("c_kv", [P, BT, 2, P])
        kv_end = sb("c_kv_end", [1, BT, P])
        q = sb("c_q", [P, BT, H * S])
        peak = sb("c_peak", [P, 4])
        total = sb("c_total", [P, 4])
        inverse = sb("c_inverse", [P, 4])
        e = sb("c_e", [P, 4, L])
        e_t = sb("c_e_t", [P, 2, 2, H * S])
        e_t_end = sb("c_e_t_end", [1, 2, H * S])
        mixed = pair("c_mixed", [P, H, BT, S])
        w_vo = pair("c_w_vo", [P, H, D])
        w_vo_raw = sb("c_w_vo_raw", [P, 4, D])
        scratch = sb("c_scratch", [P, D])
        row_sum, neg_mean, squares = (sb(f"c_{n}", [P, 1]) for n in ("row_sum", "neg_mean", "squares"))
        sc_ps = ctx.enter_context(nc.psum_tensor("c_sc_ps", [P, 2, D], F32))
        et_ps = ctx.enter_context(nc.psum_tensor("c_et_ps", [P, 2, D], F32))
        mix_ps = ctx.enter_context(nc.psum_tensor("c_mix_ps", [P, 2, D], F32))
        out_ps = ctx.enter_context(nc.psum_tensor("c_out_ps", [P, D], F32))
        kv_ps = ctx.enter_context(nc.psum_tensor("c_kv_ps", [P, D], F32))
        table_loaded, x_loaded = sem("c_table_loaded"), sem("c_x_loaded")
        q_loaded = [sem(f"c_q_loaded{u}") for u in range(BT)]
        raw_loaded = [sem(f"c_raw_loaded{u}") for u in range(BT)]
        rotated_, kv_turned, kv_stored, pool_chained = sem("c_rotated"), sem("c_kv_turned"), sem("c_kv_stored"), sem("c_pool_chained")
        scored, peaked, exped, normed = sem("c_scored"), sem("c_peaked"), sem("c_exped"), sem("c_normed")
        turned, et_stored, mix_done, mix_stored = sem("c_turned"), sem("c_et_stored"), sem("c_mix_done"), sem("c_mix_stored")
        out_done, out_free, dve_chained = sem("c_out_done"), sem("c_out_free"), sem("c_dve_chained")
        w_vo_loaded, w_vo_rounded, w_vo_split, mix_rounded = (
            sem(f"c_{n}") for n in ("w_vo_loaded", "w_vo_rounded", "w_vo_split", "mix_rounded"))
        centred, squared, kept = sem("c_centred"), sem("c_squared"), sem("c_kept")
        CHUNKS = B * CH
        block = ctx.enter_context(nc.Block())
        q_in = q_dram.rearrange("b d h s -> b d (h s)")
        x_tiles = x.rearrange("(t p) d -> t p d", p=P)

        @block.sync
        def _(sp):
            sp.dma_start(table[:], rope_kv).then_inc(table_loaded, 16)

            def body(i):
                for u in range(BT):
                    b = BT * i + u
                    wait(sp, rotated_, b - BT + 1)
                    at = bass.ds(b, 1)
                    sp.dma_start(raw[:, u], cache_t[at].rearrange("b d l -> d (b l)")).then_inc(raw_loaded[u], 16)
                    half = DC // 2
                    for lo, hi in ((0, half), (half, 0)):
                        sp.dma_start(swapped[lo:lo + half, u], cache_t[at, hi:hi + half].rearrange("b d l -> d (b l)")).then_inc(raw_loaded[u], 16)
                    wait(sp, scored, CH * (b - BT + 1))
                    sp.dma_start(q[:, u], q_in[at].rearrange("b d x -> d (b x)")).then_inc(q_loaded[u], 16)
                sp.dma_start(x1[:, bass.ds(i, 1)].rearrange("p t d -> p (t d)"),
                             x_tiles[bass.ds(i, 1)].rearrange("t p d -> p (t d)")).then_inc(x_loaded, 16)
            repeat(sp, TILES, body)
            sp.wait_ge(x_loaded, 16 * TILES)

        @block.gpsimd
        def _(pool):
            pool.sem_clear(left_counted)
            pool.wait_ge(table_loaded, 16)

            def body(i):
                for u in range(BT):
                    b = BT * i + u
                    pool.wait_ge(raw_loaded[u], 48 * (i + 1))
                    nc.gpsimd.tensor_tensor(part[:, 0], raw[:, u], table[:, 0], ALU.mult).then_inc(pool_chained, 1)
                    nc.gpsimd.tensor_tensor(part[:, 1], swapped[:, u], table[:, 1], ALU.mult).then_inc(pool_chained, 1)
                    pool.wait_ge(pool_chained, 2 * b + 2)
                    wait(pool, scored, CH * (b - BT + 1))
                    wait(pool, kv_turned, b - BT + 1)
                    nc.gpsimd.tensor_tensor(kv_t[:, u], part[:, 0], part[:, 1], ALU.add).then_inc(rotated_, 1)
                    pool.wait_ge(rotated_, b + 1)
            repeat(pool, TILES, body)

        @block.vector
        def _(dve):
            def find_peak(n, j):
                dve.wait_ge(scored, n + 1)
                wait(dve, exped, n - 3)
                nc.vector.tensor_reduce(peak[:, j % 4:j % 4 + 1], sc_ps[:, j % 2, 0:L], AX_X, ALU.max,
                                        negate=True).then_inc(peaked, 1)

            def normalise(n, j):
                k = j % 4
                dve.wait_ge(exped, n + 1)
                nc.vector.reciprocal(inverse[:, k:k + 1], total[:, k:k + 1]).then_inc(dve_chained, 1)
                dve.wait_ge(dve_chained, n + 1)
                nc.vector.tensor_scalar(e[:, k], e[:, k], inverse[:, k:k + 1], None, ALU.mult).then_inc(normed, 1)

            def store_mixed(t, u):
                dve.wait_ge(mix_rounded, BT * t + u + 1)
                low_part(nc, mixed[1][:, :, u], mix_ps[:, u % 2].rearrange("p (h s) -> p h s", h=H), mixed[0][:, :, u]).then_inc(mix_stored, 1)

            def add_out(t):
                dve.wait_ge(x_loaded, 16 * (t + 1))
                dve.wait_ge(out_done, t + 1)
                row = x1[:, bass.ds(t, 1)].rearrange("p t d -> p (t d)")
                nc.vector.scalar_tensor_tensor(row, out_ps[:], 1.0, row, ALU.mult, ALU.add, accum_out=row_sum[:]).then_inc(out_free, 1)
                dve.wait_ge(out_free, t + 2)
                nc.vector.tensor_scalar(neg_mean[:], row_sum[:], -1.0 / D, None, ALU.mult).then_inc(centred, 1)

            def keep_moments(t):
                dve.wait_ge(squared, t + 1)
                nc.vector.tensor_copy(stat[:, 0, bass.ds(t, 1)], neg_mean[:])
                nc.vector.tensor_copy(stat[:, 1, bass.ds(t, 1)], squares[:]).then_inc(kept, 1)

            def body(i):
                first = isinstance(i, int)
                for j in range(STEPS):
                    n = STEPS * i + j
                    find_peak(n, j)
                    if j or not first:
                        normalise(n - 1, j - 1)
                    if j in stores:
                        back, u = stores[j]
                        if not (first and back):
                            store_mixed(i - back, u)
                    if j == 13 and not first:
                        add_out(i - 1)
                    if j == 15 and not first:
                        keep_moments(i - 1)
                    if first and j % CH == 3:
                        k = j // CH
                        dve.wait_ge(w_vo_rounded, k + 1)
                        low_part(nc, w_vo[1][:, 4 * k:4 * k + 4], w_vo_raw[:], w_vo[0][:, 4 * k:4 * k + 4]).then_inc(w_vo_split, 1)
            stores = {14: (0, 0), 15: (0, 1), 2: (1, 2), 5: (1, 3)}
            dve.sem_inc(out_free, 1)
            dve.sem_inc(kept, 1)
            repeat(dve, TILES, body)
            normalise(CHUNKS - 1, STEPS - 1)
            store_mixed(TILES - 1, BT - 2)
            store_mixed(TILES - 1, BT - 1)
            add_out(TILES - 1)
            keep_moments(TILES - 1)

        @block.scalar
        def _(act):
            def exponential(n, j):
                k = j % 4
                act.wait_ge(peaked, n + 1)
                wait(act, turned, n - 3)
                nc.scalar.activation(e[:, k], sc_ps[:, j % 2, 0:L], ACT.Exp, bias=peak[:, k:k + 1],
                                     accum_out=total[:, k:k + 1]).then_inc(exped, 1)

            def store_turned(n, b, j):
                u, c = (j // CH) % 2, j % CH
                act.wait_ge(turned, n + 1)
                if c == 0:
                    wait(act, mix_done, b - 1)
                nc.scalar.activation(e_t[:, u, :, c * P:(c + 1) * P], et_ps[:, j % 2, 0:2 * P].rearrange("p (k x) -> p k x", k=2), ACT.Copy)
                nc.scalar.activation(e_t_end[:, u, c * P:(c + 1) * P], et_ps[0:1, j % 2, 2 * P:3 * P], ACT.Copy).then_inc(et_stored, 1)

            def square_row(t):
                act.wait_ge(centred, t + 1)
                act.wait_ge(kept, t + 1)
                row = x1[:, bass.ds(t, 1)].rearrange("p t d -> p (t d)")
                nc.scalar.activation(scratch[:], row, ACT.Square, bias=neg_mean[:], accum_out=squares[:]).then_inc(squared, 1)

            def store_kv(b, u):
                act.wait_ge(kv_turned, b + 1)
                wait(act, mix_done, b - BT + 1)
                nc.scalar.activation(kv[:, u], kv_ps[:, 0:2 * P].rearrange("p (k x) -> p k x", k=2), ACT.Copy)
                nc.scalar.activation(kv_end[:, u], kv_ps[0:1, 2 * P:3 * P], ACT.Copy).then_inc(kv_stored, 1)

            def round_mixed(t, u):
                act.wait_ge(mix_done, BT * t + u + 1)
                if u == 0:
                    wait(act, out_done, t)
                nc.scalar.activation(mixed[0][:, :, u], mix_ps[:, u % 2].rearrange("p (h s) -> p h s", h=H), ACT.Copy).then_inc(mix_rounded, 1)

            def body(i):
                first = isinstance(i, int)
                for j in range(STEPS):
                    n, u = STEPS * i + j, j // CH
                    exponential(n, j)
                    if j >= 2 or not first:
                        store_turned(n - 2, BT * i + (j - 2) // CH, (j - 2) % STEPS)
                    if j % CH == 1:
                        store_kv(BT * i + u, u)
                    if j in rounds:
                        back, u = rounds[j]
                        if not (first and back):
                            round_mixed(i - back, u)
                    if j == 14 and not first:
                        square_row(i - 1)
                    if first and j % CH == 3:
                        k = j // CH
                        act.wait_ge(w_vo_loaded, 16 * (k + 1))
                        nc.scalar.activation(w_vo[0][:, 4 * k:4 * k + 4], w_vo_raw[:], ACT.Copy).then_inc(w_vo_rounded, 1)
                    if first and j % CH == 1 and j > 1:
                        load_output_weights(j // CH)

            def load_output_weights(k):
                wait(act, w_vo_split, k)
                act.dma_start(w_vo_raw[:], w_vo_dram[:, 4 * k:4 * k + 4]).then_inc(w_vo_loaded, 16)

            load_output_weights(0)
            rounds = {12: (0, 0), 13: (0, 1), 0: (1, 2), 4: (1, 3)}
            repeat(act, TILES, body)
            store_turned(CHUNKS - 2, B - 1, STEPS - 2)
            store_turned(CHUNKS - 1, B - 1, STEPS - 1)
            round_mixed(TILES - 1, BT - 2)
            round_mixed(TILES - 1, BT - 1)
            square_row(TILES - 1)

        @block.tensor
        def _(pe):
            def score(n, b, t, j):
                u, c = j // CH, j % CH
                if c == 0:
                    pe.wait_ge(q_loaded[u], 16 * (t + 1))
                    pe.wait_ge(rotated_, b + 1)
                wait(pe, exped, n - 1)
                nc.tensor.matmul(sc_ps[:, j % 2, 0:L], q[:, u, c * P:(c + 1) * P], kv_t[:, u],
                                 start=True, stop=True).then_inc(scored, 1)

            def turn_kv(b, u):
                pe.wait_ge(rotated_, b + 1)
                wait(pe, kv_stored, b)
                for k in range(2):
                    nc.tensor.transpose(kv_ps[:, k * P:(k + 1) * P], kv_t[:, u, k * P:(k + 1) * P], ident[:])
                nc.tensor.transpose(kv_ps[0:1, 2 * P:3 * P], kv_t[:, u, 2 * P:L], ident[:]).then_inc(kv_turned, 1)

            def turn_weights(n, j):
                pe.wait_ge(normed, n + 1)
                wait(pe, et_stored, n - 1)
                for k in range(2):
                    nc.tensor.transpose(et_ps[:, j % 2, k * P:(k + 1) * P], e[:, j % 4, k * P:(k + 1) * P], ident[:])
                nc.tensor.transpose(et_ps[0:1, j % 2, 2 * P:3 * P], e[:, j % 4, 2 * P:L], ident[:]).then_inc(turned, 1)

            def mix(b, u):
                pe.wait_ge(et_stored, CH * (b + 1))
                pe.wait_ge(kv_stored, b + 1)
                wait(pe, mix_stored, b - 1)
                out = mix_ps[:, u % 2]
                for k in range(2):
                    nc.tensor.matmul(out, kv[:, u, k], e_t[:, u % 2, k], start=k == 0, stop=False)
                nc.tensor.matmul(out, kv_end[:, u], e_t_end[:, u % 2], start=False, stop=True).then_inc(mix_done, 1)

            def project(t, heads):
                if heads[0] == 0:
                    pe.wait_ge(w_vo_split, H // 4)
                    pe.wait_ge(mix_stored, BT * (t + 1))
                    pe.wait_ge(out_free, t + 1)
                for h in heads:
                    last = multiply_parts(nc, out_ps[:], [a[:, h].rearrange("p b s -> p (b s)") for a in mixed],
                                          [w[:, h] for w in w_vo], h == 0, h == H - 1)
                if heads[-1] == H - 1:
                    last.then_inc(out_done, 1)

            shares = {5: range(0, 3), 7: range(3, 6), 8: range(6, 9), 9: range(9, 12), 11: range(12, H)}

            def body(i, first=False, final=False):
                for j in range(STEPS):
                    n, u = STEPS * i + j, j // CH
                    if not (final and j >= STEPS - 2):
                        ahead = (j + 2) % STEPS
                        t = i + (j + 2) // STEPS
                        score(n + 2, BT * t + ahead // CH, t, ahead)
                    if j % CH == 0:
                        turn_kv(BT * i + u, u)
                    if j in shares and not first:
                        project(i - 1, shares[j])
                    if j % CH == 2 and (j > CH or not first):
                        mix(BT * i + u - 1, (u - 1) % BT)
                    if j or not first:
                        turn_weights(n - 1, (j - 1) % STEPS)
            score(0, 0, 0, 0)
            score(1, 0, 0, 1)
            body(0, first=True)
            with pe.Fori(1, TILES - 1) as i:
                body(i)
            body(TILES - 1, final=True)
            turn_weights(CHUNKS - 1, STEPS - 1)
            mix(B - 1, BT - 1)
            project(TILES - 1, range(H))


def root_deviations(nc, stat, eps, name):
    with nc.semaphore(f"{name}_rooted") as rooted, nc.semaphore(f"{name}_inverted") as inverted, nc.Block() as block:
        @block.scalar
        def _(act):
            nc.scalar.activation(stat[:, 1], stat[:, 1], ACT.Sqrt, bias=eps[:], scale=1.0 / D).then_inc(rooted, 1)

        @block.vector
        def _(dve):
            dve.wait_ge(rooted, 1)
            nc.vector.reciprocal(stat[:, 1], stat[:, 1]).then_inc(inverted, 1)
            dve.wait_ge(inverted, 1)


MAGIC = 1.5 * 2.0 ** 23
TURN_HI = 6.28125
TURN_LO = 2 * PI - TURN_HI


def head_of(hh):
    chunk, k = divmod(hh, HG)
    return 8 * (chunk // 2) + 2 * k + chunk % 2


def holo_weights(nc, amp_nat, phase_nat, basis_t, basis_o, amp_o, phase_o, half_pi, basis, score_w, value_w, out_w):
    with ExitStack() as ctx:
        sb = lambda n, s: ctx.enter_context(nc.sbuf_tensor(n, s, F32))
        sem = lambda n: ctx.enter_context(nc.semaphore(n))
        NAT, OUT = CD * 3 * HARM, D
        amp = sb("h_amp", [P, NAT + OUT])
        phase = sb("h_phase", [P, NAT + OUT])
        turns = sb("h_turns", [P, NAT + OUT])
        bo = sb("h_bo", [P, CD, HARM])
        ps = ctx.enter_context(nc.psum_tensor("h_ps", [P, 8, 512], F32))
        loaded, cleared, stepped, cosined, weighed, multiplied, kept = (
            sem(f"h_{n}") for n in ("loaded", "cleared", "stepped", "cosined", "weighed", "multiplied", "kept"))
        block = ctx.enter_context(nc.Block())

        @block.sync
        def _(sp):
            sp.dma_start(phase[:, 0:NAT], phase_nat.rearrange("p t i -> p (t i)")).then_inc(loaded, 16)
            sp.wait_ge(cleared, 1)
            sp.dma_start(phase[0:HARM, NAT:], phase_o).then_inc(loaded, 16)
            sp.dma_start(amp[:, 0:NAT], amp_nat.rearrange("p t i -> p (t i)")).then_inc(loaded, 16)
            sp.wait_ge(cleared, 2)
            sp.dma_start(amp[0:HARM, NAT:], amp_o).then_inc(loaded, 16)
            sp.dma_start(bo[:], basis_o).then_inc(loaded, 16)
            sp.dma_start(basis[:], basis_t).then_inc(loaded, 16)
            sp.wait_ge(loaded, 96)

        @block.vector
        def _(dve):
            nc.vector.memset(phase[:, NAT:], 0.0).then_inc(cleared, 1)
            nc.vector.memset(amp[:, NAT:], 0.0).then_inc(cleared, 1)
            dve.wait_ge(loaded, 96)
            dve.wait_ge(cleared, 2)
            steps = (
                lambda: nc.vector.tensor_scalar(turns[:], phase[:], 1.0 / (2 * PI), MAGIC, ALU.mult, ALU.add),
                lambda: nc.vector.tensor_scalar(turns[:], turns[:], MAGIC, None, ALU.subtract),
                lambda: nc.vector.scalar_tensor_tensor(phase[:], turns[:], -TURN_HI, phase[:], ALU.mult, ALU.add),
                lambda: nc.vector.scalar_tensor_tensor(phase[:], turns[:], -TURN_LO, phase[:], ALU.mult, ALU.add),
            )
            for n, step in enumerate(steps):
                step().then_inc(stepped, 1)
                dve.wait_ge(stepped, n + 1)
            dve.wait_ge(cosined, 2)
            nc.vector.tensor_tensor(amp[:], amp[:], phase[:], ALU.mult).then_inc(weighed, 1)
            dve.wait_ge(weighed, 1)
            nc.vector.tensor_copy(out_w[:], amp[0:HARM, NAT:])
            dve.wait_ge(multiplied, 1)
            nc.vector.tensor_scalar(score_w[:].rearrange("p (t r) j -> p r t j", r=4),
                                    ps[0:HARM, 0:4, 0:4 * HARM].rearrange("p r (t j) -> p r t j", t=4),
                                    float(np.float32(1.0) / np.sqrt(np.float32(HD))), None, ALU.mult).then_inc(kept, 1)
            dve.wait_ge(kept, 1)

        @block.scalar
        def _(act):
            act.wait_ge(stepped, 4)
            nc.scalar.activation(phase[:], phase[:], ACT.Abs).then_inc(cosined, 1)
            act.wait_ge(cosined, 1)
            nc.scalar.activation(phase[:], phase[:], ACT.Sin, bias=half_pi[:], scale=-1.0).then_inc(cosined, 1)
            act.wait_ge(multiplied, 2)
            places = value_w[HARM:2 * HARM].rearrange("p (c cp k kp) j -> p c cp k kp j", c=2, cp=2, k=2)
            for r in range(4):
                for c in range(2):
                    nc.scalar.activation(places[:, c, r % 2, :, r // 2],
                                         ps[HARM:2 * HARM, 4 + r, c * 2 * HARM:(c + 1) * 2 * HARM].rearrange("p (k j) -> p k j", k=2), ACT.Copy)

        @block.tensor
        def _(pe):
            pe.wait_ge(weighed, 1)
            weights = amp[:, 0:NAT].rearrange("p (t w i) -> p t w i", t=CD, w=3)

            def rows(h):
                return slice(h % 4 * HD, h % 4 * HD + HD), h // 4

            for h in range(16):
                at, t = rows(h)
                last = nc.tensor.matmul(ps[0:HARM, h % 4, t * HARM:(t + 1) * HARM], weights[at, t, 0], weights[at, t, 1],
                                        start=True, stop=True)
            last.then_inc(multiplied, 1)
            for hh in range(16):
                h, c, k = head_of(hh), hh // 8, hh % 4 // 2
                at, t = rows(h)
                last = nc.tensor.matmul(ps[HARM:2 * HARM, 4 + h % 4, (2 * c + k) * HARM:(2 * c + k + 1) * HARM], weights[at, t, 2], bo[at, t],
                                        start=True, stop=True)
            last.then_inc(multiplied, 1)


def self_attention(nc, x1, stat, basis, score_w, value_w, out_w, ident, loads):
    with ExitStack() as ctx:
        sb = lambda n, s: ctx.enter_context(nc.sbuf_tensor(n, s, F32))
        sem = lambda n: ctx.enter_context(nc.semaphore(n))
        HH = 16
        xn = sb("d_xn", [P, 2, D])
        xn_t = sb("d_xn_t", [P, CD, P])
        reduced = sb("d_reduced", [P, 2, P])
        keys = sb("d_keys", [P, 2, BT, 2, S])
        u_sb = sb("d_u", [P, 2, BT, HG, S])
        shifted = sb("d_shifted", [P, 2, HH, S])
        e = sb("d_e", [P, 2, HH, S])
        peak, total, inverse = (sb(f"d_{n}", [P, 2, HH]) for n in ("peak", "total", "inverse"))
        e_t = sb("d_e_t", [P, HH, P])
        z_sb = sb("d_z", [P, HH, HARM])
        ro_sb = sb("d_ro", [HARM, P])
        scratch = sb("d_scratch", [P, D])
        row_sum, neg_mean, squares = (sb(f"d_{n}", [P, 1]) for n in ("row_sum", "neg_mean", "squares"))
        ps = ctx.enter_context(nc.psum_tensor("d_ps", [P, 8, D], F32))
        T_BANK, R_BANK, U_BANK, S_BANK, P_BANK, Z_BANK = 0, 1, 2, 4, 5, 6
        fetched, normed, turned, turned_out = sem("d_fetched"), sem("d_normed"), sem("d_turned"), sem("d_turned_out")
        reduced_done, reduced_out = sem("d_reduced_done"), sem("d_reduced_out")
        u_done, u_out_a, u_out_d = sem("d_u_done"), sem("d_u_out_a"), sem("d_u_out_d")
        scored, peaked, shifted_out, exped, summed, inverted, weighed = (
            sem(f"d_{n}") for n in ("scored", "peaked", "shifted_out", "exped", "summed", "inverted", "weighed"))
        e_turned, e_out_a, e_out_d = sem("d_e_turned"), sem("d_e_out_a"), sem("d_e_out_d")
        z_done, z_out_a, z_out_d = sem("d_z_done"), sem("d_z_out_a"), sem("d_z_out_d")
        ro_done, ro_out, out_done, added = sem("d_ro_done"), sem("d_ro_out"), sem("d_out_done"), sem("d_added")
        centred, squared, kept, cleared = sem("d_centred"), sem("d_squared"), sem("d_kept"), sem("d_cleared")
        TURNS = TILES // 2
        block = ctx.enter_context(nc.Block())

        def row_of(t):
            return x1[:, bass.ds(t, 1)].rearrange("p t d -> p (t d)")

        def copy_blocks(engine, batches):
            for b in batches:
                at = slice(b * S, (b + 1) * S)
                out, in_ = e_t[at, :, at], ps[at, P_BANK].rearrange("p (h s) -> p h s", h=HH)
                last = nc.vector.tensor_copy(out, in_) if engine == "dve" else nc.scalar.activation(out, in_, ACT.Copy)
            return last

        def in_steps(engine, step):
            step(0, 0, mid=False, old=False)
            step(1, 1, old=False)
            with engine.Fori(1, TURNS) as i:
                step(2 * i, 0)
                step(2 * i + 1, 1)
            step(TILES, 0, new=False)
            step(TILES + 1, 1, new=False, mid=False)

        @block.sync
        def _(sp):
            loads.first(sp)

        @block.gpsimd
        def _(pool):
            nc.gpsimd.memset(e_t[:], 0.0).then_inc(cleared, 1)
            nc.gpsimd.memset(keys[:], 0.0).then_inc(cleared, 1)

            def body(i):
                for v in range(2):
                    t = 2 * i + v
                    wait(pool, turned, t - 1)
                    nc.gpsimd.tensor_tensor(xn[:, v], row_of(t), stat[:, 0, bass.ds(t, 1)].to_broadcast([P, D]), ALU.add).then_inc(fetched, 1)
                    pool.wait_ge(fetched, t + 1)
                    nc.gpsimd.tensor_tensor(xn[:, v], xn[:, v], stat[:, 1, bass.ds(t, 1)].to_broadcast([P, D]), ALU.mult).then_inc(normed, 1)
            repeat(pool, TURNS, body)

        @block.tensor
        def _(pe):
            def turn_input(t, v):
                pe.wait_ge(normed, t + 1)
                wait(pe, turned_out, t)
                for c in range(CD):
                    last = nc.tensor.transpose(ps[:, T_BANK, c * P:(c + 1) * P], xn[:, v, c * P:(c + 1) * P], ident[:])
                last.then_inc(turned, 1)

            def reduce_input(t, v):
                pe.wait_ge(turned_out, t + 1)
                wait(pe, reduced_out, t)
                wait(pe, ro_out, t - 1)
                for m in range(2):
                    for c in range(CD):
                        last = nc.tensor.matmul(ps[:, R_BANK, m * P:(m + 1) * P], basis[:, c, m * P:(m + 1) * P], xn_t[:, c],
                                                start=c == 0, stop=c == CD - 1)
                last.then_inc(reduced_done, 1)

            def score_weights(t, v):
                pe.wait_ge(reduced_out, t + 1)
                wait(pe, u_out_a, t)
                wait(pe, u_out_d, t)
                for g in range(2):
                    for k in range(HG):
                        h = 8 * g + 2 * k
                        last = nc.tensor.matmul(ps[:, U_BANK + g, k * P:(k + 1) * P], score_w[:, h:h + 2].rearrange("p h j -> p (h j)"),
                                                reduced[0:HARM, v], start=True, stop=True)
                last.then_inc(u_done, 1)

            def score(t, v):
                pe.wait_ge(u_out_a, t + 1)
                pe.wait_ge(u_out_d, t + 1)
                wait(pe, shifted_out, t)
                out = ps[:, S_BANK].rearrange("p (g q b s) -> p g b q s", g=2, q=2, b=BT)
                for g in range(2):
                    for b in range(BT):
                        last = nc.tensor.matmul(out[:, g, b], u_sb[:, g, b].rearrange("p k s -> p (k s)"),
                                                keys[:, v, b].rearrange("p q s -> p (q s)"), start=True, stop=True)
                last.then_inc(scored, 1)

            def value_weights(t, v):
                wait(pe, z_out_a, t)
                wait(pe, z_out_d, t)
                for g in range(2):
                    last = nc.tensor.matmul(ps[:, Z_BANK + g], reduced[HARM:2 * HARM, v],
                                            value_w[HARM:2 * HARM, 8 * g:8 * g + 8].rearrange("p h j -> p (h j)"), start=True, stop=True)
                last.then_inc(z_done, 1)

            def turn_weights(t, v):
                pe.wait_ge(weighed, t + 1)
                wait(pe, added, t)
                for c in range(HG):
                    last = nc.tensor.transpose(ps[:, P_BANK, c * P:(c + 1) * P],
                                               e[:, v, 4 * c:4 * c + 4].rearrange("p b s -> p (b s)"), ident[:])
                last.then_inc(e_turned, 1)

            def mix(t):
                for done in (e_out_a, e_out_d, z_out_a, z_out_d):
                    pe.wait_ge(done, t + 1)
                for h in range(HH):
                    last = nc.tensor.matmul(ps[0:HARM, R_BANK, 2 * P:3 * P], z_sb[:, h], e_t[:, h], start=h == 0, stop=h == HH - 1)
                last.then_inc(ro_done, 1)

            def project(t):
                pe.wait_ge(ro_out, t + 1)
                nc.tensor.matmul(ps[:, P_BANK], ro_sb[:], out_w[:], start=True, stop=True).then_inc(out_done, 1)

            def step(t, v, new=True, mid=True, old=True):
                if new:
                    turn_input(t, v)
                if old:
                    project(t - 2)
                if mid:
                    value_weights(t - 1, 1 - v)
                if new:
                    reduce_input(t, v)
                if mid:
                    turn_weights(t - 1, 1 - v)
                if new:
                    score_weights(t, v)
                if mid:
                    mix(t - 1)
                if new:
                    score(t, v)
            in_steps(pe, step)

        @block.vector
        def _(dve):
            def shift(t, v):
                scores = ps[:, S_BANK].rearrange("p (h s) -> p h s", h=HH)
                dve.wait_ge(scored, t + 1)
                nc.vector.tensor_reduce(peak[:, v], scores, AX_X, ALU.max).then_inc(peaked, 1)
                dve.wait_ge(peaked, t + 1)
                nc.vector.tensor_tensor(shifted[:, v], scores, peak[:, v].unsqueeze(2).to_broadcast([P, HH, S]),
                                        ALU.subtract).then_inc(shifted_out, 1)

            def weigh(t, v):
                dve.wait_ge(exped, t + 1)
                nc.vector.tensor_reduce(total[:, v], e[:, v], AX_X, ALU.add).then_inc(summed, 1)
                dve.wait_ge(summed, t + 1)
                nc.vector.reciprocal(inverse[:, v], total[:, v]).then_inc(inverted, 1)
                dve.wait_ge(inverted, t + 1)
                nc.vector.tensor_tensor(e[:, v], e[:, v], inverse[:, v].unsqueeze(2).to_broadcast([P, HH, S]), ALU.mult).then_inc(weighed, 1)

            def step(t, v, new=True, mid=True, old=True):
                if mid:
                    weigh(t - 1, 1 - v)
                if old:
                    dve.wait_ge(out_done, t - 1)
                    nc.vector.scalar_tensor_tensor(row_of(t - 2), ps[:, P_BANK], 1.0, row_of(t - 2), ALU.mult, ALU.add,
                                                   accum_out=row_sum[:]).then_inc(added, 1)
                    dve.wait_ge(added, t - 1)
                    nc.vector.tensor_scalar(neg_mean[:], row_sum[:], -1.0 / D, None, ALU.mult).then_inc(centred, 1)
                if mid:
                    dve.wait_ge(z_done, t)
                    wait(dve, ro_done, t - 1)
                    nc.vector.tensor_copy(z_sb[:, 0:8].rearrange("p h j -> p (h j)"), ps[:, Z_BANK]).then_inc(z_out_d, 1)
                if mid:
                    dve.wait_ge(e_turned, t)
                    copy_blocks("dve", (0, 1)).then_inc(e_out_d, 1)
                if old:
                    dve.wait_ge(squared, t - 1)
                    nc.vector.tensor_copy(stat[:, 0, bass.ds(t - 2, 1)], neg_mean[:])
                    nc.vector.tensor_copy(stat[:, 1, bass.ds(t - 2, 1)], squares[:]).then_inc(kept, 1)
                if new:
                    dve.wait_ge(u_done, t + 1)
                    wait(dve, scored, t)
                    nc.vector.tensor_copy(u_sb[:, 1], ps[:, U_BANK + 1].rearrange("p (k b s) -> p b k s", k=HG, b=BT)).then_inc(u_out_d, 1)
                    shift(t, v)

            dve.sem_inc(kept, 1)
            dve.wait_ge(cleared, 1)
            in_steps(dve, step)

        @block.scalar
        def _(act):
            def step(t, v, new=True, mid=True, old=True):
                if new:
                    act.wait_ge(turned, t + 1)
                    wait(act, reduced_done, t)
                    nc.scalar.activation(xn_t[:], ps[:, T_BANK].rearrange("p (c x) -> p c x", c=CD), ACT.Copy).then_inc(turned_out, 1)
                if mid:
                    act.wait_ge(z_done, t)
                    wait(act, ro_done, t - 1)
                    nc.scalar.activation(z_sb[:, 8:16].rearrange("p h j -> p (h j)"), ps[:, Z_BANK + 1], ACT.Copy).then_inc(z_out_a, 1)
                if new:
                    act.wait_ge(reduced_done, t + 1)
                    wait(act, scored, t - 1)
                    wait(act, z_done, t - 1)
                    nc.scalar.activation(reduced[:, v], ps[:, R_BANK, 0:P], ACT.Copy)
                    for parity in range(2):
                        at = slice(parity * HARM, (parity + 1) * HARM)
                        last_key = nc.scalar.activation(keys[at, v, :, parity], ps[at, R_BANK, P:2 * P].rearrange("p (b s) -> p b s", b=BT), ACT.Copy)
                    last_key.then_inc(reduced_out, 1)
                if old:
                    act.wait_ge(centred, t - 1)
                    act.wait_ge(kept, t - 1)
                    nc.scalar.activation(scratch[:], row_of(t - 2), ACT.Square, bias=neg_mean[:], accum_out=squares[:]).then_inc(squared, 1)
                if mid:
                    act.wait_ge(e_turned, t)
                    copy_blocks("act", (2, 3)).then_inc(e_out_a, 1)
                if new:
                    act.wait_ge(u_done, t + 1)
                    wait(act, scored, t)
                    nc.scalar.activation(u_sb[:, 0], ps[:, U_BANK].rearrange("p (k b s) -> p b k s", k=HG, b=BT), ACT.Copy).then_inc(u_out_a, 1)
                if mid:
                    act.wait_ge(ro_done, t)
                    wait(act, out_done, t - 1)
                    nc.scalar.activation(ro_sb[:], ps[0:HARM, R_BANK, 2 * P:3 * P], ACT.Copy).then_inc(ro_out, 1)
                if new:
                    act.wait_ge(shifted_out, t + 1)
                    wait(act, e_turned, t - 1)
                    nc.scalar.activation(e[:, v], shifted[:, v], ACT.Exp).then_inc(exped, 1)

            act.wait_ge(cleared, 2)
            in_steps(act, step)


LAYERS, PW, QUARTERS = 2, 2, 4
KQ = CF // QUARTERS


class FoldLoads:

    def __init__(self, nc, ctx, paths, ent_in, ent_out, path, columns):
        sb = lambda n, s: ctx.enter_context(nc.sbuf_tensor(n, s, F32))
        sem = lambda n: ctx.enter_context(nc.semaphore(n))
        self.ent_in, self.ent_out, self.path, self.columns = ent_in, ent_out, path, columns
        self.left = sb("f_left", [P, CF // 2, D])
        self.right = sb("f_right", [P, CF // 2, D])
        self.paths = paths
        self.col = sb("f_col", [P, 8 * CD + LAYERS * CF])
        self.quarter_loaded = [sem(f"f_quarter_loaded{q}") for q in range(2)]
        self.paths_loaded, self.col_loaded = sem("f_paths_loaded"), sem("f_col_loaded")

    def quarter(self, sp, l, q):
        at = slice(q * KQ, (q + 1) * KQ)
        slot = slice(q % 2 * KQ, (q % 2 + 1) * KQ)
        sp.dma_start(self.left[:, slot], self.ent_in[l, :, at]).then_inc(self.quarter_loaded[q % 2], 16)
        sp.dma_start(self.right[:, slot], self.ent_out[l, :, at]).then_inc(self.quarter_loaded[q % 2], 16)

    def first(self, sp):
        sp.dma_start(self.col[:], self.columns).then_inc(self.col_loaded, 16)
        self.quarter(sp, 0, 0)
        self.quarter(sp, 0, 1)
        sp.dma_start(self.paths[:], self.path[0]).then_inc(self.paths_loaded, 16)


def fold_weights(nc, loads, path, rows, half_pi, ident, folded, bias, out_norm, gate):
    PB, PH = LAYERS, LAYERS + LAYERS * PW
    with ExitStack() as ctx:
        sb = lambda n, s: ctx.enter_context(nc.sbuf_tensor(n, s, F32))
        sem = lambda n: ctx.enter_context(nc.semaphore(n))
        NR = LAYERS + 2 * LAYERS * PW + 2
        left, right, paths, col = loads.left, loads.right, loads.paths, loads.col
        quarter_loaded, paths_loaded = loads.quarter_loaded, loads.paths_loaded
        raw = sb("f_raw", [P, 2, CD, D])
        turns = raw[:, 0, 0:LAYERS * PW]
        row = sb("f_row", [P, NR, D])
        acc = sb("f_acc", [P, 2 * LAYERS, D])
        ones = sb("f_ones", [P, P])
        ps = ctx.enter_context(nc.psum_tensor("f_ps", [P, CD, D], F32))
        bias_ps = ctx.enter_context(nc.psum_tensor("f_bias_ps", [P, 2 * LAYERS, D], F32))
        rows_loaded, summed = sem("f_rows_loaded"), sem("f_summed")
        chained, cosined, multiplied, quarter_used, copied, pool_chained = (
            sem(f"f_{n}") for n in ("chained", "cosined", "multiplied", "quarter_used", "copied", "pool_chained"))
        accumulated, spread, modulated, gained, rounded, split = (
            sem(f"f_{n}") for n in ("accumulated", "spread", "modulated", "gained", "rounded", "split"))
        block = ctx.enter_context(nc.Block())
        STAGES = (0, 1, 3, 2)
        GAIN, OFFSET, ENT_B = 0, 4 * CD, 8 * CD
        MODS = slice(PH, PH + LAYERS * PW)

        @block.sync
        def _(sp):
            sp.dma_start(row[:].rearrange("p r d -> p (r d)"), rows.rearrange("(o r) d -> o (r d)", o=1).to_broadcast([P, NR * D])).then_inc(rows_loaded, 16)
            for l in range(LAYERS):
                for q in range(QUARTERS):
                    turn = QUARTERS * l + q
                    if turn >= 2:
                        sp.wait_ge(quarter_used, turn - 1)
                        sp.wait_ge(accumulated, (turn - 1) * KQ)
                        loads.quarter(sp, l, q)
                if l == 0:
                    sp.wait_ge(pool_chained, 3)
                    sp.wait_ge(summed, 1)
                    sp.dma_start(paths[:], path[1]).then_inc(paths_loaded, 16)
            sp.wait_ge(paths_loaded, 16 * LAYERS)
            sp.wait_ge(summed, LAYERS)
            gate.load(sp)

        @block.gpsimd
        def _(pool):
            nc.gpsimd.memset(ones[:], 1.0).then_inc(pool_chained, 1)
            pool.wait_ge(modulated, 1)
            for l in range(LAYERS):
                pool.wait_ge(paths_loaded, 16 * (l + 1))
                for p in range(PW):
                    mod = row[:, PH + l * PW + p].unsqueeze(1).to_broadcast([P, CD, D])
                    nc.gpsimd.tensor_tensor(paths[:, p], paths[:, p], mod, ALU.mult).then_inc(pool_chained, 1)
                pool.wait_ge(pool_chained, 1 + PW * (l + 1))
                if l:
                    pool.wait_ge(split, 2 * CD)
                nc.gpsimd.tensor_tensor(raw[:, 1], paths[:, 0], paths[:, 1], ALU.add).then_inc(summed, 1)

        @block.tensor
        def _(pe):
            def spread_bias(j, n):
                pe.wait_ge(gained, CD * (n + 1))
                nc.tensor.matmul(bias_ps[:, j], ones[:], acc[:, j], start=True, stop=True).then_inc(spread, 1)

            pe.wait_ge(pool_chained, 1)
            for l in range(LAYERS):
                for q in range(QUARTERS):
                    pe.wait_ge(quarter_loaded[q % 2], 32 * (2 * l + q // 2 + 1))
                    for k in range(q * KQ, (q + 1) * KQ):
                        slot = k % (2 * KQ)
                        for m in range(CD):
                            if l and k == 0:
                                pe.wait_ge(copied, CD * l)
                            last = nc.tensor.matmul(ps[:, m], left[:, slot, m * P:(m + 1) * P], right[:, slot], start=k == 0, stop=k == CF - 1)
                    last.then_inc(quarter_used, 1)
                    if l and q == 1:
                        spread_bias(0, 0)
                        spread_bias(1, 1)
            spread_bias(3, 2)
            spread_bias(2, 3)

        @block.scalar
        def _(act):
            act.wait_ge(chained, 5)
            nc.scalar.activation(turns, row[:, MODS], ACT.Abs).then_inc(cosined, 1)
            act.wait_ge(cosined, 1)
            nc.scalar.activation(row[:, MODS], turns, ACT.Sin, bias=half_pi[:], scale=-1.0).then_inc(cosined, 1)
            act.wait_ge(cosined, 2)
            for n, j in enumerate(STAGES):
                if j % 2 == 0:
                    act.wait_ge(quarter_used, QUARTERS * (j // 2 + 1))
                    for m in range(CD):
                        nc.scalar.activation(raw[:, 0, m], ps[:, m], ACT.Copy).then_inc(copied, 1)
                for m in range(CD):
                    act.wait_ge(gained, CD * n + m + 1)
                    nc.scalar.activation(folded[0][:, j, m], raw[:, j % 2, m], ACT.Copy).then_inc(rounded, 1)

        @block.vector
        def _(dve):
            count = [0]

            def link(instruction):
                count[0] += 1
                instruction.then_inc(chained, 1)
                dve.wait_ge(chained, count[0])

            def sum_entangled(l):
                for k in range(CF):
                    if k % KQ == 0:
                        q = k // KQ
                        dve.wait_ge(quarter_loaded[q % 2], 32 * (2 * l + q // 2 + 1))
                    slot, sum_ = k % (2 * KQ), acc[:, 2 * l]
                    at = col[:, ENT_B + l * CF + k:ENT_B + l * CF + k + 1]
                    step = (nc.vector.tensor_scalar(sum_, right[:, slot], at, None, ALU.mult) if k == 0 else
                            nc.vector.scalar_tensor_tensor(sum_, right[:, slot], at, sum_, ALU.mult, ALU.add))
                    step.then_inc(accumulated, 1)
                    dve.wait_ge(accumulated, l * CF + k + 1)

            def finish(j, n):
                if j % 2 == 0:
                    dve.wait_ge(copied, CD * (j // 2 + 1))
                else:
                    link(nc.vector.memset(acc[:, j], 0.0))
                    dve.wait_ge(summed, j // 2 + 1)
                matrix = raw[:, j % 2]
                for m in range(CD):
                    square = matrix[:, m, m * P:(m + 1) * P]
                    link(nc.vector.tensor_tensor(square, square, ident[:], ALU.add))
                    link(nc.vector.scalar_tensor_tensor(acc[:, j], matrix[:, m], col[:, OFFSET + j * CD + m:OFFSET + j * CD + m + 1],
                                                        acc[:, j], ALU.mult, ALU.add))
                    nc.vector.tensor_scalar(matrix[:, m], matrix[:, m], col[:, GAIN + j * CD + m:GAIN + j * CD + m + 1], None, ALU.mult).then_inc(gained, 1)
                for m in range(CD):
                    dve.wait_ge(rounded, CD * n + m + 1)
                    low_part(nc, folded[1][:, j, m], matrix[:, m], folded[0][:, j, m]).then_inc(split, 1)

            def keep_bias(j, n):
                dve.wait_ge(spread, n + 1)
                if j % 2 == 0:
                    link(nc.vector.tensor_tensor(bias[:, j], bias_ps[:, j], row[:, j // 2], ALU.add))
                    return
                link(nc.vector.tensor_copy(bias[:, j], bias_ps[:, j]))
                for p in range(PW):
                    r = j // 2 * PW + p
                    link(nc.vector.tensor_tensor(row[:, PB + r], row[:, PB + r], row[:, PH + r], ALU.mult))
                    link(nc.vector.tensor_tensor(bias[:, j], bias[:, j], row[:, PB + r], ALU.add))

            dve.wait_ge(rows_loaded, 16)
            dve.wait_ge(loads.col_loaded, 16)
            phases = row[:, MODS]
            link(nc.vector.tensor_scalar(phases, phases, PI / 4, None, ALU.subtract))
            link(nc.vector.tensor_scalar(turns, phases, 1.0 / (2 * PI), MAGIC, ALU.mult, ALU.add))
            link(nc.vector.tensor_scalar(turns, turns, MAGIC, None, ALU.subtract))
            flat = lambda a: a.rearrange("p r d -> p (r d)")
            link(nc.vector.scalar_tensor_tensor(flat(phases), flat(turns), -TURN_HI, flat(phases), ALU.mult, ALU.add))
            link(nc.vector.scalar_tensor_tensor(flat(phases), flat(turns), -TURN_LO, flat(phases), ALU.mult, ALU.add))
            dve.wait_ge(cosined, 2)
            nc.vector.tensor_scalar(phases, phases, float(np.sqrt(2.0)), None, ALU.mult).then_inc(modulated, 1)
            dve.wait_ge(modulated, 1)
            nc.vector.tensor_copy(out_norm[:], row[:, NR - 2:NR])
            sum_entangled(0)
            finish(0, 0)
            finish(1, 1)
            sum_entangled(1)
            keep_bias(0, 0)
            keep_bias(1, 1)
            finish(3, 2)
            finish(2, 3)
            keep_bias(3, 2)
            keep_bias(2, 3)


class GateWeights:

    def __init__(self, nc, ctx, paths, gate_w, gate_b):
        self.gate_w, self.gate_b = gate_w, gate_b
        self.angle, self.sigma = paths[:, 0], paths[:, 1]
        self.bias = ctx.enter_context(nc.sbuf_tensor("e_gb", [P, 2, CD], F32))
        self.loaded = ctx.enter_context(nc.semaphore("e_loaded"))

    def load(self, sp):
        sp.dma_start(self.angle, self.gate_w[:, 0]).then_inc(self.loaded, 16)
        sp.dma_start(self.sigma, self.gate_w[:, 1]).then_inc(self.loaded, 16)
        sp.dma_start(self.bias[:], self.gate_b).then_inc(self.loaded, 16)


def feed_forward(nc, x2, stat, gate, folded, bias, out_norm, eps, half_pi, ident, out):
    with ExitStack() as ctx:
        sb = lambda n, s, dtype=F32: ctx.enter_context(nc.sbuf_tensor(n, s, dtype))
        pair = lambda n, s: [sb(f"{n}_{part}", s, F32R) for part in ("high", "low")]
        sem = lambda n: ctx.enter_context(nc.semaphore(n))
        G, STEPS = 4, 4
        UNITS, TURNS = G * STEPS, TILES // G
        T = G * P
        y = sb("e_y", [P, G, D])
        weights = pair("e_weights", [P, 2, CD, D])
        minus_quarter = sb("e_minus_quarter", [P, 1])
        xn = sb("e_xn", [P, G, D])
        xn_t = pair("e_xn_t", [P, CD, T])
        angle, sigma, gb, loaded = gate.angle, gate.sigma, gate.bias, gate.loaded
        h_t = pair("e_h_t", [P, CD, T])
        total, neg_mean, squares, deviation, rstd = (sb(f"e_{n}", [P, G]) for n in ("total", "neg_mean", "squares", "deviation", "rstd"))
        scratch = sb("e_scratch", [P, D])
        turn_ps = ctx.enter_context(nc.psum_tensor("e_turn_ps", [P, 2, D], F32))
        mm_ps = ctx.enter_context(nc.psum_tensor("e_mm_ps", [P, 4, D], F32))
        preset = sem("e_preset")
        fetched, normed, x_turned, x_turned_out = sem("e_fetched"), sem("e_normed"), sem("e_x_turned"), sem("e_x_turned_out")
        gated, angled, folded_angle, sined, sigmad, h_ready = (
            sem(f"e_{n}") for n in ("gated", "angled", "folded_angle", "sined", "sigmad", "h_ready"))
        multiplied, biased, centred, squared, rooted, inverted, y_normed, y_turned, y_out = (
            sem(f"e_{n}") for n in ("multiplied", "biased", "centred", "squared", "rooted", "inverted", "y_normed", "y_turned", "y_out"))
        weights_rounded, weights_split, x_split, h_rounded, h_split, y_split = (
            sem(f"e_{n}") for n in ("weights_rounded", "weights_split", "x_split", "h_rounded", "h_split", "y_split"))
        gained, summed, stored = sem("e_gained"), sem("e_summed"), sem("e_stored")
        block = ctx.enter_context(nc.Block())
        out_tiles = out.rearrange("(i u p) d -> i p u d", u=G, p=P)
        MM = UNITS - G
        next_inputs = {UNITS - 3: (0,), UNITS - 2: (1, 2), UNITS - 1: (3,)}
        taken_inputs = {UNITS - 2: (0,), UNITS - 1: (1, 2, 3)}

        def row_of(t):
            return x2[:, bass.ds(t, 1)].rearrange("p t d -> p (t d)")

        @block.sync
        def _(sp):
            def body(i):
                sp.wait_ge(summed, G * (i + 1))
                sp.dma_start(out_tiles[bass.ds(i, 1)].rearrange("i p u d -> p (i u) d"), y[:]).then_inc(stored, 16)
            repeat(sp, TURNS, body)
            sp.wait_ge(stored, 16 * TURNS)

        @block.gpsimd
        def _(pool):
            nc.gpsimd.memset(minus_quarter[:], -PI / 4).then_inc(preset, 1)

            def normalise_tiles(i):
                for u in range(G):
                    t = G * i + u
                    wait(pool, x_turned, t - G + 1)
                    nc.gpsimd.tensor_tensor(xn[:, u], row_of(t), stat[:, 0, bass.ds(t, 1)].to_broadcast([P, D]), ALU.add).then_inc(fetched, 1)
                    pool.wait_ge(fetched, t + 1)
                    nc.gpsimd.tensor_tensor(xn[:, u], xn[:, u], stat[:, 1, bass.ds(t, 1)].to_broadcast([P, D]), ALU.mult).then_inc(normed, 1)

            def body(i, final=False):
                if not final:
                    normalise_tiles(i + 1)
                for u in range(G):
                    t = G * i + u
                    done = 2 * t
                    pool.wait_ge(y_normed, UNITS * i + MM + u + 1)
                    nc.gpsimd.tensor_tensor(y[:, u], y[:, u], out_norm[:, 0], ALU.mult).then_inc(gained, 1)
                    pool.wait_ge(gained, done + 1)
                    nc.gpsimd.tensor_tensor(y[:, u], y[:, u], out_norm[:, 1], ALU.add).then_inc(gained, 1)
            normalise_tiles(0)
            repeat_to_last(pool, TURNS, body)

        RING = 2 * CD + UNITS

        @block.tensor
        def _(pe):
            def turn_input(t, u, i=None):
                pe.wait_ge(normed, t + 1)
                if u >= 2:
                    pe.wait_ge(x_split, t - 1)
                elif i is not None:
                    pe.wait_ge(y_split, MM * (i + 1) - 1 + u)
                for c in range(CD):
                    last = nc.tensor.transpose(turn_ps[:, u % 2, c * P:(c + 1) * P], xn[:, u, c * P:(c + 1) * P], ident[:])
                last.then_inc(x_turned, 1)

            def free_bank(i, r):
                before = r - 4
                if before < 0:
                    before += RING
                    i = i - 1
                if isinstance(i, int) and i < 0:
                    return
                if before < CD:
                    pe.wait_ge(angled, CD * i + before + 1)
                elif before < 2 * CD:
                    pe.wait_ge(sigmad, CD * i + before - CD + 1)
                else:
                    pe.wait_ge(biased, UNITS * i + before - 2 * CD + 1)

            def gate(i, r):
                free_bank(i, r)
                which, f = divmod(r, CD)
                for c in range(CD):
                    last = multiply_parts(nc, mm_ps[:, r % 4], [w[:, which, c, f * P:(f + 1) * P] for w in weights],
                                          [a[:, c] for a in xn_t], c == 0, c == CD - 1)
                last.then_inc(gated, 1)

            def multiply(i, q):
                j, u = divmod(q, G)
                if q == 0:
                    pe.wait_ge(h_split, CD * (i + 1))
                if j:
                    pe.wait_ge(y_split, MM * i + q - G + 1)
                free_bank(i, 2 * CD + q)
                for c in range(CD):
                    last = multiply_parts(nc, mm_ps[:, q % 4], [a[:, c, u * P:(u + 1) * P] for a in h_t],
                                          [w[:, j, c] for w in folded], c == 0, c == CD - 1)
                last.then_inc(multiplied, 1)

            def turn_y(i, q):
                pe.wait_ge(y_normed, UNITS * i + q + 1)
                if q >= 2:
                    pe.wait_ge(y_split, MM * i + q - 1)
                for c in range(CD):
                    last = nc.tensor.transpose(turn_ps[:, q % 2, c * P:(c + 1) * P], y[:, q % G, c * P:(c + 1) * P], ident[:])
                last.then_inc(y_turned, 1)

            pe.wait_ge(weights_split, 2)

            for u in range(G):
                turn_input(u, u)

            def body(i, final=False):
                pe.wait_ge(x_split, G * (i + 1))
                for r in range(2 * CD):
                    gate(i, r)
                for q in range(UNITS):
                    multiply(i, q)
                    if 2 <= q < MM + 2:
                        turn_y(i, q - 2)
                    if q in next_inputs and not final:
                        for u in next_inputs[q]:
                            turn_input(G * (i + 1) + u, u, i)
            repeat_to_last(pe, TURNS, body)

        @block.scalar
        def _(act):
            act.wait_ge(loaded, 48)
            for which, raw in enumerate((angle, sigma)):
                nc.scalar.activation(weights[0][:, which], raw[:], ACT.Copy).then_inc(weights_rounded, 1)
            act.wait_ge(preset, 1)
            act.wait_ge(weights_split, 2)

            def round_input(i, u):
                act.wait_ge(x_turned, G * i + u + 1)
                if u == 0:
                    wait(act, gated, 2 * CD * i)
                nc.scalar.activation(xn_t[0][:, :, u * P:(u + 1) * P], turn_ps[:, u % 2].rearrange("p (c x) -> p c x", c=CD), ACT.Copy).then_inc(x_turned_out, 1)

            for u in range(G):
                round_input(0, u)

            def body(i, final=False):
                for f in range(CD):
                    act.wait_ge(gated, 2 * CD * i + f + 1)
                    if f == 0:
                        wait(act, h_split, CD * i)
                    nc.scalar.activation(angle[:, f], mm_ps[:, f], ACT.Tanh, bias=gb[:, 0, f:f + 1]).then_inc(angled, 1)
                act.wait_ge(angled, CD * (i + 1))
                nc.scalar.activation(angle[:], angle[:], ACT.Abs, bias=minus_quarter[:], scale=PI).then_inc(folded_angle, 1)
                act.wait_ge(folded_angle, i + 1)
                nc.scalar.activation(angle[:], angle[:], ACT.Sin, bias=half_pi[:], scale=-1.0).then_inc(sined, 1)
                for f in range(CD):
                    act.wait_ge(gated, 2 * CD * i + CD + f + 1)
                    nc.scalar.activation(sigma[:, f], mm_ps[:, f], ACT.Sigmoid, bias=gb[:, 1, f:f + 1]).then_inc(sigmad, 1)
                for f in range(CD):
                    act.wait_ge(h_ready, CD * i + f + 1)
                    if f == 0:
                        wait(act, multiplied, UNITS * i)
                    nc.scalar.activation(h_t[0][:, f], angle[:, f], ACT.Copy).then_inc(h_rounded, 1)
                for q in range(UNITS):
                    u = q % G
                    n = UNITS * i + q
                    if 3 <= q < MM + 3:
                        store_turned(i, q - 3)
                    if q in taken_inputs and not final:
                        for v in taken_inputs[q]:
                            round_input(i + 1, v)
                    act.wait_ge(centred, n + 1)
                    wait(act, rooted, n)
                    nc.scalar.activation(scratch[:], y[:, u], ACT.Square, bias=neg_mean[:, u:u + 1], accum_out=squares[:, u:u + 1]).then_inc(squared, 1)
                    act.wait_ge(squared, n + 1)
                    nc.scalar.activation(deviation[:, u:u + 1], squares[:, u:u + 1], ACT.Sqrt, bias=eps[:], scale=1.0 / D).then_inc(rooted, 1)

            def store_turned(i, q):
                j, u = divmod(q, G)
                act.wait_ge(y_turned, MM * i + q + 1)
                act.wait_ge(multiplied, UNITS * i + q + 1)
                nc.scalar.activation(h_t[0][:, :, u * P:(u + 1) * P], turn_ps[:, q % 2].rearrange("p (c x) -> p c x", c=CD), ACT.Copy).then_inc(y_out, 1)

            repeat_to_last(act, TURNS, body)

        @block.vector
        def _(dve):
            def take(i, q):
                j, u = divmod(q, G)
                n = UNITS * i + q
                dve.wait_ge(multiplied, n + 1)
                if q >= G:
                    dve.wait_ge(y_turned, MM * i + q - G + 1)
                else:
                    wait(dve, stored, 16 * i)
                nc.vector.scalar_tensor_tensor(y[:, u], mm_ps[:, q % 4], 1.0, bias[:, j], ALU.mult, ALU.add, accum_out=total[:, u:u + 1]).then_inc(biased, 1)
                dve.wait_ge(biased, n + 1)
                nc.vector.tensor_scalar(neg_mean[:, u:u + 1], total[:, u:u + 1], -1.0 / D, None, ALU.mult).then_inc(centred, 1)

            def normalise(i, q):
                u, n = q % G, UNITS * i + q
                dve.wait_ge(rooted, n + 1)
                nc.vector.reciprocal(rstd[:, u:u + 1], deviation[:, u:u + 1]).then_inc(inverted, 1)
                dve.wait_ge(inverted, n + 1)
                nc.vector.tensor_scalar(y[:, u], y[:, u], neg_mean[:, u:u + 1], rstd[:, u:u + 1], ALU.add, ALU.mult).then_inc(y_normed, 1)

            def split_turned(i, q):
                u = q % G
                at = slice(u * P, (u + 1) * P)
                dve.wait_ge(y_out, MM * i + q + 1)
                low_part(nc, h_t[1][:, :, at], turn_ps[:, q % 2].rearrange("p (c x) -> p c x", c=CD), h_t[0][:, :, at]).then_inc(y_split, 1)

            dve.wait_ge(loaded, 48)
            for which, raw in enumerate((angle, sigma)):
                dve.wait_ge(weights_rounded, which + 1)
                low_part(nc, weights[1][:, which], raw[:], weights[0][:, which]).then_inc(weights_split, 1)

            def split_input(i, u):
                at = slice(u * P, (u + 1) * P)
                dve.wait_ge(x_turned_out, G * i + u + 1)
                low_part(nc, xn_t[1][:, :, at], turn_ps[:, u % 2].rearrange("p (c x) -> p c x", c=CD), xn_t[0][:, :, at]).then_inc(x_split, 1)

            for u in range(G):
                split_input(0, u)

            def body(i, final=False):
                dve.wait_ge(sined, i + 1)
                for f in range(CD):
                    dve.wait_ge(sigmad, CD * i + f + 1)
                    nc.vector.scalar_tensor_tensor(angle[:, f], angle[:, f], float(np.sqrt(2.0)), sigma[:, f], ALU.mult, ALU.mult).then_inc(h_ready, 1)
                for f in range(CD):
                    dve.wait_ge(h_rounded, CD * i + f + 1)
                    low_part(nc, h_t[1][:, f], angle[:, f], h_t[0][:, f]).then_inc(h_split, 1)
                for q in range(UNITS):
                    if 3 <= q < MM + 3:
                        split_turned(i, q - 3)
                    if q in taken_inputs and not final:
                        for v in taken_inputs[q]:
                            split_input(i + 1, v)
                    take(i, q)
                    if q:
                        normalise(i, q - 1)
                normalise(i, UNITS - 1)
                for u in range(G):
                    dve.wait_ge(gained, 2 * (G * i + u + 1))
                    nc.vector.scalar_tensor_tensor(y[:, u], y[:, u], 1.0, row_of(G * i + u), ALU.mult, ALU.add).then_inc(summed, 1)
            repeat_to_last(dve, TURNS, body)


def perceiver_block(nc, x, cache_t, packed, rope_q, rope_kv, amp_nat, phase_nat, basis_t, basis_o, amp_o, phase_o,
                    ent_in, ent_out, path, columns, rows, gate_w, gate_b, out):
    q_dram = nc.dram_tensor("carried_queries", (B, DC, H, S), F32, kind="Internal").ap()
    w_vo_dram = nc.dram_tensor("output_weights", (P, H, D), F32, kind="Internal").ap()
    with ExitStack() as ctx:
        sb = lambda n, s: ctx.enter_context(nc.sbuf_tensor(n, s, F32))
        ident = sb("ident", [P, P])
        stat = sb("stat", [P, 2, TILES])
        eps = sb("eps", [P, 1])
        half_pi = sb("half_pi", [P, 1])
        ready = ctx.enter_context(nc.semaphore("ident_ready"))
        with nc.Block() as block:
            @block.gpsimd
            def _(pool):
                nc.gpsimd.memset(ident[:], 0.0).then_inc(ready, 1)
                nc.gpsimd.memset(eps[:], EPS).then_inc(ready, 1)
                nc.gpsimd.memset(half_pi[:], PI / 2).then_inc(ready, 1)
                pool.wait_ge(ready, 3)
                nc.gpsimd.affine_select(out=ident[:], in_=ident[:], compare_op=ALU.not_equal, fill=1.0,
                                        base=0, pattern=[[-1, P]], channel_multiplier=1).then_inc(ready, 1)
                pool.wait_ge(ready, 4)
        with ExitStack() as scope:
            x_t = [scope.enter_context(nc.sbuf_tensor(f"x_t_{part}", [P, CD, S, B], F32R)) for part in ("high", "low")]
            heads = HeadWeights(nc, scope, packed, rope_q)
            used = normalise_input(nc, x, x_t, ident, eps, heads)
            used += query_path(nc, heads, x_t, w_vo_dram, q_dram)
            left_counted = range(min(used), max(used) + 1)
        x1 = sb("x1", [P, TILES, D])
        cross_attention(nc, cache_t, rope_kv, x, q_dram, w_vo_dram, x1, stat, ident, left_counted)
        root_deviations(nc, stat, eps, "x1")
        folded = [ctx.enter_context(nc.sbuf_tensor(f"folded_{part}", [P, 4, CD, D], F32R)) for part in ("high", "low")]
        bias, out_norm = sb("bias", [P, 4, D]), sb("out_norm", [P, 2, D])
        paths = sb("paths", [P, PW, CD, D])
        gate = GateWeights(nc, ctx, paths, gate_w, gate_b)
        with ExitStack() as fold_scope:
            loads = FoldLoads(nc, fold_scope, paths, ent_in, ent_out, path, columns)
            with ExitStack() as scope:
                basis, score_w, value_w, out_w = (scope.enter_context(nc.sbuf_tensor(n, shape, F32)) for n, shape in (
                    ("basis", [P, CD, 2 * P]), ("score_w", [HARM, 16, HARM]), ("value_w", [P, 16, HARM]), ("out_w", [HARM, D])))
                holo_weights(nc, amp_nat, phase_nat, basis_t, basis_o, amp_o, phase_o, half_pi, basis, score_w, value_w, out_w)
                self_attention(nc, x1, stat, basis, score_w, value_w, out_w, ident, loads)
            root_deviations(nc, stat, eps, "x2")
            fold_weights(nc, loads, path, rows, half_pi, ident, folded, bias, out_norm, gate)
        feed_forward(nc, x1, stat, gate, folded, bias, out_norm, eps, half_pi, ident, out)


def rope_tables(length, dim):
    inv = (1.0 / 10000.0 ** (np.arange(0, dim, 2, dtype=np.float32) / np.float32(dim))).astype(np.float32)
    f = np.arange(length, dtype=np.float32)[:, None] * inv[None, :]
    sin = np.repeat(np.sin(f.astype(np.float64)).astype(np.float32), 2, axis=-1)
    cos = np.repeat(np.cos(f.astype(np.float64)).astype(np.float32), 2, axis=-1)
    return sin, cos


def kernel(**inputs):
    import concourse.bacc as bacc
    from concourse.bass_utils import run_bass_kernel_spmd

    g = {name.replace("L0_", ""): np.asarray(a) for name, a in inputs.items()}
    sin_q, cos_q = rope_tables(S, DQ)
    sin_k, cos_k = rope_tables(L, DC)
    sign_q = np.where(np.arange(DQ) < DQ // 2, np.float32(1), np.float32(-1))
    swap_q = (np.arange(DQ) + DQ // 2) % DQ
    rope_q = np.stack([cos_q.T, (sin_q[:, swap_q] * sign_q).T]).reshape(2, CQ, P, S).transpose(2, 0, 1, 3)
    sign_k = np.where(np.arange(DC) < DC // 2, np.float32(-1), np.float32(1))
    rope_kv = np.stack([cos_k.T, (sin_k * sign_k).T], axis=1)

    w_qr = g["xattn_W_qr"]
    w_qr2 = np.concatenate([w_qr[:, DQ // 2:], w_qr[:, :DQ // 2]], axis=1)
    rows = lambda a, c: a.reshape(H, c, P, -1).transpose(0, 2, 1, 3).reshape(H, P, -1)
    w_kr = np.zeros((H, P, P), np.float32)
    w_kr[:, :R] = g["xattn_W_kr"].transpose(0, 2, 1)
    packed = np.concatenate([
        rows(g["xattn_Wq"].reshape(H, K, D).transpose(0, 2, 1), CD),
        rows(g["xattn_w_kc_q"].transpose(0, 2, 1), CQ),
        rows(w_qr, CQ), rows(w_qr2, CQ), w_kr, g["xattn_w_kc_kv"],
        g["xattn_Wo"].T.reshape(H, K, D)], axis=2)

    by_row = lambda a: a.reshape(CD, P, -1).transpose(1, 0, 2)
    three = lambda kind: by_row(np.concatenate([g[f"attn_{kind}_{n}"] for n in "qkv"], axis=1))

    column = lambda a: a.reshape(-1, P).T
    gains = [np.ones(D, np.float32), g["ffn_ln3_g"][0], g["ffn_ln4_g"][0], g["ffn_ln3_g"][1]]
    offsets = [np.zeros(D, np.float32), g["ffn_ln3_b"][0], g["ffn_ln4_b"][0], g["ffn_ln3_b"][1]]
    columns = np.concatenate([column(a) for a in (*gains, *offsets, *g["ffn_ent_b"])], axis=1)
    rows_ = np.concatenate([g["ffn_ent_pb"], g["ffn_path_b"].reshape(-1, D), g["ffn_phase"].reshape(-1, D),
                            g["ffn_ln4_g"][1:], g["ffn_ln4_b"][1:]])
    ent = lambda a: a.reshape(2, CF, P, D).transpose(0, 2, 1, 3)

    arrays = {
        "x": g["x"].reshape(B * S, D), "cache_t": g["ctx_512"].transpose(0, 2, 1), "packed": packed,
        "rope_q": rope_q, "rope_kv": rope_kv,
        "amp_nat": three("amp"), "phase_nat": three("phase"),
        "basis_t": by_row(np.concatenate([g[f"attn_basis_{n}"].T for n in "qvkk"], axis=1)),
        "basis_o": by_row(g["attn_basis_o"].T), "amp_o": g["attn_amp_o"].T, "phase_o": g["attn_phase_o"].T,
        "ent_in": ent(g["ffn_ent_w"].transpose(0, 2, 1)), "ent_out": ent(g["ffn_ent_pw"]),
        "path": g["ffn_path_w"].reshape(2, 2, CD, P, D).transpose(0, 3, 1, 2, 4),
        "columns": columns, "rows": rows_,
        "gate_w": np.stack([by_row(g["ffn_ph_w"]), by_row(g["ffn_amp_w"])], axis=1),
        "gate_b": np.stack([column(g["ffn_ph_b"]), column(g["ffn_amp_b"])], axis=1),
    }
    arrays = {name: np.ascontiguousarray(a) for name, a in arrays.items()}
    nc = bacc.Bacc("TRN2", target_bir_lowering=False, num_devices=1)
    args = [nc.dram_tensor(name, a.shape, mybir.dt.from_np(a.dtype), kind="ExternalInput").ap() for name, a in arrays.items()]
    out = nc.dram_tensor("out", (B * S, D), F32, kind="ExternalOutput").ap()
    perceiver_block(nc, *args, out)
    result = run_bass_kernel_spmd(nc, [arrays], core_ids=[0])
    return result.results[0]["out"].reshape(B, S, D)
```
